# Optimizing a Trainium2 kernel written in Bass

```python
import numpy as np
import jax
import jax.numpy as jnp

def _softmax(x, axis=-1):
    return jax.nn.softmax(x, axis=axis)

def _gelu(x):
    return jax.nn.gelu(x, approximate=True)

def _silu(x):
    return jax.nn.silu(x)

def _sigmoid(x):
    return jax.nn.sigmoid(x)

def _layernorm(x, axis=-1, eps=1e-05):
    m = jnp.mean(x, axis=axis, keepdims=True)
    v = jnp.var(x, axis=axis, keepdims=True)
    return (x - m) / jnp.sqrt(v + eps)

def _scatter_add(tgt, idx, src, axis=0):
    return tgt.at[idx].add(src)

def _segment_sum(src, seg, n):
    return jax.ops.segment_sum(src, seg, n)
kernel_name = 'mk_decoder_postln_d2_seqx_r4_653bee'

def setup_inputs(seed: int=0):
    np.random.seed(seed)
    _w = jnp.asarray

    def _rec_inputs():
        import jax
        import jax.numpy as jnp
        _rk = jax.random.key(seed)
        x = 7.22e-05 + 1 * jax.random.normal(jax.random.fold_in(_rk, 1), (4, 512, 256), jnp.float32)
        _lenS = 512 - jax.random.randint(jax.random.fold_in(_rk, 7), (4,), 0, max(1, 512 // 4) + 1, jnp.int32)
        _lenS2 = 512 - jax.random.randint(jax.random.fold_in(_rk, 8), (4,), 0, max(1, 512 // 4) + 1, jnp.int32)
        _ctx_1024P = jax.random.normal(jax.random.fold_in(_rk, 11), (4, 16, 256), jnp.float32)
        _ctx_1024c = jax.random.dirichlet(jax.random.fold_in(_rk, 511), 0.3 * jnp.ones((16,), jnp.float32), (4, 512))
        _ctx_1024t = jnp.einsum('bsk,bkd->bsd', _ctx_1024c, _ctx_1024P)
        _ctx_1024t = _ctx_1024t * jax.lax.rsqrt(jnp.mean(jnp.square(_ctx_1024t)) + 1e-12) * 0.953939
        ctx_1024 = 4.13588e-05 + 0.999923 * (_ctx_1024t + 0.3 * jax.random.normal(jax.random.fold_in(_rk, 611), (4, 512, 256), jnp.float32))
        _validS = jnp.arange(512)[None, :] < _lenS[:, None]
        _validS2 = jnp.arange(512)[None, :] < _lenS2[:, None]
        _causal = jnp.tril(jnp.ones((512, 512), dtype=bool))
        mask_Bx1xS2_ik0 = jnp.where(jnp.broadcast_to(_validS2[:, None, :], (4, 1, 512)), 0, 1).astype(jnp.int32)
        mask_BxSxS2_ik0 = jnp.where(jnp.broadcast_to(_validS2[:, None, :], (4, 512, 512)), 0, 1).astype(jnp.int32)
        return (x, ctx_1024, mask_Bx1xS2_ik0, mask_BxSxS2_ik0)
    x, ctx_1024, mask_Bx1xS2_ik0, mask_BxSxS2_ik0 = _rec_inputs()

    def _L0_attn_setup():
        import jax, jax.numpy as jnp
        import numpy as np
        import math
        HEAD_SIZE = 128

        def rotate_every_two(x):
            x1 = x[..., ::2]
            x2 = x[..., 1::2]
            return jnp.stack((-x2, x1), axis=-1).reshape(x.shape)

        def rope_table(seq_len, dtype=jnp.float32):
            pos = jnp.arange(seq_len, dtype=jnp.float32)
            inv = 10000.0 ** (jnp.arange(0, HEAD_SIZE, 2, dtype=jnp.float32) / HEAD_SIZE)
            radians = pos[:, None] / inv
            sincos = jnp.stack((jnp.sin(radians), jnp.cos(radians)), axis=-1).reshape(seq_len, -1)
            t = jnp.repeat(sincos, 2, axis=-1)
            return t.astype(dtype)
        key = jax.random.key(seed)
        ks = jax.random.split(key, 7)
        B, S, H = (2, 1024, 256)
        sd = 1.0 / math.sqrt(H)
        return {'hidden_states': jax.random.normal(ks[0], (B, S, H), dtype=jnp.float32), 'Wq': jax.random.normal(ks[1], (H, H), dtype=jnp.float32) * sd, 'bq': jax.random.normal(ks[2], (H,), dtype=jnp.float32) * sd, 'Wk': jax.random.normal(ks[3], (H, H), dtype=jnp.float32) * sd, 'bk': jax.random.normal(ks[4], (H,), dtype=jnp.float32) * sd, 'Wv': jax.random.normal(ks[5], (H, H), dtype=jnp.float32) * sd, 'bv': jax.random.normal(ks[6], (H,), dtype=jnp.float32) * sd}
    _L0_attn_all = _L0_attn_setup()
    _L0_attn_in = {k: v for k, v in _L0_attn_all.items() if k in ('Wq', 'bq', 'Wk', 'bk', 'Wv', 'bv')}
    del _L0_attn_all

    def _L0_xattn_setup():
        import jax, jax.numpy as jnp
        import numpy as np
        B, S, D = (4, 512, 256)
        NEG = -10000000000.0
        key = jax.random.key(seed)
        ks = jax.random.split(key, 10)
        inv = 1.0 / np.sqrt(D)
        return {'Q': jax.random.normal(ks[0], (B, S, D), dtype=jnp.float32), 'K': jax.random.normal(ks[1], (B, S, D), dtype=jnp.float32), 'V': jax.random.normal(ks[2], (B, S, D), dtype=jnp.float32), 'attention_mask': jax.random.randint(ks[3], (B, 1, S), 0, 2, dtype=jnp.int32), 'Wq': jax.random.uniform(ks[4], (D, D), jnp.float32, -inv, inv), 'bq': jnp.zeros((D,), jnp.float32), 'Wk': jax.random.uniform(ks[5], (D, D), jnp.float32, -inv, inv), 'bk': jnp.zeros((D,), jnp.float32), 'Wv': jax.random.uniform(ks[6], (D, D), jnp.float32, -inv, inv), 'bv': jnp.zeros((D,), jnp.float32)}
    _L0_xattn_all = _L0_xattn_setup()
    _L0_xattn_in = {k: v for k, v in _L0_xattn_all.items() if k in ('Wq', 'bq', 'Wk', 'bk', 'Wv', 'bv')}
    del _L0_xattn_all

    def _L0_ffn_setup():
        import jax, jax.numpy as jnp
        import numpy as np
        B, T, D, E, K = (2, 512, 256, 8, 2)
        H = 2 * D
        key = jax.random.key(seed)
        ks = jax.random.split(key, 5)
        s = 0.02
        return {'x': jax.random.normal(ks[0], (B, T, D), jnp.float32), 'Wr': jax.random.normal(ks[1], (D, E), jnp.float32) * s, 'br': jnp.zeros((E,), jnp.float32), 'W1': jax.random.normal(ks[2], (E, D, H), jnp.float32) * s, 'b1': jnp.zeros((E, H), jnp.float32), 'W2': jax.random.normal(ks[3], (E, H, D), jnp.float32) * s, 'b2': jnp.zeros((E, D), jnp.float32)}
    _L0_ffn_all = _L0_ffn_setup()
    _L0_ffn_in = {k: v for k, v in _L0_ffn_all.items() if k in ('Wr', 'br', 'W1', 'b1', 'W2', 'b2')}
    del _L0_ffn_all

    def _L1_attn_setup():
        import jax, jax.numpy as jnp
        import numpy as np
        B, S, D, H = (2, 512, 256, 16)
        DH = D // H
        key = jax.random.key(seed)
        ks = jax.random.split(key, 5)
        scale = 1.0 / np.sqrt(D)
        return {'in_features': jax.random.normal(ks[0], (B, S, D), jnp.float32), 'Wq': jax.random.normal(ks[1], (D, D), jnp.float32) * scale, 'Wk': jax.random.normal(ks[2], (D, D), jnp.float32) * scale, 'Wv': jax.random.normal(ks[3], (D, D), jnp.float32) * scale, 'Wo': jax.random.normal(ks[4], (D, D), jnp.float32) * scale}
    _L1_attn_all = _L1_attn_setup()
    _L1_attn_in = {k: v for k, v in _L1_attn_all.items() if k in ('Wq', 'Wk', 'Wv', 'Wo')}
    del _L1_attn_all

    def _L1_xattn_setup():
        import jax, jax.numpy as jnp
        import numpy as np
        N_HEADS = 16
        N_UNITS = 256
        D_K = N_UNITS // N_HEADS
        B, S = (4, 512)
        key = jax.random.key(seed)
        ks = jax.random.split(key, 12)
        sc = 1.0 / np.sqrt(N_UNITS)
        inp = {'query': jax.random.normal(ks[0], (B, S, N_UNITS), jnp.float32), 'key': jax.random.normal(ks[1], (B, S, N_UNITS), jnp.float32), 'value': jax.random.normal(ks[2], (B, S, N_UNITS), jnp.float32), 'mask': jnp.tril(jnp.ones((S, S), jnp.int32))[None].repeat(B, axis=0), 'Wq': jax.random.normal(ks[3], (N_UNITS, N_UNITS), jnp.float32) * sc, 'bq': jnp.zeros((N_UNITS,), jnp.float32), 'Wk': jax.random.normal(ks[4], (N_UNITS, N_UNITS), jnp.float32) * sc, 'bk': jnp.zeros((N_UNITS,), jnp.float32), 'Wv': jax.random.normal(ks[5], (N_UNITS, N_UNITS), jnp.float32) * sc, 'bv': jnp.zeros((N_UNITS,), jnp.float32), 'Wo': jax.random.normal(ks[6], (N_UNITS, N_UNITS), jnp.float32) * sc, 'bo': jnp.zeros((N_UNITS,), jnp.float32)}
        return inp
    _L1_xattn_all = _L1_xattn_setup()
    _L1_xattn_in = {k: v for k, v in _L1_xattn_all.items() if k in ('Wq', 'bq', 'Wk', 'bk', 'Wv', 'bv', 'Wo', 'bo')}
    del _L1_xattn_all

    def _L1_ffn_setup():
        import jax, jax.numpy as jnp
        import numpy as np
        DIM = 256
        DEPTH = 6
        HEADS = 16
        DIM_HEAD = 64
        WINDOW = 64
        INNER = HEADS * DIM_HEAD
        DIM_INNER = int(DIM * 4 * 2 / 3)
        QK_SCALE = 8.0

        def shift_tokens(t):
            a, s = jnp.split(t, 2, -1)
            s = jnp.pad(s, ((0, 0), (1, 0), (0, 0)))[:, :-1]
            return jnp.concatenate([a, s], -1)

        def l2norm(t):
            return t / jnp.maximum(jnp.linalg.norm(t, axis=-1, keepdims=True), 1e-12)

        def rotate_half(x):
            x1, x2 = jnp.split(x, 2, -1)
            return jnp.concatenate([-x2, x1], -1)

        def rotary_tables(n):
            half = jnp.arange(0, DIM_HEAD, 2, dtype=jnp.float32)
            inv_freq = 1.0 / 10000.0 ** (half / DIM_HEAD)
            t = jnp.arange(n, dtype=jnp.float32)
            freqs = t[:, None] * inv_freq[None, :]
            freqs = jnp.concatenate([freqs, freqs], -1)
            base_scale = (half + 0.4 * DIM_HEAD) / (1.4 * DIM_HEAD)
            power = (t - n // 2) / (WINDOW // 2)
            scale = base_scale[None, :] ** power[:, None]
            scale = jnp.concatenate([scale, scale], -1)
            return (freqs, scale)

        def local_attention(q, k, v):
            b, h, n, d = q.shape
            w = WINDOW
            nw = n // w
            bq = q.reshape(b, h, nw, w, d)
            bk = k.reshape(b, h, nw, w, d)
            bv = v.reshape(b, h, nw, w, d)

            def look(t):
                p = jnp.pad(t, ((0, 0), (0, 0), (1, 0), (0, 0), (0, 0)))
                return jnp.concatenate([p[:, :, :nw], p[:, :, 1:]], axis=3)
            bk2, bv2 = (look(bk), look(bv))
            seq = jnp.arange(n).reshape(nw, w)
            seq_p = jnp.pad(seq, ((1, 0), (0, 0)), constant_values=-1)
            jt = jnp.concatenate([seq_p[:nw], seq_p[1:]], axis=1)
            it = seq[:, :, None]
            jb = jt[:, None, :]
            mask = (it < jb) | (it > jb + w) | (jb == -1)
            sim = jnp.einsum('bhwie,bhwje->bhwij', bq, bk2) * QK_SCALE
            sim = jnp.where(mask, -jnp.finfo(sim.dtype).max, sim)
            attn = jax.nn.softmax(sim, -1)
            out = jnp.einsum('bhwij,bhwje->bhwie', attn, bv2)
            return out.reshape(b, h, n, d)

        def attn_layer(x, Wqkv, qs, ksc, Wo):
            b, n, _ = x.shape
            qkv = x @ Wqkv
            q, k, v = jnp.split(qkv, 3, -1)
            sh = lambda t: t.reshape(b, n, HEADS, DIM_HEAD).transpose(0, 2, 1, 3)
            q, k, v = (sh(q), sh(k), sh(v))
            q = l2norm(q) * qs
            k = l2norm(k) * ksc
            freqs, scale = rotary_tables(n)
            cos, sin = (jnp.cos(freqs), jnp.sin(freqs))
            q = q * cos * scale + rotate_half(q) * sin * scale
            inv = 1.0 / scale
            k = k * cos * inv + rotate_half(k) * sin * inv
            out = local_attention(q, k, v)
            out = out.transpose(0, 2, 1, 3).reshape(b, n, INNER)
            return out @ Wo

        def ffn_layer(x, g, bln, W1, b1, W2, b2):
            mu = x.mean(-1, keepdims=True)
            var = ((x - mu) ** 2).mean(-1, keepdims=True)
            xn = (x - mu) / jnp.sqrt(var + 1e-05) * g + bln
            hg = xn @ W1 + b1
            a, gate = jnp.split(hg, 2, -1)
            return a * jax.nn.gelu(gate, approximate=False) @ W2 + b2
        key = jax.random.key(seed)
        ks = jax.random.split(key, 8)
        B, N = (2, 512)
        init = lambda k, shape: jax.random.normal(k, shape, jnp.float32) * 0.02
        return {'x': jax.random.normal(ks[0], (B, N, DIM), jnp.float32), 'Wqkv': init(ks[1], (DEPTH, DIM, 3 * INNER)), 'q_scale': jnp.ones((DEPTH, DIM_HEAD), jnp.float32), 'k_scale': jnp.ones((DEPTH, DIM_HEAD), jnp.float32), 'Wo': init(ks[2], (DEPTH, INNER, DIM)), 'ln_g': jnp.ones((DEPTH, DIM), jnp.float32), 'ln_b': jnp.zeros((DEPTH, DIM), jnp.float32), 'W1': init(ks[3], (DEPTH, DIM, 2 * DIM_INNER)), 'b1': jnp.zeros((DEPTH, 2 * DIM_INNER), jnp.float32), 'W2': init(ks[4], (DEPTH, DIM_INNER, DIM)), 'b2': jnp.zeros((DEPTH, DIM), jnp.float32)}
    _L1_ffn_all = _L1_ffn_setup()
    _L1_ffn_in = {k: v for k, v in _L1_ffn_all.items() if k in ('Wqkv', 'q_scale', 'k_scale', 'Wo', 'ln_g', 'ln_b', 'W1', 'b1', 'W2', 'b2')}
    del _L1_ffn_all
    return {'x': x, 'ctx_1024': ctx_1024, 'mask_Bx1xS2_ik0': mask_Bx1xS2_ik0, 'mask_BxSxS2_ik0': mask_BxSxS2_ik0, 'L0_attn_Wq': _L0_attn_in['Wq'], 'L0_attn_bq': _L0_attn_in['bq'], 'L0_attn_Wk': _L0_attn_in['Wk'], 'L0_attn_bk': _L0_attn_in['bk'], 'L0_attn_Wv': _L0_attn_in['Wv'], 'L0_attn_bv': _L0_attn_in['bv'], 'L0_xattn_Wq': _L0_xattn_in['Wq'], 'L0_xattn_bq': _L0_xattn_in['bq'], 'L0_xattn_Wk': _L0_xattn_in['Wk'], 'L0_xattn_bk': _L0_xattn_in['bk'], 'L0_xattn_Wv': _L0_xattn_in['Wv'], 'L0_xattn_bv': _L0_xattn_in['bv'], 'L0_ffn_Wr': _L0_ffn_in['Wr'], 'L0_ffn_br': _L0_ffn_in['br'], 'L0_ffn_W1': _L0_ffn_in['W1'], 'L0_ffn_b1': _L0_ffn_in['b1'], 'L0_ffn_W2': _L0_ffn_in['W2'], 'L0_ffn_b2': _L0_ffn_in['b2'], 'L1_attn_Wq': _L1_attn_in['Wq'], 'L1_attn_Wk': _L1_attn_in['Wk'], 'L1_attn_Wv': _L1_attn_in['Wv'], 'L1_attn_Wo': _L1_attn_in['Wo'], 'L1_xattn_Wq': _L1_xattn_in['Wq'], 'L1_xattn_bq': _L1_xattn_in['bq'], 'L1_xattn_Wk': _L1_xattn_in['Wk'], 'L1_xattn_bk': _L1_xattn_in['bk'], 'L1_xattn_Wv': _L1_xattn_in['Wv'], 'L1_xattn_bv': _L1_xattn_in['bv'], 'L1_xattn_Wo': _L1_xattn_in['Wo'], 'L1_xattn_bo': _L1_xattn_in['bo'], 'L1_ffn_Wqkv': _L1_ffn_in['Wqkv'], 'L1_ffn_q_scale': _L1_ffn_in['q_scale'], 'L1_ffn_k_scale': _L1_ffn_in['k_scale'], 'L1_ffn_Wo': _L1_ffn_in['Wo'], 'L1_ffn_ln_g': _L1_ffn_in['ln_g'], 'L1_ffn_ln_b': _L1_ffn_in['ln_b'], 'L1_ffn_W1': _L1_ffn_in['W1'], 'L1_ffn_b1': _L1_ffn_in['b1'], 'L1_ffn_W2': _L1_ffn_in['W2'], 'L1_ffn_b2': _L1_ffn_in['b2']}

def reference(x, ctx_1024, mask_Bx1xS2_ik0, mask_BxSxS2_ik0, L0_attn_Wq, L0_attn_bq, L0_attn_Wk, L0_attn_bk, L0_attn_Wv, L0_attn_bv, L0_xattn_Wq, L0_xattn_bq, L0_xattn_Wk, L0_xattn_bk, L0_xattn_Wv, L0_xattn_bv, L0_ffn_Wr, L0_ffn_br, L0_ffn_W1, L0_ffn_b1, L0_ffn_W2, L0_ffn_b2, L1_attn_Wq, L1_attn_Wk, L1_attn_Wv, L1_attn_Wo, L1_xattn_Wq, L1_xattn_bq, L1_xattn_Wk, L1_xattn_bk, L1_xattn_Wv, L1_xattn_bv, L1_xattn_Wo, L1_xattn_bo, L1_ffn_Wqkv, L1_ffn_q_scale, L1_ffn_k_scale, L1_ffn_Wo, L1_ffn_ln_g, L1_ffn_ln_b, L1_ffn_W1, L1_ffn_b1, L1_ffn_W2, L1_ffn_b2):
    import jax
    import jax.numpy as jnp

    def _L0_attn_ref(hidden_states, Wq, bq, Wk, bk, Wv, bv):
        import jax, jax.numpy as jnp
        import numpy as np
        import math
        HEAD_SIZE = 128

        def rotate_every_two(x):
            x1 = x[..., ::2]
            x2 = x[..., 1::2]
            return jnp.stack((-x2, x1), axis=-1).reshape(x.shape)

        def rope_table(seq_len, dtype=jnp.float32):
            pos = jnp.arange(seq_len, dtype=jnp.float32)
            inv = 10000.0 ** (jnp.arange(0, HEAD_SIZE, 2, dtype=jnp.float32) / HEAD_SIZE)
            radians = pos[:, None] / inv
            sincos = jnp.stack((jnp.sin(radians), jnp.cos(radians)), axis=-1).reshape(seq_len, -1)
            t = jnp.repeat(sincos, 2, axis=-1)
            return t.astype(dtype)
        B, S, H = hidden_states.shape
        t = rope_table(S, hidden_states.dtype)
        q = hidden_states @ Wq.T + bq
        k = hidden_states @ Wk.T + bk
        v = hidden_states @ Wv.T + bv
        q = q * t + rotate_every_two(q) * t
        k = k * t + rotate_every_two(k) * t
        scale = math.sqrt(HEAD_SIZE)
        scores = jnp.einsum('bsh,bth->bst', q, k) / scale
        probs = jax.nn.softmax(scores, axis=-1)
        out = jnp.einsum('bst,bth->bsh', probs, v)
        return out

    def _L0_xattn_ref(Q, K, V, attention_mask, Wq, bq, Wk, bk, Wv, bv):
        import jax, jax.numpy as jnp
        import numpy as np
        B, S, D = (4, 512, 256)
        NEG = -10000000000.0
        q = jnp.einsum('bsd,ed->bse', Q, Wq) + bq
        k = jnp.einsum('bsd,ed->bse', K, Wk) + bk
        v = jnp.einsum('bsd,ed->bse', V, Wv) + bv
        scores = jnp.einsum('bqd,bkd->bqk', q, k) / jnp.sqrt(jnp.float32(D))
        scores = jnp.where(attention_mask == 0, jnp.float32(NEG), scores)
        causal = jnp.triu(jnp.full((S, S), NEG, dtype=jnp.float32), k=1)
        scores = scores + causal
        attn = jax.nn.softmax(scores, axis=-1)
        return jnp.einsum('bqk,bkd->bqd', attn, v)

    def _L0_ffn_ref(x, Wr, br, W1, b1, W2, b2):
        import jax, jax.numpy as jnp
        import numpy as np
        B, T, D, E, K = (2, 512, 256, 8, 2)
        H = 2 * D
        logits = jnp.einsum('btd,de->bte', x, Wr) + br
        topv, topi = jax.lax.top_k(logits, K)
        sel_mask = jax.nn.one_hot(topi, E, dtype=logits.dtype).sum(-2) > 0
        neg_inf = jnp.finfo(logits.dtype).min
        gates = jax.nn.softmax(jnp.where(sel_mask, logits, neg_inf), axis=-1)
        h = jax.nn.relu(jnp.einsum('btd,edh->bteh', x, W1) + b1)
        out = jnp.einsum('bte,bteh,ehd->btd', gates, h, W2)
        out = out + jnp.einsum('bte,ed->btd', gates, b2)
        return out

    def _L1_attn_ref(in_features, Wq, Wk, Wv, Wo):
        import jax, jax.numpy as jnp
        import numpy as np
        B, S, D, H = (2, 512, 256, 16)
        DH = D // H
        seq_len = in_features.shape[-2]
        q = in_features @ Wq.T
        k = in_features @ Wk.T
        v = in_features @ Wv.T

        def split(x):
            return jnp.moveaxis(x.reshape(*x.shape[:-1], H, DH), -3, -2)
        q, k, v = (split(q), split(k), split(v))
        scores = jnp.einsum('...hqd,...hkd->...hqk', q, k) / np.sqrt(DH)
        causal = jnp.triu(jnp.ones((seq_len, seq_len), bool), k=1)
        scores = jnp.where(causal, jnp.float32(-1000000000.0), scores)
        weights = jax.nn.softmax(scores, axis=-1)
        out = jnp.einsum('...hqk,...hkd->...hqd', weights, v)
        out = jnp.moveaxis(out, -3, -2).reshape(*in_features.shape[:-1], D)
        return out @ Wo.T

    def _L1_xattn_ref(query, key, value, mask, Wq, bq, Wk, bk, Wv, bv, Wo, bo):
        import jax, jax.numpy as jnp
        import numpy as np
        N_HEADS = 16
        N_UNITS = 256
        D_K = N_UNITS // N_HEADS
        B, S = (4, 512)
        b, s, _ = query.shape

        def proj(x, W, bias):
            return (x @ W.T + bias).reshape(b, s, N_HEADS, D_K).transpose(0, 2, 1, 3)
        q = proj(query, Wq, bq)
        k = proj(key, Wk, bk)
        v = proj(value, Wv, bv)
        scores = jnp.einsum('bhqd,bhkd->bhqk', q, k) / np.sqrt(D_K)
        scores = jnp.where(mask[:, None, :, :] == 0, jnp.float32(-1000000000.0), scores)
        attn = jax.nn.softmax(scores, axis=-1)
        out = jnp.einsum('bhqk,bhkd->bhqd', attn, v)
        out = out.transpose(0, 2, 1, 3).reshape(b, s, N_UNITS)
        return out @ Wo.T + bo

    def _L1_ffn_ref(x, Wqkv, q_scale, k_scale, Wo, ln_g, ln_b, W1, b1, W2, b2):
        import jax, jax.numpy as jnp
        import numpy as np
        DIM = 256
        DEPTH = 6
        HEADS = 16
        DIM_HEAD = 64
        WINDOW = 64
        INNER = HEADS * DIM_HEAD
        DIM_INNER = int(DIM * 4 * 2 / 3)
        QK_SCALE = 8.0

        def shift_tokens(t):
            a, s = jnp.split(t, 2, -1)
            s = jnp.pad(s, ((0, 0), (1, 0), (0, 0)))[:, :-1]
            return jnp.concatenate([a, s], -1)

        def l2norm(t):
            return t / jnp.maximum(jnp.linalg.norm(t, axis=-1, keepdims=True), 1e-12)

        def rotate_half(x):
            x1, x2 = jnp.split(x, 2, -1)
            return jnp.concatenate([-x2, x1], -1)

        def rotary_tables(n):
            half = jnp.arange(0, DIM_HEAD, 2, dtype=jnp.float32)
            inv_freq = 1.0 / 10000.0 ** (half / DIM_HEAD)
            t = jnp.arange(n, dtype=jnp.float32)
            freqs = t[:, None] * inv_freq[None, :]
            freqs = jnp.concatenate([freqs, freqs], -1)
            base_scale = (half + 0.4 * DIM_HEAD) / (1.4 * DIM_HEAD)
            power = (t - n // 2) / (WINDOW // 2)
            scale = base_scale[None, :] ** power[:, None]
            scale = jnp.concatenate([scale, scale], -1)
            return (freqs, scale)

        def local_attention(q, k, v):
            b, h, n, d = q.shape
            w = WINDOW
            nw = n // w
            bq = q.reshape(b, h, nw, w, d)
            bk = k.reshape(b, h, nw, w, d)
            bv = v.reshape(b, h, nw, w, d)

            def look(t):
                p = jnp.pad(t, ((0, 0), (0, 0), (1, 0), (0, 0), (0, 0)))
                return jnp.concatenate([p[:, :, :nw], p[:, :, 1:]], axis=3)
            bk2, bv2 = (look(bk), look(bv))
            seq = jnp.arange(n).reshape(nw, w)
            seq_p = jnp.pad(seq, ((1, 0), (0, 0)), constant_values=-1)
            jt = jnp.concatenate([seq_p[:nw], seq_p[1:]], axis=1)
            it = seq[:, :, None]
            jb = jt[:, None, :]
            mask = (it < jb) | (it > jb + w) | (jb == -1)
            sim = jnp.einsum('bhwie,bhwje->bhwij', bq, bk2) * QK_SCALE
            sim = jnp.where(mask, -jnp.finfo(sim.dtype).max, sim)
            attn = jax.nn.softmax(sim, -1)
            out = jnp.einsum('bhwij,bhwje->bhwie', attn, bv2)
            return out.reshape(b, h, n, d)

        def attn_layer(x, Wqkv, qs, ksc, Wo):
            b, n, _ = x.shape
            qkv = x @ Wqkv
            q, k, v = jnp.split(qkv, 3, -1)
            sh = lambda t: t.reshape(b, n, HEADS, DIM_HEAD).transpose(0, 2, 1, 3)
            q, k, v = (sh(q), sh(k), sh(v))
            q = l2norm(q) * qs
            k = l2norm(k) * ksc
            freqs, scale = rotary_tables(n)
            cos, sin = (jnp.cos(freqs), jnp.sin(freqs))
            q = q * cos * scale + rotate_half(q) * sin * scale
            inv = 1.0 / scale
            k = k * cos * inv + rotate_half(k) * sin * inv
            out = local_attention(q, k, v)
            out = out.transpose(0, 2, 1, 3).reshape(b, n, INNER)
            return out @ Wo

        def ffn_layer(x, g, bln, W1, b1, W2, b2):
            mu = x.mean(-1, keepdims=True)
            var = ((x - mu) ** 2).mean(-1, keepdims=True)
            xn = (x - mu) / jnp.sqrt(var + 1e-05) * g + bln
            hg = xn @ W1 + b1
            a, gate = jnp.split(hg, 2, -1)
            return a * jax.nn.gelu(gate, approximate=False) @ W2 + b2
        for i in range(DEPTH):
            x = attn_layer(shift_tokens(x), Wqkv[i], q_scale[i], k_scale[i], Wo[i]) + x
            x = ffn_layer(shift_tokens(x), ln_g[i], ln_b[i], W1[i], b1[i], W2[i], b2[i]) + x
        return x
    x = _layernorm(x + _L0_attn_ref(x, L0_attn_Wq, L0_attn_bq, L0_attn_Wk, L0_attn_bk, L0_attn_Wv, L0_attn_bv), axis=-1)
    x = _layernorm(x + _L0_xattn_ref(x, ctx_1024, ctx_1024, mask_Bx1xS2_ik0, L0_xattn_Wq, L0_xattn_bq, L0_xattn_Wk, L0_xattn_bk, L0_xattn_Wv, L0_xattn_bv), axis=-1)
    x = _layernorm(x + _L0_ffn_ref(x, L0_ffn_Wr, L0_ffn_br, L0_ffn_W1, L0_ffn_b1, L0_ffn_W2, L0_ffn_b2), axis=-1)
    x = _layernorm(x + _L1_attn_ref(x, L1_attn_Wq, L1_attn_Wk, L1_attn_Wv, L1_attn_Wo), axis=-1)
    x = _layernorm(x + _L1_xattn_ref(x, ctx_1024, ctx_1024, mask_BxSxS2_ik0, L1_xattn_Wq, L1_xattn_bq, L1_xattn_Wk, L1_xattn_bk, L1_xattn_Wv, L1_xattn_bv, L1_xattn_Wo, L1_xattn_bo), axis=-1)
    x = _layernorm(x + _L1_ffn_ref(x, L1_ffn_Wqkv, L1_ffn_q_scale, L1_ffn_k_scale, L1_ffn_Wo, L1_ffn_ln_g, L1_ffn_ln_b, L1_ffn_W1, L1_ffn_b1, L1_ffn_W2, L1_ffn_b2), axis=-1)
    return x

_drawn_inputs = setup_inputs


def setup_inputs(seed=0):
    import zlib

    import numpy as np

    out = dict(_drawn_inputs(seed))
    spreads = {'L0_xattn_bq': (0.0, 0.8),
     'L0_xattn_bk': (0.0, 0.8),
     'L0_xattn_bv': (0.0, 0.1),
     'L0_ffn_br': (0.0, 0.1),
     'L0_ffn_b1': (0.0, 0.392),
     'L0_ffn_b2': (0.0, 0.1),
     'L1_xattn_bq': (0.0, 0.416),
     'L1_xattn_bk': (0.0, 0.8),
     'L1_xattn_bv': (0.0, 0.1),
     'L1_xattn_bo': (0.0, 0.1),
     'L1_ffn_q_scale': (1.0, 0.6),
     'L1_ffn_k_scale': (1.0, 0.6),
     'L1_ffn_ln_g': (1.0, 0.6),
     'L1_ffn_ln_b': (0.0, 0.8),
     'L1_ffn_b1': (0.0, 0.462),
     'L1_ffn_b2': (0.0, 0.1)}
    factors = {'L0_attn_bq': 3.554, 'L0_attn_bk': 4.906, 'L0_xattn_Wq': 4.321, 'L0_xattn_Wk': 4.238}
    for name, (base, spread) in spreads.items():
        noise = np.random.default_rng([zlib.crc32(name.encode()), seed]).standard_normal(out[name].shape)
        drawn = base * np.exp(spread * noise) if base else spread * noise
        out[name] = jnp.asarray(drawn.astype(out[name].dtype))
    for name, factor in factors.items():
        out[name] = (out[name] * factor).astype(out[name].dtype)
    return out
```

```python
from contextlib import ExitStack, contextmanager

import concourse.bass as bass
from concourse import mybir

P = 128
F32 = mybir.dt.float32
ALU = mybir.AluOpType
ACT = mybir.ActivationFunctionType
AX = mybir.AxisListType
PSUM_BANKS = 8
BANK = 512
LOWEST = -3.0e38
LN_EPS = 1e-5
MASKED = -1.0e30


class Psum:

    def __init__(self, shared, first=0):
        self.first = first
        self.tensor, self.filled, self.drained = shared["psum"], shared["filled"], shared["drained"]
        self.earlier = shared["contents"]
        self.bank, self.number, self.per = {}, {}, [0] * PSUM_BANKS

    def fill(self, key, bank):
        assert key not in self.bank, key
        self.bank[key], self.number[key] = bank, self.per[bank] + 1
        self.per[bank] += 1

    def finish(self, shared, iterations):
        shared["contents"] = [n + iterations * m for n, m in zip(self.earlier, self.per)]

    def ap(self, key):
        return self.tensor[:, self.bank[key], :]

    def sem_filled(self, key):
        return self.filled[self.bank[key]]

    def sem_drained(self, key):
        return self.drained[self.bank[key]]

    def start(self, key, it):
        b = self.bank[key]
        return it * self.per[b] + (self.earlier[b] - self.first * self.per[b])

    def before(self, key, it):
        return self.start(key, it) + (self.number[key] - 1)

    def last_time(self, key, it):
        assert self.earlier[self.bank[key]] + self.number[key] > self.per[self.bank[key]]
        return self.start(key, it) + (self.number[key] - self.per[self.bank[key]])

    def count(self, key, it):
        return self.start(key, it) + self.number[key]


def stage_l1_ffn(nc, shared, w, tabs):
    ident, x_all = shared["ident"], shared["x"]
    L, D, QKV = w["Wqkv"].shape
    INNER = QKV // 3
    HID = w["W2"].shape[1]
    H, DH = 16, 64
    TB = 4
    NB = x_all.shape[1] // TB
    KC = D // P
    OC = INNER // P
    HC = -(-HID // P)
    HREM = HID - (HC - 1) * P
    HALF = INNER // 2
    G = H // 4
    QK_SCALE = 8.0

    with ExitStack() as ctx:
        def sb(name, shape):
            return ctx.enter_context(nc.sbuf_tensor("f_" + name, shape, F32))

        def sem(name):
            return shared["sems"].enter_context(nc.semaphore("f_" + name))

        wqkv = sb("wqkv", [P, KC, QKV])
        wo = sb("wo", [P, OC, D])
        w1 = sb("w1", [P, KC, 2 * HID])
        w2 = sb("w2", [P, HC, D])
        ln_g = sb("ln_g", [P, KC])
        ln_b = sb("ln_b", [P, KC])
        b1a = sb("b1a", [P, HC])
        b1g = sb("b1g", [P, HC])
        b2 = sb("b2", [P, D])
        qks = sb("qks", [P, 4, DH])
        rope = sb("rope", [P, TB, 4, DH])
        tab = sb("tab", [P, TB, 4, DH])
        band = sb("band", [P, 2, 2 * P])
        xin = sb("xin", [P, TB, D])
        xsT = sb("xsT", [P, KC, TB * P + 1])
        raw = sb("raw", [P, 8, HALF])
        sq = sb("sq", [P, 2, HALF])
        rot = sb("rot", [P, 2, 2, HALF])
        ss = sb("ss", [P, 2, 4 * 8])
        rn = sb("rn", [P, 2, 4 * 8])
        half_pow = sb("half_pow", [P, 4 * 8])
        rq8 = sb("rq8", [P, 2, H])
        qT = sb("qT", [P, H // 2, P])
        kT = sb("kT", [P, H // 2, (TB + 1) * P])
        v = sb("v", [P, TB, INNER])
        prob = sb("prob", [P, 12, 2 * P])
        mx = sb("mx", [P, 2, H])
        nb = sb("nb", [P, 2, H])
        sums = sb("sums", [P, 2, H])
        rs = sb("rs", [P, 2, H])
        pT = sb("pT", [P, 4, BANK])
        oT = sb("oT", [P, OC, P])
        xs = sb("xs", [P, TB, P])
        xn = sb("xn", [P, TB, D])
        xnT = sb("xnT", [P, KC, TB * P])
        stat = sb("stat", [P, TB, 12])
        mv = sb("mv", [P, TB, 2])
        rstd = sb("rstd", [P, 2, TB])
        x1 = sb("x1", [P, TB, D])
        hT = sb("hT", [P, HC, TB * P])

        w_attn = sem("w_attn")
        w_wo = sem("w_wo")
        w_ffn = sem("w_ffn")
        consts = sem("consts")
        pads = sem("pads")
        passed = sem("passed")
        tab_ready = sem("tab_ready")
        xin_ready = sem("xin_ready")
        sq_ready = sem("sq_ready")
        rot_ready = sem("rot_ready")
        rope_done = sem("rope_done")
        ss_ready = sem("ss_ready")
        ssm_ready = sem("ssm_ready")
        rn_ready = sem("rn_ready")
        qk_ready = sem("qk_ready")
        nb_ready = sem("nb_ready")
        exp_ready = sem("exp_ready")
        pv_done = sem("pv_done")
        rs_ready = sem("rs_ready")
        prob_ready = sem("prob_ready")
        x1_ready = sem("x1_ready")
        attn_weights = sem("attn_weights")
        wo_weights = sem("wo_weights")
        ffn_weights = sem("ffn_weights")
        xs_ready = sem("xs_ready")
        stat_ready = sem("stat_ready")
        mv_ready = sem("mv_ready")
        eps_ready = sem("eps_ready")
        rstd_ready = sem("rstd_ready")
        xn_ready = sem("xn_ready")
        x1b_ready = sem("x1b_ready")
        x_ready = sem("x_ready")
        h_ready = sem("h_ready")

        def scores_on(t):
            for g in range(G + 3):
                if g < G:
                    yield ("s", t, g)
                if 1 <= g <= G:
                    yield ("r", t, g - 1)
                if 2 <= g <= G + 1:
                    yield ("pt", t, g - 2)
                if 3 <= g:
                    yield ("pv", t, g - 3)
                if g == 1 and t >= 1:
                    yield ("wo", t - 1)
                if g == G - 1 and t + 2 < TB:
                    yield ("qkv", t + 2)

        attention_start = [("tab",), ("xt",), ("qkv", 0), ("qkv", 1)]
        attention_rest = []
        for t in range(TB):
            attention_rest += [("tr", t), *scores_on(t)]
        attention_rest += [("wo", TB - 1), ("xin",)]
        norm_start = [("xs",), ("ln",)]
        mlp_rest = [("xnt",)] + [("f1", c) for c in range(HC)] + [("f2", t) for t in range(TB)]

        def merged():
            out = norm_start + attention_start[:3]
            out += mlp_rest[:3] + attention_start[3:] + mlp_rest[3:]
            return out + attention_rest

        ITS = L * NB
        phases = []
        for steps, first, end in ((attention_start + attention_rest, 0, 1), (merged(), 1, ITS),
                                  (norm_start + mlp_rest, ITS, ITS + 1)):
            ps = Psum(shared, first)
            ring = {"p": 0, "t": 0}
            for step in steps:
                kind = step[0]
                if kind in ("xt", "tr", "xnt", "pt"):
                    for i in range(4 if kind == "tr" else 2):
                        ps.fill(step + (i,), 2 + ring["t"] % 2)
                        ring["t"] += 1
                elif kind == "qkv":
                    for i in range(6):
                        ps.fill(step + (i,), ring["p"] % 2)
                        ring["p"] += 1
                elif kind == "s":
                    for i in range(2):
                        ps.fill(step + (i,), 4 + i)
                elif kind == "pv" and step[2] % 2 == 0:
                    ps.fill(("o", step[1], step[2] // 2), 6 + step[2] // 2 % 2)
                elif kind == "wo":
                    ps.fill(step, ring["p"] % 2)
                    ring["p"] += 1
                elif kind == "f1":
                    for i in range(2):
                        ps.fill(step + (i,), 4 + 2 * (step[1] % 2) + i)
                elif kind == "f2":
                    ps.fill(step, 4 + step[1] % 4)
            ps.finish(shared, end - first)
            phases.append((steps, ps, first, end))

        @contextmanager
        def each(engine, first, end):
            if end - first == 1:
                yield first
            else:
                with engine.Fori(first, end) as it:
                    yield it

        def mlp_of(it):
            return it - 1

        NQ = 4 * TB
        NG = G * TB

        def heads(ap):
            return ap.rearrange("p (h d) -> p h d", d=DH)

        block = ctx.enter_context(nc.Block())

        @block.sync
        def _(sp):
            def load_attn(l):
                sp.dma_start(wqkv[:], w["Wqkv"][l].rearrange("(c p) n -> p c n", p=P)).then_inc(w_attn, 16)
                for i, name in enumerate(("q_scale", "q_swap", "k_scale", "k_swap")):
                    sp.dma_start(qks[:, i, :], w[name][l].partition_broadcast(P)).then_inc(w_attn, 16)

            def load_wo(l):
                sp.dma_start(wo[:], w["Wo"][l].rearrange("(c p) n -> p c n", p=P)).then_inc(w_wo, 16)

            def load_ffn(l):
                sp.dma_start(w1[:], w["W1"][l].rearrange("(c p) n -> p c n", p=P)).then_inc(w_ffn, 16)
                sp.dma_start(w2[:, 0:HC - 1, :],
                             w["W2"][l][0:(HC - 1) * P].rearrange("(c p) n -> p c n", p=P)).then_inc(w_ffn, 16)
                sp.dma_start(w2[0:HREM, HC - 1, :], w["W2"][l][(HC - 1) * P:HID]).then_inc(w_ffn, 16)
                sp.dma_start(ln_g[:], w["ln_g"][l]).then_inc(w_ffn, 16)
                sp.dma_start(ln_b[:], w["ln_b"][l]).then_inc(w_ffn, 16)
                sp.dma_start(b1a[:], w["b1a"][l]).then_inc(w_ffn, 16)
                sp.dma_start(b1g[:], w["b1g"][l]).then_inc(w_ffn, 16)
                sp.dma_start(b2[:], w["b2"][l].partition_broadcast(P)).then_inc(w_ffn, 16)

            def announce(l, which=("attn", "wo", "ffn")):
                if "attn" in which:
                    sp.wait_ge(w_attn, (l + 1) * 80)
                    sp.sem_inc(attn_weights, NB)
                if "wo" in which:
                    sp.wait_ge(w_wo, (l + 1) * 16)
                    sp.sem_inc(wo_weights, NB)
                if "ffn" in which:
                    sp.wait_ge(w_ffn, (l + 1) * 128)
                    sp.sem_inc(ffn_weights, NB)

            sp.dma_start(rope[:], tabs["rope"]).then_inc(consts, 16)
            sp.dma_start(band[:], tabs["band"]).then_inc(consts, 16)
            load_attn(0)
            load_ffn(0)
            load_wo(0)
            announce(0)
            ps = phases[1][1]
            with sp.Fori(1, L) as l:
                last = l * NB - 1
                key = ("qkv", TB - 1, 5)
                sp.wait_ge(ps.sem_filled(key), ps.count(key, last))
                load_attn(l)
                key = ("wo", TB - 1)
                sp.wait_ge(ps.sem_filled(key), ps.count(key, last))
                load_wo(l)
                announce(l, ("attn", "wo"))
                key = ("f2", TB - 1)
                sp.wait_ge(ps.sem_drained(key), ps.count(key, last + 1))
                load_ffn(l)
                announce(l, ("ffn",))

        @block.tensor
        def _(pe):
            def transposes(key, it, parts):
                pe.wait_ge(ps.sem_drained(key), ps.before(key, it))
                for n, (slot, src) in enumerate(parts):
                    mm = nc.tensor.transpose(ps.ap(key)[:, slot * P:(slot + 1) * P], src, ident[:])
                mm.then_inc(ps.sem_filled(key), 1)

            def wait_drained(key, it):
                pe.wait_ge(ps.sem_drained(key), ps.count(key, it))

            pe.wait_ge(pads, 1)
            for steps, ps, first, end in phases:
                with each(pe, first, end) as it:
                    for step in steps:
                        kind = step[0]
                        if kind == "xt":
                            pe.wait_ge(xin_ready, it + 1)
                            for c in range(KC):
                                transposes(("xt", c), it, [(t, xin[:, t, c * P:(c + 1) * P]) for t in range(TB)])
                        elif kind == "qkv":
                            t = step[1]
                            if t == 0:
                                for c in range(KC):
                                    wait_drained(("xt", c), it)
                                pe.wait_ge(attn_weights, it + 1)
                            for i in range(6):
                                key = step + (i,)
                                pe.wait_ge(ps.sem_drained(key), ps.before(key, it))
                                for c in range(KC):
                                    mm = nc.tensor.matmul(ps.ap(key), xsT[:, c, t * P:(t + 1) * P],
                                                          wqkv[:, c, i * HALF:(i + 1) * HALF],
                                                          start=c == 0, stop=c == KC - 1)
                                mm.then_inc(ps.sem_filled(key), 1)
                        elif kind == "tr":
                            t = step[1]
                            for i in range(4):
                                s = 4 * t + i
                                if i < 2:
                                    pe.wait_ge(rope_done, it * NQ + s + 1)
                                else:
                                    pe.wait_ge(qk_ready, it * 2 * TB + 2 * t + i - 1)
                                transposes(step + (i,), it, [(n, raw[:, s % 8, n * P:(n + 1) * P]) for n in range(4)])
                        elif kind == "s":
                            t, g = step[1:]
                            if g % 2 == 0:
                                wait_drained(("tr", t, g // 2), it)
                                wait_drained(("tr", t, 2 + g // 2), it)
                            for i in range(2):
                                key = step + (i,)
                                pe.wait_ge(ps.sem_drained(key), ps.before(key, it))
                                rows = slice(i * DH, (i + 1) * DH)
                                for n in range(2):
                                    mm = nc.tensor.matmul(ps.ap(key)[:, n * 2 * P:(n + 1) * 2 * P],
                                                          qT[rows, 2 * g + n, :],
                                                          kT[rows, 2 * g + n, t * P:(t + 2) * P],
                                                          start=True, stop=True)
                                mm.then_inc(ps.sem_filled(key), 1)
                        elif kind == "pt":
                            t, g = step[1:]
                            pe.wait_ge(prob_ready, it * NG + t * G + g + 1)
                            for i in range(2):
                                parts = [(2 * n + k, prob[:, (4 * (t * G + g) + 2 * i + n) % 12, k * P:(k + 1) * P])
                                         for n in range(2) for k in range(2) if t or k]
                                transposes(step + (i,), it, parts)
                        elif kind == "pv":
                            t, g = step[1:]
                            okey = ("o", t, g // 2)
                            if g % 2 == 0:
                                pe.wait_ge(ps.sem_drained(okey), ps.before(okey, it))
                            for i in range(2):
                                wait_drained(("pt", t, g, i), it)
                                pair = 2 * g + i
                                slot = (2 * (t * G + g) + i) % 4
                                for k in range(2):
                                    for n in range(2):
                                        h = 2 * pair + n
                                        if t or k:
                                            mm = nc.tensor.matmul(
                                                ps.ap(okey)[n * DH:(n + 1) * DH, pair % 4 * P:(pair % 4 + 1) * P],
                                                v[:, t - 1 + k, h * DH:(h + 1) * DH],
                                                pT[:, slot, (2 * n + k) * P:(2 * n + k + 1) * P],
                                                start=(k == 0 or t == 0), stop=k == 1, skip_group_check=True)
                            mm.then_inc(pv_done, 1)
                            if g % 2 == 1:
                                pe.wait_ge(pv_done, it * NG + t * G + g + 1)
                                pe.sem_inc(ps.sem_filled(okey), 1)
                        elif kind == "wo":
                            t = step[1]
                            if t == 0:
                                pe.wait_ge(wo_weights, it + 1)
                            for i in range(2):
                                wait_drained(("o", t, i), it)
                            pe.wait_ge(ps.sem_drained(step), ps.before(step, it))
                            for c in range(OC):
                                mm = nc.tensor.matmul(ps.ap(step)[:, 0:D], oT[:, c, :], wo[:, c, :],
                                                      start=c == 0, stop=c == OC - 1)
                            mm.then_inc(ps.sem_filled(step), 1)
                        elif kind == "xnt":
                            for c in range(KC):
                                pe.wait_ge(xn_ready, mlp_of(it) + 1)
                                transposes(step + (c,), it, [(t, xn[:, t, c * P:(c + 1) * P]) for t in range(TB)])
                        elif kind == "f1":
                            ch = step[1]
                            if ch == 0:
                                pe.wait_ge(ffn_weights, mlp_of(it) + 1)
                                for c in range(KC):
                                    wait_drained(("xnt", c), it)
                            m = P if ch < HC - 1 else HREM
                            for i in range(2):
                                key = step + (i,)
                                pe.wait_ge(ps.sem_drained(key), ps.before(key, it))
                                for c in range(KC):
                                    at = i * HID + ch * P
                                    mm = nc.tensor.matmul(ps.ap(key)[0:m, :], w1[:, c, at:at + m], xnT[:, c, :],
                                                          start=c == 0, stop=c == KC - 1)
                                mm.then_inc(ps.sem_filled(key), 1)
                        elif kind == "f2":
                            t = step[1]
                            pe.wait_ge(ps.sem_drained(step), ps.before(step, it))
                            for c in range(HC):
                                if t == 0:
                                    pe.wait_ge(h_ready, mlp_of(it) * HC + c + 1)
                                m = P if c < HC - 1 else HREM
                                mm = nc.tensor.matmul(ps.ap(step)[:, 0:D], hT[0:m, c, t * P:(t + 1) * P],
                                                      w2[0:m, c, :], start=c == 0, stop=c == HC - 1)
                            mm.then_inc(ps.sem_filled(step), 1)

        def evacuate_probs(eng, copy, ps, step, it, i):
            t, g = step[1:]
            n = t * G + g
            key = step + (i,)
            if n >= 2:
                eng.wait_ge(pv_done, it * NG + n - 1)
            eng.wait_ge(ps.sem_filled(key), ps.count(key, it))
            first = 0 if t else 1
            src = ps.ap(key).rearrange("p (n k q) -> p n k q", n=2, k=2)[:, :, first:2, :]
            dst = pT[:, (2 * n + i) % 4, :].rearrange("p (n k q) -> p n k q", n=2, k=2)[:, :, first:2, :]
            copy(dst, src).then_inc(ps.sem_drained(key), 1)

        @block.scalar
        def _(act):
            def wait_filled(key, it):
                act.wait_ge(ps.sem_filled(key), ps.count(key, it))

            act.wait_ge(pads, 1)
            for steps, ps, first, end in phases:
                with each(act, first, end) as it:
                    for step in steps:
                        kind = step[0]
                        if kind == "xt":
                            for c in range(KC):
                                key = ("xt", c)
                                wait_filled(key, it)
                                nc.scalar.copy(xsT[:, c, c:c + TB * P], ps.ap(key)).then_inc(ps.sem_drained(key), 1)
                        elif kind == "qkv":
                            t = step[1]
                            for i in range(6):
                                key = step + (i,)
                                if i < 4 and t >= 2:
                                    old = ("tr", t - 2, i)
                                    wait_filled(old, it)
                                wait_filled(key, it)
                                dst = raw[:, (4 * t + i) % 8, :] if i < 4 else v[:, t, (i - 4) * HALF:(i - 3) * HALF]
                                nc.scalar.copy(dst, ps.ap(key)).then_inc(ps.sem_drained(key), 1)
                        elif kind == "tr":
                            t = step[1]
                            for i in range(4):
                                key = step + (i,)
                                wait_filled(key, it)
                                src = ps.ap(key).rearrange("p (n q) -> p n q", q=P)
                                n = 4 * (i % 2)
                                dst = qT[:, n:n + 4, :] if i < 2 else kT[:, n:n + 4, (t + 1) * P:(t + 2) * P]
                                nc.scalar.copy(dst, src).then_inc(ps.sem_drained(key), 1)
                        elif kind == "s":
                            t, g = step[1:]
                            act.wait_ge(nb_ready, it * NG + t * G + g + 1)
                            for n in range(4):
                                h = 4 * g + n
                                pr = prob[:, (4 * (t * G + g) + n) % 12, :]
                                ex = nc.scalar.activation(pr, pr, ACT.Exp, bias=nb[:, t % 2, h:h + 1],
                                                          scale=rq8[:, t % 2, h:h + 1],
                                                          accum_out=sums[:, t % 2, h:h + 1])
                            ex.then_inc(exp_ready, 1)
                        elif kind == "pt":
                            evacuate_probs(act, nc.scalar.copy, ps, step, it, 0)
                        elif kind == "pv":
                            t, g = step[1:]
                            if g % 2 == 1:
                                key = ("o", t, g // 2)
                                if t >= 1:
                                    wait_filled(("wo", t - 1), it)
                                wait_filled(key, it)
                                nc.scalar.copy(oT[:, 4 * (g // 2):4 * (g // 2) + 4, :],
                                               ps.ap(key).rearrange("p (n q) -> p n q", q=P)
                                               ).then_inc(ps.sem_drained(key), 1)
                        elif kind == "xs":
                            act.wait_ge(x1_ready, mlp_of(it) + 1)
                            act.dma_start(xs[1:P, :, :], x1[0:P - 1, :, P:D]).then_inc(xs_ready, 16)
                            act.dma_start(xs[0:1, 1:TB, :], x1[P - 1:P, 0:TB - 1, P:D]).then_inc(xs_ready, 16)
                        elif kind == "xnt":
                            act.wait_ge(ffn_weights, mlp_of(it) + 1)
                            for c in range(KC):
                                key = step + (c,)
                                wait_filled(key, it)
                                nc.scalar.activation(xnT[:, c, :], ps.ap(key), ACT.Identity, bias=ln_b[:, c:c + 1],
                                                     scale=ln_g[:, c:c + 1]).then_inc(ps.sem_drained(key), 1)
                        elif kind == "f1":
                            ch = step[1]
                            m = P if ch < HC - 1 else HREM
                            key = step + (1,)
                            wait_filled(key, it)
                            nc.scalar.activation(hT[0:m, ch, :], ps.ap(key)[0:m], ACT.Gelu,
                                                 bias=b1g[0:m, ch:ch + 1]).then_inc(ps.sem_drained(key), 1)

        @block.vector
        def _(dve):
            def wait_filled(key, it):
                dve.wait_ge(ps.sem_filled(key), ps.count(key, it))

            def wait_drained(key, it):
                dve.wait_ge(ps.sem_drained(key), ps.count(key, it))

            def evac(out, in_):
                return nc.vector.tensor_copy(out, in_)

            nc.vector.memset(kT[:, :, 0:P], 0.0)
            nc.vector.memset(xsT[:, 1, 0:1], 0.0)
            nc.vector.memset(xs[0:1, 0, :], 0.0)
            nc.vector.memset(half_pow[:], -0.5).then_inc(pads, 1)
            dve.wait_ge(consts, 32)
            for steps, ps, first, end in phases:
                with each(dve, first, end) as it:
                    for step in steps:
                        kind = step[0]
                        if kind == "qkv":
                            t = step[1]
                            if t == 0:
                                dve.wait_ge(tab_ready, it + 1)
                            for i in range(4):
                                s = 4 * t + i
                                wait_drained(step + (i,), it)
                                if s >= 2:
                                    dve.wait_ge(rope_done, it * NQ + s - 1)
                                q = raw[:, s % 8, :]
                                kindq = 2 * (i // 2)
                                cos = tab[:, t:t + 1, kindq, :].broadcast_to([P, 8, DH])
                                sin = tab[:, t:t + 1, kindq + 1, :].broadcast_to([P, 8, DH])
                                nc.vector.tensor_tensor(heads(rot[:, s % 2, 0, :]), heads(q), cos, ALU.mult)
                                swapped = q.rearrange("p (h two d) -> p h two d", two=2, d=DH // 2)[:, :, ::-1, :]
                                nc.vector.tensor_tensor(
                                    rot[:, s % 2, 1, :].rearrange("p (h two d) -> p h two d", two=2, d=DH // 2),
                                    swapped, sin.rearrange("p h (two d) -> p h two d", two=2),
                                    ALU.mult).then_inc(rot_ready, 1)
                                dve.wait_ge(sq_ready, it * NQ + s + 1)
                                nc.vector.tensor_reduce(ss[:, t % 2, 8 * i:8 * i + 8], heads(sq[:, s % 2, :]), AX.X,
                                                        ALU.add).then_inc(ss_ready, 1)
                            dve.wait_ge(ss_ready, it * NQ + 4 * t + 4)
                            nc.vector.tensor_scalar(ss[:, t % 2, :], ss[:, t % 2, :], 1e-24, None,
                                                    ALU.max).then_inc(ssm_ready, 1)
                            dve.wait_ge(rn_ready, it * TB + t + 1)
                            nc.vector.tensor_scalar(rq8[:, t % 2, :], rn[:, t % 2, 0:H], QK_SCALE, None, ALU.mult)
                            for i in range(2, 4):
                                s = 4 * t + i
                                dve.wait_ge(rope_done, it * NQ + s + 1)
                                k = heads(raw[:, s % 8, :])
                                norm = rn[:, t % 2, 8 * i:8 * i + 8].unsqueeze(2).broadcast_to([P, 8, DH])
                                nc.vector.tensor_tensor(k, k, norm, ALU.mult).then_inc(qk_ready, 1)
                        elif kind == "s":
                            t, g = step[1:]
                            n = t * G + g
                            if n >= 3:
                                old = ("pt", (n - 3) // G, (n - 3) % G)
                                for i in range(2):
                                    wait_filled(old + (i,), it)
                            for i in range(2):
                                key = step + (i,)
                                wait_filled(key, it)
                                dve.sem_inc(passed, 1)
                                for j in range(2):
                                    h = 4 * g + 2 * j + i
                                    red = nc.vector.tensor_tensor_reduce(
                                        prob[:, (4 * n + 2 * j + i) % 12, :], ps.ap(key)[:, j * 2 * P:(j + 1) * 2 * P],
                                        band[:, min(t, 1), :], 1.0, LOWEST, ALU.add, ALU.max,
                                        mx[:, t % 2, h:h + 1])
                                red.then_inc(ps.sem_drained(key), 1)
                            for i in range(2):
                                wait_drained(step + (i,), it)
                            nc.vector.scalar_tensor_tensor(
                                out=nb[:, t % 2, 4 * g:4 * g + 4], in0=mx[:, t % 2, 4 * g:4 * g + 4], scalar=-1.0,
                                in1=rq8[:, t % 2, 4 * g:4 * g + 4], op0=ALU.mult, op1=ALU.mult).then_inc(nb_ready, 1)
                        elif kind == "pt":
                            evacuate_probs(dve, evac, ps, step, it, 1)
                        elif kind == "r":
                            t, g = step[1:]
                            dve.wait_ge(exp_ready, it * NG + t * G + g + 1)
                            nc.vector.reciprocal(rs[:, t % 2, 4 * g:4 * g + 4],
                                                 sums[:, t % 2, 4 * g:4 * g + 4]).then_inc(rs_ready, 1)
                        elif kind == "wo":
                            t = step[1]
                            wait_filled(step, it)
                            nc.vector.tensor_tensor(x1[:, t, :], ps.ap(step)[:, 0:D],
                                                    x_all[:, it % NB * TB + t, :],
                                                    ALU.add).then_inc(ps.sem_drained(step), 1)
                            if t == TB - 1:
                                wait_drained(step, it)
                                dve.sem_inc(x1_ready, 1)
                        elif kind == "ln":
                            f = mlp_of(it)
                            dve.wait_ge(xs_ready, (f + 1) * 32)
                            for t in range(TB):
                                nc.vector.bn_stats(stat[:, t, 0:6], x1[:, t, 0:P])
                                ins = nc.vector.bn_stats(stat[:, t, 6:12], xs[:, t, :])
                            ins.then_inc(stat_ready, 1)
                            dve.wait_ge(stat_ready, f + 1)
                            dve.sem_inc(passed, 1)
                            for t in range(TB):
                                agg = nc.vector.bn_aggr(mv[:, t, :], stat[:, t, :])
                            agg.then_inc(mv_ready, 1)
                            dve.wait_ge(mv_ready, f + 1)
                            nc.vector.tensor_scalar(rstd[:, 0, :], mv[:, :, 1], LN_EPS, None,
                                                    ALU.add).then_inc(eps_ready, 1)
                            dve.wait_ge(rstd_ready, f + 1)
                            for t in range(TB):
                                for c, src in enumerate((x1[:, t, 0:P], xs[:, t, :])):
                                    ins = nc.vector.tensor_scalar(xn[:, t, c * P:(c + 1) * P], src, mv[:, t, 0:1],
                                                                  rstd[:, 1, t:t + 1], ALU.subtract, ALU.mult)
                            ins.then_inc(xn_ready, 1)
                        elif kind == "f1":
                            ch = step[1]
                            m = P if ch < HC - 1 else HREM
                            f = mlp_of(it)
                            if ch == 0:
                                dve.wait_ge(ffn_weights, f + 1)
                            wait_filled(step + (0,), it)
                            wait_drained(step + (1,), it)
                            nc.vector.scalar_tensor_tensor(
                                out=hT[0:m, ch, :], in0=ps.ap(step + (0,))[0:m], scalar=b1a[0:m, ch:ch + 1],
                                in1=hT[0:m, ch, :], op0=ALU.add, op1=ALU.mult).then_inc(h_ready, 1)
                            dve.wait_ge(h_ready, f * HC + ch + 1)
                            dve.sem_inc(ps.sem_drained(step + (0,)), 1)
                        elif kind == "f2":
                            t = step[1]
                            if t == 0:
                                dve.wait_ge(x1b_ready, mlp_of(it) + 1)
                            wait_filled(step, it)
                            nc.vector.tensor_tensor(x_all[:, mlp_of(it) % NB * TB + t, :], ps.ap(step)[:, 0:D],
                                                    xn[:, t, :], ALU.add).then_inc(ps.sem_drained(step), 1)
                            if t == TB - 1:
                                wait_drained(step, it)
                                dve.sem_inc(x_ready, 1)

        @block.gpsimd
        def _(pool):
            pool.wait_ge(pads, 1)
            pool.wait_ge(consts, 32)

            def copy_x(it):
                nc.gpsimd.tensor_copy(xin[:], x_all[:, bass.ds(it % NB * TB, TB), :]).then_inc(xin_ready, 1)

            copy_x(0)
            pool.sem_inc(x_ready, NB - 1)
            for steps, ps, first, end in phases:
                with each(pool, first, end) as it:
                    for step in steps:
                        kind = step[0]
                        if kind == "xin":
                            pool.wait_ge(x_ready, it + 1)
                            copy_x(it + 1)
                        elif kind == "tab":
                            pool.wait_ge(attn_weights, it + 1)
                            for i in range(4):
                                ins = nc.gpsimd.tensor_tensor(tab[:, :, i, :], rope[:, :, i, :],
                                                              qks[:, i:i + 1, :].broadcast_to([P, TB, DH]), ALU.mult)
                            ins.then_inc(tab_ready, 1)
                        elif kind == "qkv":
                            t = step[1]
                            for i in range(4):
                                s = 4 * t + i
                                key = step + (i,)
                                pool.wait_ge(ps.sem_drained(key), ps.count(key, it))
                                if s >= 2:
                                    pool.wait_ge(ss_ready, it * NQ + s - 1)
                                q = raw[:, s % 8, :]
                                nc.gpsimd.tensor_tensor(sq[:, s % 2, :], q, q, ALU.mult).then_inc(sq_ready, 1)
                                pool.wait_ge(rot_ready, it * NQ + s + 1)
                                pool.wait_ge(sq_ready, it * NQ + s + 1)
                                nc.gpsimd.tensor_tensor(q, rot[:, s % 2, 0, :], rot[:, s % 2, 1, :],
                                                        ALU.add).then_inc(rope_done, 1)
                            pool.wait_ge(ssm_ready, it * TB + t + 1)
                            nc.gpsimd.tensor_tensor(rn[:, t % 2, :], ss[:, t % 2, :], half_pow[:],
                                                    ALU.pow).then_inc(rn_ready, 1)
                        elif kind == "r":
                            t, g = step[1:]
                            n = t * G + g
                            pool.wait_ge(rs_ready, it * NG + n + 1)
                            pr = prob[:, 4 * n % 12:4 * n % 12 + 4, :]
                            nc.gpsimd.tensor_tensor(pr, pr, rs[:, t % 2, 4 * g:4 * g + 4].unsqueeze(2).broadcast_to(
                                [P, 4, 2 * P]), ALU.mult).then_inc(prob_ready, 1)
                        elif kind == "ln":
                            f = mlp_of(it)
                            pool.wait_ge(eps_ready, f + 1)
                            nc.gpsimd.tensor_tensor(rstd[:, 1, :], rstd[:, 0, :], half_pow[:, 0:TB],
                                                    ALU.pow).then_inc(rstd_ready, 1)
                        elif kind == "xnt":
                            for c in range(KC):
                                key = step + (c,)
                                pool.wait_ge(ps.sem_filled(key), ps.count(key, it))
                            pool.wait_ge(ffn_weights, mlp_of(it) + 1)
                            nc.gpsimd.tensor_tensor(xn[:], x1[:], b2[:].unsqueeze(1).broadcast_to([P, TB, D]),
                                                    ALU.add).then_inc(x1b_ready, 1)


class Norm:

    def __init__(self, nc, shared, ctx, stage, y):
        self.nc, self.y, self.x_all, self.half_pow = nc, y, shared["x"], shared["half_pow"]
        self.tiles = y.shape[1]

        def sb(name, shape):
            return ctx.enter_context(nc.sbuf_tensor(f"{stage}_{name}", shape, F32))

        def sem(name):
            return shared["sems"].enter_context(nc.semaphore(f"{stage}_{name}"))

        self.stat = sb("stat", [P, self.tiles, 6])
        self.mv = sb("mv", [P, self.tiles, 2])
        self.rstd = sb("rstd", [P, 2, self.tiles])
        self.stat_ready = sem("stat_ready")
        self.mv_ready = sem("mv_ready")
        self.eps_ready = sem("eps_ready")
        self.rstd_ready = sem("rstd_ready")
        self.x_ready = sem("x_ready")
        self.passed = sem("passed")

    def vector(self, dve, it):
        nc, n = self.nc, self.tiles
        for t in range(n):
            ins = nc.vector.bn_stats(self.stat[:, t, :], self.y[:, t, :])
        ins.then_inc(self.stat_ready, 1)
        dve.wait_ge(self.stat_ready, it + 1)
        dve.sem_inc(self.passed, 1)
        for t in range(n):
            ins = nc.vector.bn_aggr(self.mv[:, t, :], self.stat[:, t, :])
        ins.then_inc(self.mv_ready, 1)
        dve.wait_ge(self.mv_ready, it + 1)
        nc.vector.tensor_scalar(self.rstd[:, 0, :], self.mv[:, :, 1], LN_EPS, None, ALU.add).then_inc(self.eps_ready, 1)
        dve.wait_ge(self.rstd_ready, it + 1)
        for t in range(n):
            ins = nc.vector.tensor_scalar(self.x_all[:, it * n + t, :], self.y[:, t, :], self.mv[:, t, 0:1],
                                          self.rstd[:, 1, t:t + 1], ALU.subtract, ALU.mult)
        ins.then_inc(self.x_ready, 1)

    def gpsimd(self, pool, it):
        pool.wait_ge(self.eps_ready, it + 1)
        self.nc.gpsimd.tensor_tensor(self.rstd[:, 1, :], self.rstd[:, 0, :], self.half_pow[:, 0:self.tiles],
                                     ALU.pow).then_inc(self.rstd_ready, 1)


def stage_wide_attention(nc, shared, stage, w, rope, cross):
    ident, x_all = shared["ident"], shared["x"]
    D = x_all.shape[2]
    TB = 4
    NB = x_all.shape[1] // TB
    S = TB * P
    KC = D // P
    scale = float(D) ** -0.5 if cross else 128.0 ** -0.5

    with ExitStack() as ctx:
        def sb(name, shape, dt=F32):
            return ctx.enter_context(nc.sbuf_tensor(f"{stage}_{name}", shape, dt))

        def sem(name):
            return shared["sems"].enter_context(nc.semaphore(f"{stage}_{name}"))

        ps = Psum(shared)
        xin = sb("xin", [P, TB, D])
        xb = sb("xb", [P, TB, D])
        xT = sb("xT", [P, KC, S])
        qT = sb("qT", [P, KC, S])
        kT = sb("kT", [P, KC, S])
        v = sb("v", [P, TB, D])
        prob = sb("prob", [P, 2, S])
        pT = sb("pT", [P, 2, S])
        mx = sb("mx", [P, TB])
        nb = sb("nb", [P, TB])
        sums = sb("sums", [P, TB])
        rs = sb("rs", [P, TB])
        y = sb("y", [P, TB, D])
        norm = Norm(nc, shared, ctx, stage, y)
        if cross:
            srcT = sb("srcT", [P, KC, S])
            mask_int = sb("mask_int", [P, S], mybir.dt.int32)
            keep = sb("keep", [P, S])
            gone = sb("gone", [P, S])
            add_mask = sb("add_mask", [P, TB, S])
        else:
            srcT = xT
        src_ready = sem("src_ready")
        mask_landed = sem("mask_landed")
        keep_ready = sem("keep_ready")
        gone_ready = sem("gone_ready")
        add_mask_ready = sem("add_mask_ready")
        weights_ready = sem("weights_ready")
        xin_ready = sem("xin_ready")
        xb_ready = sem("xb_ready")
        scaled_ready = sem("scaled_ready")
        mx_ready = sem("mx_ready")
        nb_ready = sem("nb_ready")
        exp_ready = sem("exp_ready")
        rs_ready = sem("rs_ready")
        y_ready = sem("y_ready")

        steps = [("xin",), ("xt",), ("q",), ("k",), ("v",)]
        for t in range(TB):
            steps.append(("s", t))
            if t >= 1:
                steps.append(("pt", t - 1))
            if t >= 1:
                steps.append(("pv", t - 1))
        steps += [("pt", TB - 1), ("pv", TB - 1), ("ln",)]
        banks = {"xt": (0, 1), "q": (2, 3), "k": (0, 1), "v": (2, 3)}
        for step in steps:
            kind = step[0]
            if kind in banks:
                for i in range(2):
                    ps.fill(step + (i,), banks[kind][i])
            elif kind == "s":
                ps.fill(step, 4 + step[1] % 2)
            elif kind == "pt":
                ps.fill(step, 0 + step[1] % 2)
            elif kind == "pv":
                ps.fill(step, 6 + step[1] % 2)

        ps.finish(shared, NB)

        block = ctx.enter_context(nc.Block())

        @block.sync
        def _(sp):
            if not cross:
                return
            with sp.Fori(0, NB) as it:
                key = ("s", 2)
                sp.wait_ge(ps.sem_filled(key), ps.last_time(key, it))
                sp.dma_start(srcT[:], w["ctxT"][it].rearrange("(c p) s -> p c s", p=P)).then_inc(src_ready, 16)
                sp.dma_start(mask_int[:], w["mask"][it].partition_broadcast(P)).then_inc(mask_landed, 16)

        @block.tensor
        def _(pe):
            def empty(key, it):
                pe.wait_ge(ps.sem_drained(key), ps.before(key, it))

            def drained(key, it):
                pe.wait_ge(ps.sem_drained(key), ps.count(key, it))

            pe.wait_ge(w["landed"], w["loads"])
            if rope is not None:
                pe.wait_ge(weights_ready, 1)
            with pe.Fori(0, NB) as it:
                for step in steps:
                    kind = step[0]
                    if kind == "xt":
                        pe.wait_ge(xin_ready, it + 1)
                        for c in range(KC):
                            key = step + (c,)
                            empty(key, it)
                            for t in range(TB):
                                mm = nc.tensor.transpose(ps.ap(key)[:, t * P:(t + 1) * P],
                                                         xin[:, t, c * P:(c + 1) * P], ident[:])
                            mm.then_inc(ps.sem_filled(key), 1)
                    elif kind in ("q", "k"):
                        if kind == "q":
                            for c in range(KC):
                                drained(("xt", c), it)
                        elif cross:
                            pe.wait_ge(src_ready, (it + 1) * 16)
                        for e in range(KC):
                            key = step + (e,)
                            empty(key, it)
                            for c in range(KC):
                                mm = nc.tensor.matmul(ps.ap(key), w["W" + kind][:, c, e * P:(e + 1) * P],
                                                      (xT if kind == "q" else srcT)[:, c, :],
                                                      start=c == 0, stop=c == KC - 1)
                            mm.then_inc(ps.sem_filled(key), 1)
                    elif kind == "v":
                        for i in range(2):
                            key = step + (i,)
                            empty(key, it)
                            for n in range(2):
                                t = 2 * i + n
                                for c in range(KC):
                                    mm = nc.tensor.matmul(ps.ap(key)[:, n * D:(n + 1) * D],
                                                          srcT[:, c, t * P:(t + 1) * P], w["Wv"][:, c, :],
                                                          start=c == 0, stop=c == KC - 1)
                            mm.then_inc(ps.sem_filled(key), 1)
                    elif kind == "s":
                        t = step[1]
                        if t == 0:
                            for e in range(KC):
                                drained(("q", e), it)
                                drained(("k", e), it)
                        empty(step, it)
                        for e in range(KC):
                            mm = nc.tensor.matmul(ps.ap(step), qT[:, e, t * P:(t + 1) * P], kT[:, e, :],
                                                  start=e == 0, stop=e == KC - 1)
                        mm.then_inc(ps.sem_filled(step), 1)
                    elif kind == "pt":
                        t = step[1]
                        pe.wait_ge(exp_ready, it * TB + t + 1)
                        empty(step, it)
                        for n in range(TB):
                            mm = nc.tensor.transpose(ps.ap(step)[:, n * P:(n + 1) * P],
                                                     prob[:, t % 2, n * P:(n + 1) * P], ident[:])
                        mm.then_inc(ps.sem_filled(step), 1)
                    elif kind == "pv":
                        t = step[1]
                        if t == 0:
                            for i in range(2):
                                drained(("v", i), it)
                        drained(("pt", t), it)
                        empty(step, it)
                        for n in range(TB):
                            mm = nc.tensor.matmul(ps.ap(step)[:, 0:D], pT[:, t % 2, n * P:(n + 1) * P], v[:, n, :],
                                                  start=n == 0, stop=n == TB - 1)
                        mm.then_inc(ps.sem_filled(step), 1)

        @block.scalar
        def _(act):
            def filled(key, it):
                act.wait_ge(ps.sem_filled(key), ps.count(key, it))

            with act.Fori(0, NB) as it:
                for step in steps:
                    kind = step[0]
                    if kind == "xin":
                        key = ("pv", 0)
                        act.wait_ge(ps.sem_drained(key), ps.last_time(key, it))
                        nc.scalar.copy(xin[:], x_all[:, bass.ds(it * TB, TB), :]).then_inc(xin_ready, 1)
                    elif kind == "xt":
                        for c in range(KC):
                            filled(step + (c,), it)
                            nc.scalar.copy(xT[:, c, :], ps.ap(step + (c,))).then_inc(ps.sem_drained(step + (c,)), 1)
                    elif kind == "v":
                        for i in range(2):
                            filled(step + (i,), it)
                            nc.scalar.copy(v[:, 2 * i:2 * i + 2, :], ps.ap(step + (i,)).rearrange(
                                "p (t d) -> p t d", d=D)).then_inc(ps.sem_drained(step + (i,)), 1)
                    elif kind == "s":
                        t = step[1]
                        act.wait_ge(nb_ready, it * TB + t + 1)
                        if t >= 2:
                            filled(("pt", t - 2), it)
                        if cross:
                            nc.scalar.activation(prob[:, t % 2, :], prob[:, t % 2, :], ACT.Exp, bias=nb[:, t:t + 1],
                                                 accum_out=sums[:, t:t + 1]).then_inc(exp_ready, 1)
                        else:
                            nc.scalar.activation(prob[:, t % 2, :], ps.ap(step), ACT.Exp, bias=nb[:, t:t + 1],
                                                 scale=scale, accum_out=sums[:, t:t + 1]).then_inc(exp_ready, 1)
                            act.wait_ge(exp_ready, it * TB + t + 1)
                            act.sem_inc(ps.sem_drained(step), 1)
                    elif kind == "pt":
                        t = step[1]
                        if t >= 2:
                            filled(("pv", t - 2), it)
                        filled(step, it)
                        nc.scalar.copy(pT[:, t % 2, :], ps.ap(step)).then_inc(ps.sem_drained(step), 1)

        @block.vector
        def _(dve):
            def filled(key, it):
                dve.wait_ge(ps.sem_filled(key), ps.count(key, it))

            dve.wait_ge(w["landed"], w["loads"])
            if rope is not None:
                for name in ("Wq", "Wk"):
                    plain = w[name + "_plain"][:].rearrange("p c (e two) -> p c e two", two=2)
                    out = w[name][:].rearrange("p c (e two) -> p c e two", two=2)
                    nc.vector.tensor_tensor(out[:, :, :, 0], plain[:, :, :, 0], plain[:, :, :, 1], ALU.subtract)
                    nc.vector.tensor_tensor(out[:, :, :, 1], plain[:, :, :, 1], plain[:, :, :, 0], ALU.add)
                for name in ("bq", "bk"):
                    ins = nc.vector.tensor_tensor(w[name + "_swap"][:], w[name + "_swap"][:], w["pair_sign"][:], ALU.mult)
                ins.then_inc(weights_ready, 1)
                dve.wait_ge(weights_ready, 1)
                for name in ("bq", "bk"):
                    ins = nc.vector.tensor_tensor(w[name][:], w[name][:], w[name + "_swap"][:], ALU.add)
                ins.then_inc(weights_ready, 1)
                dve.wait_ge(weights_ready, 2)
            with dve.Fori(0, NB) as it:
                for step in steps:
                    kind = step[0]
                    if kind in ("q", "k"):
                        dst = qT if kind == "q" else kT
                        for e in range(KC):
                            key = step + (e,)
                            filled(key, it)
                            bias = w["b" + kind][:, e:e + 1]
                            if rope is not None:
                                ins = nc.vector.scalar_tensor_tensor(out=dst[:, e, :], in0=ps.ap(key), scalar=bias,
                                                                     in1=rope[:, e, :], op0=ALU.add, op1=ALU.mult)
                            else:
                                ins = nc.vector.tensor_scalar(dst[:, e, :], ps.ap(key), bias, None, ALU.add)
                            ins.then_inc(ps.sem_drained(key), 1)
                        if kind == "q" and cross:
                            dve.wait_ge(mask_landed, (it + 1) * 16)
                            nc.vector.tensor_scalar(keep[:], mask_int[:], 0.0, None,
                                                    ALU.not_equal).then_inc(keep_ready, 1)
                            dve.wait_ge(keep_ready, it + 1)
                            nc.vector.tensor_scalar(gone[:], keep[:], 1e10, -1e10, ALU.mult,
                                                    ALU.add).then_inc(gone_ready, 1)
                            dve.wait_ge(gone_ready, it + 1)
                            nc.vector.tensor_tensor(add_mask[:], w["causal"][:],
                                                    gone[:].unsqueeze(1).broadcast_to([P, TB, S]),
                                                    ALU.add).then_inc(add_mask_ready, 1)
                            dve.wait_ge(add_mask_ready, it + 1)
                    elif kind == "s":
                        t = step[1]
                        filled(step, it)
                        if cross:
                            if t >= 2:
                                filled(("pt", t - 2), it)
                            nc.vector.scalar_tensor_tensor(out=prob[:, t % 2, :], in0=ps.ap(step), scalar=scale,
                                                           in1=keep[:], op0=ALU.mult,
                                                           op1=ALU.mult).then_inc(ps.sem_drained(step), 1)
                            dve.wait_ge(ps.sem_drained(step), ps.count(step, it))
                            dve.sem_inc(norm.passed, 1)
                            nc.vector.tensor_tensor_reduce(prob[:, t % 2, :], prob[:, t % 2, :], add_mask[:, t, :], 1.0,
                                                           LOWEST, ALU.add, ALU.max,
                                                           mx[:, t:t + 1]).then_inc(mx_ready, 1)
                        else:
                            nc.vector.reduce_max(mx[:, t:t + 1], ps.ap(step), AX.X).then_inc(mx_ready, 1)
                        dve.wait_ge(mx_ready, it * TB + t + 1)
                        nc.vector.tensor_scalar(nb[:, t:t + 1], mx[:, t:t + 1], -1.0 if cross else -scale, None,
                                                ALU.mult).then_inc(nb_ready, 1)
                    elif kind == "pv":
                        t = step[1]
                        dve.wait_ge(exp_ready, it * TB + t + 1)
                        nc.vector.reciprocal(rs[:, t:t + 1], sums[:, t:t + 1]).then_inc(rs_ready, 1)
                        if t == 0:
                            dve.wait_ge(xb_ready, it + 1)
                        dve.wait_ge(rs_ready, it * TB + t + 1)
                        filled(step, it)
                        nc.vector.scalar_tensor_tensor(out=y[:, t, :], in0=ps.ap(step)[:, 0:D], scalar=rs[:, t:t + 1],
                                                       in1=xb[:, t, :], op0=ALU.mult, op1=ALU.add).then_inc(y_ready, 1)
                        dve.wait_ge(y_ready, it * TB + t + 1)
                        dve.sem_inc(ps.sem_drained(step), 1)
                    elif kind == "ln":
                        norm.vector(dve, it)

        @block.gpsimd
        def _(pool):
            pool.wait_ge(w["landed"], w["loads"])
            with pool.Fori(0, NB) as it:
                key = ("pv", TB - 1)
                pool.wait_ge(ps.sem_drained(key), ps.last_time(key, it))
                pool.wait_ge(xin_ready, it + 1)
                for c in range(KC):
                    key = ("xt", c)
                    pool.wait_ge(ps.sem_filled(key), ps.count(key, it))
                nc.gpsimd.tensor_tensor(xb[:], xin[:], w["bv"][:].unsqueeze(1).broadcast_to([P, TB, D]),
                                        ALU.add).then_inc(xb_ready, 1)
                norm.gpsimd(pool, it)


def stage_moe(nc, shared, w):
    ident, x_all = shared["ident"], shared["x"]
    D = x_all.shape[2]
    TB = 4
    NB = x_all.shape[1] // TB
    S = TB * P
    KC = D // P
    E = w["Wr"].shape[2]
    HID = w["W1"].shape[3]
    HC = HID // P
    TOP_K = 2

    with ExitStack() as ctx:
        def sb(name, shape):
            return ctx.enter_context(nc.sbuf_tensor(f"m_{name}", shape, F32))

        def sem(name):
            return shared["sems"].enter_context(nc.semaphore(f"m_{name}"))

        ps = Psum(shared)
        xin = sb("xin", [P, TB, D])
        xT = sb("xT", [P, KC, S])
        logits = sb("logits", [P, TB, E])
        above = sb("above", [P, TB, E, E])
        equal = sb("equal", [P, TB, E, E])
        rank = sb("rank", [P, TB, E])
        top = sb("top", [P, TB])
        gates = sb("gates", [P, TB, E])
        total = sb("total", [P, TB])
        gT = sb("gT", [E, S])
        hT = sb("hT", [P, 2, HC, S])
        acc = sb("acc", [P, TB, D])
        norm = Norm(nc, shared, ctx, "m", acc)
        xin_ready = sem("xin_ready")
        routed = sem("routed")
        centred_ready = sem("centred_ready")
        exp_ready = sem("exp_ready")
        gates_ready = sem("gates_ready")
        acc_ready = sem("acc_ready")
        CHAIN = 10

        steps = [("xin",), ("xt",), ("route",), ("h", 0, 0), ("h", 0, 1), ("h", 0, 2), ("gt",), ("h", 0, 3)]
        steps += [("b2", t) for t in range(TB)]
        for e in range(1, E + 1):
            for c in range(HC):
                if e < E:
                    steps.append(("h", e, c))
                steps.append(("o", e - 1, c))
        steps.append(("ln",))
        ring = {"h": 0, "o": 0}
        for step in steps:
            kind = step[0]
            if kind == "xt":
                ps.fill(step + (0,), 0)
                ps.fill(step + (1,), 1)
            elif kind == "route":
                ps.fill(step, 2)
            elif kind == "gt":
                ps.fill(step, 3)
            elif kind == "h":
                ps.fill(step, (4, 5, 0, 1)[ring["h"] % 4])
                ring["h"] += 1
            elif kind in ("o", "b2"):
                ps.fill(step, (6, 7, 2, 3)[ring["o"] % 4])
                ring["o"] += 1

        ps.finish(shared, NB)

        block = ctx.enter_context(nc.Block())

        @block.tensor
        def _(pe):
            def empty(key, it):
                pe.wait_ge(ps.sem_drained(key), ps.before(key, it))

            def drained(key, it):
                pe.wait_ge(ps.sem_drained(key), ps.count(key, it))

            pe.wait_ge(w["landed"], w["loads"])
            with pe.Fori(0, NB) as it:
                for step in steps:
                    kind = step[0]
                    if kind == "xt":
                        pe.wait_ge(xin_ready, it + 1)
                        for c in range(KC):
                            key = step + (c,)
                            empty(key, it)
                            for t in range(TB):
                                mm = nc.tensor.transpose(ps.ap(key)[:, t * P:(t + 1) * P],
                                                         xin[:, t, c * P:(c + 1) * P], ident[:])
                            mm.then_inc(ps.sem_filled(key), 1)
                    elif kind == "route":
                        for c in range(KC):
                            drained(("xt", c), it)
                        empty(step, it)
                        for t in range(TB):
                            for c in range(KC):
                                mm = nc.tensor.matmul(ps.ap(step)[:, t * E:(t + 1) * E],
                                                      xT[:, c, t * P:(t + 1) * P], w["Wr"][:, c, :],
                                                      start=c == 0, stop=c == KC - 1)
                        mm.then_inc(ps.sem_filled(step), 1)
                    elif kind == "gt":
                        pe.wait_ge(gates_ready, it + 1)
                        empty(step, it)
                        for t in range(TB):
                            mm = nc.tensor.transpose(ps.ap(step)[0:E, t * P:(t + 1) * P], gates[:, t, :], ident[:])
                        mm.then_inc(ps.sem_filled(step), 1)
                    elif kind == "b2":
                        t = step[1]
                        drained(("gt",), it)
                        empty(step, it)
                        nc.tensor.matmul(ps.ap(step)[:, 0:D], gT[:, t * P:(t + 1) * P], w["b2"][:], start=True,
                                         stop=True).then_inc(ps.sem_filled(step), 1)
                    elif kind == "h":
                        e, ch = step[1:]
                        empty(step, it)
                        for c in range(KC):
                            mm = nc.tensor.matmul(ps.ap(step), w["W1"][:, e, c, ch * P:(ch + 1) * P], xT[:, c, :],
                                                  start=c == 0, stop=c == KC - 1)
                        mm.then_inc(ps.sem_filled(step), 1)
                    elif kind == "o":
                        e, t = step[1:]
                        if t == 0:
                            for c in range(HC):
                                drained(("h", e, c), it)
                        empty(step, it)
                        for c in range(HC):
                            mm = nc.tensor.matmul(ps.ap(step)[:, 0:D], hT[:, e % 2, c, t * P:(t + 1) * P],
                                                  w["W2"][:, e, c, :], start=c == 0, stop=c == HC - 1)
                        mm.then_inc(ps.sem_filled(step), 1)

        @block.scalar
        def _(act):
            def filled(key, it):
                act.wait_ge(ps.sem_filled(key), ps.count(key, it))

            act.wait_ge(w["landed"], w["loads"])
            with act.Fori(0, NB) as it:
                for step in steps:
                    kind = step[0]
                    if kind == "xin":
                        key = ("b2", TB - 1)
                        act.wait_ge(ps.sem_drained(key), ps.last_time(key, it))
                        nc.scalar.copy(xin[:], x_all[:, bass.ds(it * TB, TB), :]).then_inc(xin_ready, 1)
                    elif kind == "xt":
                        for c in range(KC):
                            filled(step + (c,), it)
                            nc.scalar.copy(xT[:, c, :], ps.ap(step + (c,))).then_inc(ps.sem_drained(step + (c,)), 1)
                    elif kind == "h":
                        e, ch = step[1:]
                        if e >= 2:
                            filled(("o", e - 2, TB - 1), it)
                        filled(step, it)
                        nc.scalar.activation(hT[:, e % 2, ch, :], ps.ap(step), ACT.Relu,
                                             bias=w["b1"][:, e, ch:ch + 1]).then_inc(ps.sem_drained(step), 1)
                        if (e, ch) == (0, 0):
                            act.wait_ge(centred_ready, it + 1)
                            nc.scalar.activation(gates[:], gates[:], ACT.Exp).then_inc(exp_ready, 1)
                    elif kind == "gt":
                        filled(step, it)
                        nc.scalar.copy(gT[:], ps.ap(step)[0:E, :]).then_inc(ps.sem_drained(step), 1)

        @block.vector
        def _(dve):
            def filled(key, it):
                dve.wait_ge(ps.sem_filled(key), ps.count(key, it))

            dve.wait_ge(w["landed"], w["loads"])
            with dve.Fori(0, NB) as it:
                for step in steps:
                    kind = step[0]
                    if kind == "route":
                        done = [0]

                        def chained(ins):
                            done[0] += 1
                            ins.then_inc(routed, 1)
                            dve.wait_ge(routed, it * CHAIN + done[0])

                        filled(step, it)
                        nc.vector.tensor_tensor(logits[:], ps.ap(step)[:, 0:TB * E].rearrange(
                            "p (t e) -> p t e", e=E), w["br"][:].unsqueeze(1).broadcast_to([P, TB, E]),
                            ALU.add).then_inc(ps.sem_drained(step), 1)
                        dve.wait_ge(ps.sem_drained(step), ps.count(step, it))
                        mine = logits[:].unsqueeze(3).broadcast_to([P, TB, E, E])
                        other = logits[:].unsqueeze(2).broadcast_to([P, TB, E, E])
                        for t in range(TB):
                            nc.vector.tensor_tensor(above[:, t], other[:, t], mine[:, t], ALU.is_gt)
                            ins = nc.vector.tensor_tensor(equal[:, t], other[:, t], mine[:, t], ALU.is_equal)
                        chained(ins)
                        chained(nc.vector.tensor_tensor(equal[:], equal[:],
                                                        w["before"][:].unsqueeze(1).broadcast_to([P, TB, E, E]),
                                                        ALU.mult))
                        chained(nc.vector.tensor_tensor(above[:], above[:], equal[:], ALU.add))
                        nc.vector.tensor_reduce(rank[:], above[:], AX.X, ALU.add)
                        chained(nc.vector.tensor_reduce(top[:], logits[:], AX.X, ALU.max))
                        nc.vector.tensor_tensor(gates[:], logits[:], top[:].unsqueeze(2).broadcast_to([P, TB, E]),
                                                ALU.subtract).then_inc(centred_ready, 1)
                        chained(nc.vector.tensor_scalar(rank[:], rank[:], TOP_K - 0.5, None, ALU.is_lt))
                        dve.wait_ge(exp_ready, it + 1)
                        chained(nc.vector.tensor_tensor(gates[:], gates[:], rank[:], ALU.mult))
                        chained(nc.vector.tensor_reduce(total[:], gates[:], AX.X, ALU.add))
                        chained(nc.vector.reciprocal(total[:], total[:]))
                        chained(nc.vector.tensor_tensor(gates[:], gates[:],
                                                        total[:].unsqueeze(2).broadcast_to([P, TB, E]), ALU.mult))
                        dve.sem_inc(gates_ready, 1)
                        done[0] += 1
                        dve.sem_inc(routed, 1)
                        assert done[0] == CHAIN, done
                    elif kind == "b2":
                        t = step[1]
                        filled(step, it)
                        nc.vector.tensor_tensor(acc[:, t, :], ps.ap(step)[:, 0:D], xin[:, t, :],
                                                ALU.add).then_inc(acc_ready, 1)
                        dve.wait_ge(acc_ready, it * TB + t + 1)
                        dve.sem_inc(ps.sem_drained(step), 1)
                    elif kind == "o":
                        e, t = step[1:]
                        before = ("o", e - 1, t) if e else ("b2", t)
                        dve.wait_ge(ps.sem_drained(before), ps.count(before, it))
                        filled(step, it)
                        nc.vector.scalar_tensor_tensor(out=acc[:, t, :], in0=ps.ap(step)[:, 0:D],
                                                       scalar=gates[:, t, e:e + 1], in1=acc[:, t, :], op0=ALU.mult,
                                                       op1=ALU.add).then_inc(ps.sem_drained(step), 1)
                    elif kind == "ln":
                        for t in range(TB):
                            key = ("o", E - 1, t)
                            dve.wait_ge(ps.sem_drained(key), ps.count(key, it))
                        norm.vector(dve, it)

        @block.gpsimd
        def _(pool):
            with pool.Fori(0, NB) as it:
                norm.gpsimd(pool, it)


def stage_head_attention(nc, shared, stage, w, cross):
    ident, x_all = shared["ident"], shared["x"]
    D = x_all.shape[2]
    TB = 4
    NB = x_all.shape[1] // TB
    S = TB * P
    KC = D // P
    H, DH, ROWS = 16, 16, 32
    HPC = P // ROWS
    QC = H // HPC
    scale = float(DH) ** -0.5

    with ExitStack() as ctx:
        def sb(name, shape, dt=F32):
            return ctx.enter_context(nc.sbuf_tensor(f"{stage}_{name}", shape, dt))

        def sem(name):
            return shared["sems"].enter_context(nc.semaphore(f"{stage}_{name}"))

        ps = Psum(shared)
        xin = sb("xin", [P, TB, D])
        xT = sb("xT", [P, KC, S])
        qT = sb("qT", [P, QC, S])
        kT = sb("kT", [P, QC, S])
        v = sb("v", [P, TB, D])
        prob = sb("prob", [P, 4, S])
        pT = sb("pT", [P, 3, S])
        mx = sb("mx", [P, 2, H])
        nb = sb("nb", [P, 2, H])
        sums = sb("sums", [P, 2, H])
        rs = sb("rs", [P, 2, H])
        o_tok = sb("o_tok", [P, D])
        oT = sb("oT", [P, KC, P])
        y = sb("y", [P, TB, D])
        norm = Norm(nc, shared, ctx, stage, y)
        srcT = sb("srcT", [P, KC, S]) if cross else xT
        mask_int = sb("mask_int", [P, TB, S], mybir.dt.int32) if cross else None
        add_mask = sb("add_mask", [P, TB, S]) if cross else w["causal"]
        src_ready = sem("src_ready")
        mask_landed = sem("mask_landed")
        masked = sem("masked")
        mask_ready = sem("mask_ready")
        xin_ready = sem("xin_ready")
        mx_ready = sem("mx_ready")
        nb_ready = sem("nb_ready")
        exp_ready = sem("exp_ready")
        rs_ready = sem("rs_ready")
        y_ready = sem("y_ready")

        LAG = 1
        units = [(t, h) for t in range(TB) for h in range(H)]
        N = len(units)
        steps = [("xin",), ("xt",), ("q",), ("k",), ("v",)]
        for n in range(N + 3):
            if n < N:
                steps.append(("s", n))
            if 2 <= n < N + 2:
                steps.append(("pt", n - 2))
            if 3 <= n:
                steps.append(("pv", n - 3))
                if (n - 3) % H == H - 1:
                    steps.append(("ot", (n - 3) // H))
                if (n - 3) % H == 2 and n > H:
                    steps.append(("wo", (n - 3) // H - 1))
        steps += [("wo", TB - 1), ("ln",)]
        for step in steps:
            kind = step[0]
            if kind in ("xt", "v"):
                for i in range(2):
                    ps.fill(step + (i,), i)
            elif kind in ("q", "k"):
                for i in range(QC):
                    ps.fill(step + (i,), 2 + i)
            elif kind == "s":
                ps.fill(step, (4, 5, 0)[step[1] % 3])
            elif kind == "pt":
                ps.fill(step, 2 + step[1] % 2)
            elif kind == "pv" and step[1] % H == 0:
                ps.fill(("o", step[1] // H), 6)
            elif kind == "ot":
                ps.fill(step, 1)
            elif kind == "wo":
                ps.fill(step, 7)

        def keys(t):
            return S if cross else (t + 1) * P

        ps.finish(shared, NB)

        block = ctx.enter_context(nc.Block())

        @block.sync
        def _(sp):
            if not cross:
                return
            with sp.Fori(0, NB) as it:
                key = ("s", H)
                sp.wait_ge(ps.sem_filled(key), ps.last_time(key, it))
                sp.dma_start(srcT[:], w["ctxT"][it].rearrange("(c p) s -> p c s", p=P)).then_inc(src_ready, 16)
                sp.dma_start(mask_int[:], w["mask"][it].rearrange("(t p) s -> p t s", p=P)).then_inc(mask_landed, 16)

        @block.tensor
        def _(pe):
            def empty(key, it):
                pe.wait_ge(ps.sem_drained(key), ps.before(key, it))

            def drained(key, it):
                pe.wait_ge(ps.sem_drained(key), ps.count(key, it))

            pe.wait_ge(w["landed"], w["loads"])
            with pe.Fori(0, NB) as it:
                for step in steps:
                    kind = step[0]
                    if kind == "xt":
                        pe.wait_ge(xin_ready, it + 1)
                        for c in range(KC):
                            key = step + (c,)
                            empty(key, it)
                            for t in range(TB):
                                mm = nc.tensor.transpose(ps.ap(key)[:, t * P:(t + 1) * P],
                                                         xin[:, t, c * P:(c + 1) * P], ident[:])
                            mm.then_inc(ps.sem_filled(key), 1)
                    elif kind in ("q", "k"):
                        if kind == "q":
                            for c in range(KC):
                                drained(("xt", c), it)
                        elif cross:
                            pe.wait_ge(src_ready, (it + 1) * 16)
                        for e in range(QC):
                            key = step + (e,)
                            empty(key, it)
                            for c in range(KC):
                                mm = nc.tensor.matmul(ps.ap(key), w["W" + kind][:, c, e * P:(e + 1) * P],
                                                      (xT if kind == "q" else srcT)[:, c, :],
                                                      start=c == 0, stop=c == KC - 1)
                            mm.then_inc(ps.sem_filled(key), 1)
                    elif kind == "v":
                        for i in range(2):
                            key = step + (i,)
                            empty(key, it)
                            for n in range(2):
                                t = 2 * i + n
                                for c in range(KC):
                                    mm = nc.tensor.matmul(ps.ap(key)[:, n * D:(n + 1) * D],
                                                          srcT[:, c, t * P:(t + 1) * P], w["Wv"][:, c, :],
                                                          start=c == 0, stop=c == KC - 1)
                            mm.then_inc(ps.sem_filled(key), 1)
                    elif kind == "s":
                        n = step[1]
                        t, h = units[n]
                        if t == 0 and h % HPC == 0:
                            drained(("q", h // HPC), it)
                            drained(("k", h // HPC), it)
                        empty(step, it)
                        rows = slice(h % HPC * ROWS, h % HPC * ROWS + DH)
                        nc.tensor.matmul(ps.ap(step)[:, 0:keys(t)], qT[rows, h // HPC, t * P:(t + 1) * P],
                                         kT[rows, h // HPC, 0:keys(t)], start=True,
                                         stop=True).then_inc(ps.sem_filled(step), 1)
                    elif kind == "pt":
                        n = step[1]
                        t, h = units[n]
                        pe.wait_ge(exp_ready, it * N + n + 1)
                        empty(step, it)
                        for k in range(keys(t) // P):
                            mm = nc.tensor.transpose(ps.ap(step)[:, k * P:(k + 1) * P],
                                                     prob[:, n % 4, k * P:(k + 1) * P], ident[:])
                        mm.then_inc(ps.sem_filled(step), 1)
                    elif kind == "pv":
                        n = step[1]
                        t, h = units[n]
                        if n == 0:
                            for i in range(2):
                                drained(("v", i), it)
                        drained(("pt", n), it)
                        okey = ("o", t)
                        if h == 0:
                            empty(okey, it)
                        for k in range(keys(t) // P):
                            mm = nc.tensor.matmul(ps.ap(okey)[:, h * DH:(h + 1) * DH],
                                                  pT[:, n % 3, k * P:(k + 1) * P], v[:, k, h * DH:(h + 1) * DH],
                                                  start=k == 0, stop=k == keys(t) // P - 1)
                        if h == H - 1:
                            mm.then_inc(ps.sem_filled(okey), 1)
                    elif kind == "ot":
                        t = step[1]
                        drained(("o", t), it)
                        empty(step, it)
                        for c in range(KC):
                            mm = nc.tensor.transpose(ps.ap(step)[:, c * P:(c + 1) * P], o_tok[:, c * P:(c + 1) * P],
                                                     ident[:])
                        mm.then_inc(ps.sem_filled(step), 1)
                    elif kind == "wo":
                        t = step[1]
                        drained(("ot", t), it)
                        empty(step, it)
                        for c in range(KC):
                            mm = nc.tensor.matmul(ps.ap(step)[:, 0:D], oT[:, c, :], w["Wo"][:, c, :],
                                                  start=c == 0, stop=c == KC - 1)
                        mm.then_inc(ps.sem_filled(step), 1)

        def copy_probs(eng, copy, n, it):
            t, h = units[n]
            if n >= 3:
                old = ("pt", n - 1)
                eng.wait_ge(ps.sem_filled(old), ps.count(old, it))
            key = ("pt", n)
            eng.wait_ge(ps.sem_filled(key), ps.count(key, it))
            copy(pT[:, n % 3, 0:keys(t)], ps.ap(key)[:, 0:keys(t)]).then_inc(ps.sem_drained(key), 1)

        def on_scalar(n):
            return n % 3 == 0

        @block.scalar
        def _(act):
            def filled(key, it):
                act.wait_ge(ps.sem_filled(key), ps.count(key, it))

            act.wait_ge(w["landed"], w["loads"])
            with act.Fori(0, NB) as it:
                for step in steps:
                    kind = step[0]
                    if kind == "xin":
                        key = ("wo", TB - 1)
                        act.wait_ge(ps.sem_drained(key), ps.last_time(key, it))
                        nc.scalar.copy(xin[:], x_all[:, bass.ds(it * TB, TB), :]).then_inc(xin_ready, 1)
                    elif kind == "xt":
                        for c in range(KC):
                            filled(step + (c,), it)
                            nc.scalar.copy(xT[:, c, :], ps.ap(step + (c,))).then_inc(ps.sem_drained(step + (c,)), 1)
                    elif kind == "k":
                        for e in range(QC):
                            key = step + (e,)
                            filled(key, it)
                            if cross:
                                ins = nc.scalar.activation(kT[:, e, :], ps.ap(key), ACT.Identity,
                                                           bias=w["bk"][:, e:e + 1])
                            else:
                                ins = nc.scalar.copy(kT[:, e, :], ps.ap(key))
                            ins.then_inc(ps.sem_drained(key), 1)
                    elif kind == "s":
                        n = step[1]
                        t, h = units[n]
                        act.wait_ge(nb_ready, it * N + n + 1)
                        pr = prob[:, n % 4, 0:keys(t)]
                        nc.scalar.activation(pr, pr, ACT.Exp, bias=nb[:, t % 2, h:h + 1], scale=scale,
                                             accum_out=sums[:, t % 2, h:h + 1]).then_inc(exp_ready, 1)
                    elif kind == "pt" and on_scalar(step[1]):
                        copy_probs(act, nc.scalar.copy, step[1], it)
                    elif kind == "ot":
                        t = step[1]
                        if t:
                            filled(("wo", t - 1), it)
                        filled(step, it)
                        nc.scalar.copy(oT[:], ps.ap(step)[:, 0:D].rearrange("p (c q) -> p c q", q=P)
                                       ).then_inc(ps.sem_drained(step), 1)

        @block.vector
        def _(dve):
            def filled(key, it):
                dve.wait_ge(ps.sem_filled(key), ps.count(key, it))

            dve.wait_ge(w["landed"], w["loads"])
            with dve.Fori(0, NB) as it:
                for step in steps:
                    kind = step[0]
                    if kind == "q":
                        for e in range(QC):
                            key = step + (e,)
                            filled(key, it)
                            if cross:
                                ins = nc.vector.tensor_scalar(qT[:, e, :], ps.ap(key), w["bq"][:, e:e + 1], None,
                                                              ALU.add)
                            else:
                                ins = nc.vector.tensor_copy(qT[:, e, :], ps.ap(key))
                            ins.then_inc(ps.sem_drained(key), 1)
                    elif kind == "v":
                        for i in range(2):
                            key = step + (i,)
                            filled(key, it)
                            out = v[:, 2 * i:2 * i + 2, :]
                            src = ps.ap(key).rearrange("p (t d) -> p t d", d=D)
                            if cross:
                                ins = nc.vector.tensor_tensor(out, src, w["bv"][:].unsqueeze(1).broadcast_to(
                                    [P, 2, D]), ALU.add)
                            else:
                                ins = nc.vector.tensor_copy(out, src)
                            ins.then_inc(ps.sem_drained(key), 1)
                        if cross:
                            dve.wait_ge(mask_landed, (it + 1) * 16)
                            nc.vector.tensor_scalar(add_mask[:], mask_int[:], 0.0, MASKED, ALU.is_equal,
                                                    ALU.mult).then_inc(mask_ready, 1)
                            dve.wait_ge(mask_ready, it + 1)
                    elif kind == "s":
                        n = step[1]
                        t, h = units[n]
                        if n >= 4:
                            filled(("pt", n - 4), it)
                        filled(step, it)
                        dve.sem_inc(norm.passed, 1)
                        nc.vector.tensor_tensor_reduce(prob[:, n % 4, 0:keys(t)], ps.ap(step)[:, 0:keys(t)],
                                                       add_mask[:, t, 0:keys(t)], 1.0, LOWEST, ALU.add, ALU.max,
                                                       mx[:, t % 2, h:h + 1]).then_inc(ps.sem_drained(step), 1)
                        dve.wait_ge(ps.sem_drained(step), ps.count(step, it))
                        nc.vector.tensor_scalar(nb[:, t % 2, h:h + 1], mx[:, t % 2, h:h + 1], -scale, None,
                                                ALU.mult).then_inc(nb_ready, 1)
                    elif kind == "pt" and not on_scalar(step[1]):
                        copy_probs(dve, nc.vector.tensor_copy, step[1], it)
                    elif kind == "pv" and step[1] % H == H - 1:
                        t = step[1] // H
                        dve.wait_ge(exp_ready, it * N + step[1] + 1)
                        nc.vector.reciprocal(rs[:, t % 2, :], sums[:, t % 2, :]).then_inc(rs_ready, 1)
                        dve.wait_ge(rs_ready, it * TB + t + 1)
                        if t:
                            filled(("ot", t - 1), it)
                        filled(("o", t), it)
                        nc.vector.tensor_tensor(
                            o_tok[:].rearrange("p (h d) -> p h d", d=DH),
                            ps.ap(("o", t))[:, 0:D].rearrange("p (h d) -> p h d", d=DH),
                            rs[:, t % 2, :].unsqueeze(2).broadcast_to([P, H, DH]), ALU.mult
                        ).then_inc(ps.sem_drained(("o", t)), 1)
                    elif kind == "wo":
                        t = step[1]
                        filled(step, it)
                        nc.vector.tensor_tensor(y[:, t, :], ps.ap(step)[:, 0:D], xin[:, t, :],
                                                ALU.add).then_inc(ps.sem_drained(step), 1)
                        dve.wait_ge(ps.sem_drained(step), ps.count(step, it))
                        dve.sem_inc(y_ready, 1)
                    elif kind == "ln":
                        if cross:
                            for t in range(TB):
                                ins = nc.vector.tensor_tensor(y[:, t, :], y[:, t, :], w["bo"][:], ALU.add)
                            ins.then_inc(masked, 1)
                            dve.wait_ge(masked, it + 1)
                        norm.vector(dve, it)

        @block.gpsimd
        def _(pool):
            with pool.Fori(0, NB) as it:
                norm.gpsimd(pool, it)


def mk_decoder(nc, ins, out):
    B, S, D = ins["x"].shape
    TILES = B * S // P
    scratch = nc.dram_tensor("x_before_mlp", [P, TILES, D], F32, kind="Internal").ap()
    with ExitStack() as ctx:
        def sb(c, name, shape, dt=F32):
            return c.enter_context(nc.sbuf_tensor(name, shape, dt))

        psum = ctx.enter_context(nc.psum_tensor("psum", [P, PSUM_BANKS, BANK], F32))
        ident = sb(ctx, "ident", [P, P])
        half_pow = sb(ctx, "half_pow", [P, 32])
        x_all = sb(ctx, "x_all", [P, TILES, D])
        shared = {"psum": psum, "ident": ident, "x": x_all, "half_pow": half_pow}
        landed = {n: ctx.enter_context(nc.semaphore("landed_" + n)) for n in ("x", "a0", "x0", "moe", "a1", "x1")}
        shared["sems"] = ctx
        for n in ("filled", "drained"):
            shared[n] = [ctx.enter_context(nc.semaphore(f"bank{b}_{n}")) for b in range(PSUM_BANKS)]
        shared["contents"] = [8] * PSUM_BANKS
        made = ctx.enter_context(nc.semaphore("made"))
        saved = ctx.enter_context(nc.semaphore("saved"))

        with ExitStack() as early:
            loads = []

            def weight(stage, name, shape, src):
                t = sb(early, f"w_{stage}_{name}", shape)
                loads.append((stage, t[:], src))
                return t

            def chunks(ap):
                return ap.rearrange("(c p) n -> p c n", p=P)

            a0, x0, moe, a1, x1 = {}, {}, {}, {}, {}
            KC = D // P
            for n in ("Wq", "Wk"):
                a0[n + "_plain"] = weight("a0", n, [P, KC, D], chunks(ins["L0_attn_" + n]))
                a0[n] = sb(early, "w_a0_turned_" + n, [P, KC, D])
            a0["Wv"] = weight("a0", "Wv", [P, KC, D], chunks(ins["L0_attn_Wv"]))
            for n in ("bq", "bk", "bq_swap", "bk_swap"):
                a0[n] = weight("a0", n, [P, KC], ins["L0_attn_" + n])
            a0["pair_sign"] = weight("a0", "pair_sign", [P, KC], ins["pair_sign"])
            a0["bv"] = weight("a0", "bv", [P, D], ins["L0_attn_bv"].partition_broadcast(P))
            rope = weight("a0", "rope", [P, KC, S], ins["rope_pairs"])
            for n in ("Wq", "Wk", "Wv"):
                x0[n] = weight("x0", n, [P, KC, D], chunks(ins["L0_xattn_" + n]))
            for n in ("bq", "bk"):
                x0[n] = weight("x0", n, [P, KC], ins["L0_xattn_" + n])
            x0["bv"] = weight("x0", "bv", [P, D], ins["L0_xattn_bv"].partition_broadcast(P))
            x0["causal"] = weight("x0", "causal", [P, S // P, S], ins["causal"])
            x0["ctxT"] = ins["ctxT"]
            x0["mask"] = ins["mask_Bx1xS2_ik0"].rearrange("b a s -> b (a s)")
            E, _, HID = ins["L0_ffn_W1"].shape
            moe["Wr"] = weight("moe", "Wr", [P, KC, E], chunks(ins["L0_ffn_Wr"]))
            moe["br"] = weight("moe", "br", [P, E], ins["L0_ffn_br"].partition_broadcast(P))
            moe["before"] = weight("moe", "before", [P, E, E], ins["before"].rearrange(
                "e f -> (e f)").partition_broadcast(P).rearrange("p (e f) -> p e f", e=E))
            moe["b1"] = weight("moe", "b1", [P, E, HID // P], ins["L0_ffn_b1"])
            moe["b2"] = weight("moe", "b2", [E, D], ins["L0_ffn_b2"])
            moe["W1"] = weight("moe", "W1", [P, E, KC, HID], ins["L0_ffn_W1"].rearrange("e (c p) n -> p e c n", p=P))
            moe["W2"] = weight("moe", "W2", [P, E, HID // P, D],
                               ins["L0_ffn_W2"].rearrange("e (c p) n -> p e c n", p=P))
            for st, d, pre in (("a1", a1, "L1_attn_"), ("x1", x1, "L1_xattn_")):
                for n in ("Wq", "Wk"):
                    d[n] = weight(st, n, [P, KC, 2 * D], chunks(ins[pre + n]))
                for n in ("Wv", "Wo"):
                    d[n] = weight(st, n, [P, KC, D], chunks(ins[pre + n]))
            a1["causal"] = x0["causal"]
            for n in ("bq", "bk"):
                x1[n] = weight("x1", n, [P, 4], ins["L1_xattn_" + n])
            for n in ("bv", "bo"):
                x1[n] = weight("x1", n, [P, D], ins["L1_xattn_" + n].partition_broadcast(P))
            x1["ctxT"], x1["mask"] = ins["ctxT"], ins["mask_BxSxS2_ik0"]
            for st, d in (("a0", a0), ("x0", x0), ("moe", moe), ("a1", a1), ("x1", x1)):
                d["landed"], d["loads"] = landed[st], 16 * sum(1 for s, _, _ in loads if s == st)

            with nc.Block() as block:
                @block.sync
                def _(sp):
                    sp.dma_start(ident[:], ins["ident"]).then_inc(landed["x"], 16)
                    sp.dma_start(x_all[:], ins["x"].rearrange("b (t p) d -> p (b t) d", p=P)
                                 ).then_inc(landed["x"], 16)
                    for st, dst, src in loads:
                        sp.dma_start(dst, src).then_inc(landed[st], 16)
                    sp.wait_ge(landed["x"], 32)

                @block.vector
                def _(dve):
                    for bank in range(PSUM_BANKS):
                        dve.sem_inc(shared["filled"][bank], 8)
                        dve.sem_inc(shared["drained"][bank], 8)
                    nc.vector.memset(half_pow[:], -0.5).then_inc(made, 1)
                    dve.wait_ge(made, 1)

            stage_wide_attention(nc, shared, "a0", a0, rope, cross=False)
            stage_wide_attention(nc, shared, "x0", x0, None, cross=True)
            stage_moe(nc, shared, moe)
            stage_head_attention(nc, shared, "a1", a1, cross=False)
            stage_head_attention(nc, shared, "x1", x1, cross=True)

        with nc.Block() as block:
            @block.sync
            def _(sp):
                sp.dma_start(scratch, x_all[:]).then_inc(saved, 16)
                sp.wait_ge(saved, 16)
        stage_l1_ffn(nc, shared, ins, ins)
        stage_final(nc, shared, scratch, out)


def stage_final(nc, shared, scratch, out):
    x_all = shared["x"]
    _, TILES, D = x_all.shape
    TB = 4
    NB = TILES // TB
    with ExitStack() as ctx:
        x_old = ctx.enter_context(nc.sbuf_tensor("x_old", [P, TILES, D], F32))
        y = ctx.enter_context(nc.sbuf_tensor("z_y", [P, TILES, D], F32))
        norm = Norm(nc, shared, ctx, "z", y)
        old_landed = ctx.enter_context(nc.semaphore("z_old_landed"))
        summed = ctx.enter_context(nc.semaphore("z_summed"))
        stored = ctx.enter_context(nc.semaphore("z_stored"))
        out_v = out.rearrange("b (t p) d -> p (b t) d", p=P)
        with nc.Block() as block:
            @block.sync
            def _(sp):
                sp.dma_start(x_old[:], scratch).then_inc(old_landed, 16)
                sp.wait_ge(norm.x_ready, 1)
                sp.dma_start(out_v, x_all[:]).then_inc(stored, 16)
                sp.wait_ge(stored, 16)

            @block.vector
            def _(dve):
                dve.wait_ge(old_landed, 16)
                nc.vector.tensor_tensor(y[:], x_old[:], x_all[:], ALU.add).then_inc(summed, 1)
                dve.wait_ge(summed, 1)
                norm.vector(dve, 0)

            @block.gpsimd
            def _(pool):
                norm.gpsimd(pool, 0)


def tables():
    import numpy as np

    f32 = np.float32
    S, D, E, DH = 512, 256, 8, 64
    t = {"ident": np.eye(P, dtype=f32)}
    pos = np.arange(S, dtype=f32)
    inv = (f32(10000.0) ** (np.arange(0, 128, 2, dtype=f32) / f32(128))).astype(f32)
    rad = (pos[:, None] / inv).astype(f32)
    sincos = np.repeat(np.stack((np.sin(rad), np.cos(rad)), axis=-1).reshape(S, -1), 2, axis=-1)
    t["rope_pairs"] = sincos.T.reshape(D // P, P, S).transpose(1, 0, 2)
    t["pair_sign"] = np.where(np.arange(P) % 2 == 0, -1, 1)[:, None] * np.ones((1, D // P))
    q, k = np.arange(S)[:, None], np.arange(S)[None]
    tiled = lambda a: a.reshape(S // P, P, S).transpose(1, 0, 2)
    t["causal"] = tiled(np.where(k > q, -1e10, 0.0))
    t["before"] = np.where(np.arange(E)[None] < np.arange(E)[:, None], 1.0, 0.0)
    half = np.arange(0, DH, 2, dtype=f32)
    freq = (f32(1.0) / f32(10000.0) ** (half / f32(DH))).astype(f32)
    ang = np.concatenate([pos[:, None] * freq[None]] * 2, -1).astype(f32)
    base = ((half + f32(0.4 * DH)) / f32(1.4 * DH)).astype(f32)
    power = ((pos - S // 2) / 32).astype(f32)
    sc = (base[None] ** power[:, None]).astype(f32)
    sc = np.concatenate([sc, sc], -1)
    sign = np.where(np.arange(DH) < DH // 2, -1, 1).astype(f32)
    cos, sin = np.cos(ang), np.sin(ang) * sign
    inv_sc = (f32(1.0) / sc).astype(f32)
    t["rope"] = np.stack([cos * sc, sin * sc, cos * inv_sc, sin * inv_sc], 1).reshape(S // P, P, 4, DH).transpose(
        1, 0, 2, 3)
    p, j = np.arange(P)[:, None], np.arange(2 * P)[None]
    near = (P + p - j >= 0) & (P + p - j <= 64)
    t["band"] = np.stack([np.where(near & (j >= P), 0.0, -1e30), np.where(near, 0.0, -1e30)], 1)
    return {n: np.ascontiguousarray(a, dtype=f32) for n, a in t.items()}


def lay_out(inputs):
    import numpy as np

    a = {n: np.asarray(v) for n, v in inputs.items()}
    D = a["x"].shape[-1]
    g = {n: a[n] for n in ("x", "mask_Bx1xS2_ik0", "mask_BxSxS2_ik0")}
    g["ctxT"] = a["ctx_1024"].transpose(0, 2, 1)

    def columns(v, chunks):
        out = np.zeros(v.shape[:-1] + (chunks * P,), v.dtype)
        out[..., :v.shape[-1]] = v
        return out.reshape(v.shape[:-1] + (chunks, P)).swapaxes(-1, -2)

    def spaced(v):
        out = np.zeros(v.shape[:-1] + (D // 16, 32), v.dtype)
        out[..., :16] = v.reshape(v.shape[:-1] + (D // 16, 16))
        return out.reshape(v.shape[:-1] + (2 * D,))

    for n in ("Wq", "Wk", "Wv"):
        g["L0_attn_" + n] = a["L0_attn_" + n].T
        g["L0_xattn_" + n] = a["L0_xattn_" + n].T
    for n in ("bq", "bk"):
        g["L0_attn_" + n] = columns(a["L0_attn_" + n], D // P)
        g["L0_attn_" + n + "_swap"] = columns(a["L0_attn_" + n].reshape(-1, 2)[:, ::-1].reshape(-1), D // P)
        g["L0_xattn_" + n] = columns(a["L0_xattn_" + n], D // P)
    for n in ("L0_attn_bv", "L0_xattn_bv", "L0_ffn_Wr", "L0_ffn_br", "L0_ffn_W1", "L0_ffn_W2", "L0_ffn_b2",
              "L1_xattn_bv", "L1_xattn_bo"):
        g[n] = a[n]
    g["L0_ffn_b1"] = columns(a["L0_ffn_b1"], a["L0_ffn_b1"].shape[1] // P).transpose(1, 0, 2)
    for pre in ("L1_attn_", "L1_xattn_"):
        for n in ("Wq", "Wk"):
            g[pre + n] = spaced(a[pre + n].T)
        for n in ("Wv", "Wo"):
            g[pre + n] = a[pre + n].T
    for n in ("bq", "bk"):
        g["L1_xattn_" + n] = columns(spaced(a["L1_xattn_" + n]), 2 * D // P)
    for n in ("Wqkv", "Wo", "W1", "W2", "b2"):
        g[n] = a["L1_ffn_" + n]
    for n in ("q", "k"):
        s = a[f"L1_ffn_{n}_scale"]
        g[n + "_scale"] = s
        g[n + "_swap"] = np.concatenate([s[:, s.shape[1] // 2:], s[:, :s.shape[1] // 2]], 1)
    for n in ("ln_g", "ln_b"):
        g[n] = columns(a["L1_ffn_" + n], D // P)
    hid = a["L1_ffn_W2"].shape[1]
    g["b1a"] = columns(a["L1_ffn_b1"][:, :hid], -(-hid // P))
    g["b1g"] = columns(a["L1_ffn_b1"][:, hid:], -(-hid // P))
    return {n: np.ascontiguousarray(v) for n, v in g.items()}


def kernel(**inputs):
    import concourse.bacc as _bacc
    from concourse import mybir as _mybir
    from concourse.bass_utils import run_bass_kernel_spmd as _run

    nc = _bacc.Bacc("TRN2", target_bir_lowering=False, num_devices=1)
    laid = lay_out(inputs)
    laid.update(tables())
    arrays = {f"in_{n}": v for n, v in laid.items()}
    ins = {n: nc.dram_tensor(f"in_{n}", v.shape, _mybir.dt.from_np(v.dtype), kind="ExternalInput").ap()
           for n, v in laid.items()}
    out = nc.dram_tensor("out", laid["x"].shape, F32, kind="ExternalOutput").ap()
    mk_decoder(nc, ins, out)
    r = _run(nc, [arrays], core_ids=[0])
    return r.results[0]["out"]
```

```python
from contextlib import ExitStack, contextmanager

import concourse.bass as bass
from concourse import mybir

P = 128
F32 = mybir.dt.float32
ALU = mybir.AluOpType
ACT = mybir.ActivationFunctionType
AX = mybir.AxisListType
PSUM_BANKS = 8
BANK = 512
LOWEST = -3.0e38
LN_EPS = 1e-5
MASKED = -1.0e30


class Psum:

    def __init__(self, shared, first=0):
        self.first = first
        self.tensor, self.filled, self.drained = shared["psum"], shared["filled"], shared["drained"]
        self.earlier = shared["contents"]
        self.bank, self.number, self.per = {}, {}, [0] * PSUM_BANKS

    def fill(self, key, bank):
        assert key not in self.bank, key
        self.bank[key], self.number[key] = bank, self.per[bank] + 1
        self.per[bank] += 1

    def finish(self, shared, iterations):
        shared["contents"] = [n + iterations * m for n, m in zip(self.earlier, self.per)]

    def ap(self, key):
        return self.tensor[:, self.bank[key], :]

    def sem_filled(self, key):
        return self.filled[self.bank[key]]

    def sem_drained(self, key):
        return self.drained[self.bank[key]]

    def start(self, key, it):
        b = self.bank[key]
        return it * self.per[b] + (self.earlier[b] - self.first * self.per[b])

    def before(self, key, it):
        return self.start(key, it) + (self.number[key] - 1)

    def last_time(self, key, it):
        assert self.earlier[self.bank[key]] + self.number[key] > self.per[self.bank[key]]
        return self.start(key, it) + (self.number[key] - self.per[self.bank[key]])

    def count(self, key, it):
        return self.start(key, it) + self.number[key]


def stage_l1_ffn(nc, shared, w, tabs):
    ident, x_all = shared["ident"], shared["x"]
    L, D, QKV = w["Wqkv"].shape
    INNER = QKV // 3
    HID = w["W2"].shape[1]
    H, DH = 16, 64
    WINDOW = 64
    TB = 4
    NB = x_all.shape[1] // TB
    KC = D // P
    OC = INNER // P
    HC = -(-HID // P)
    HREM = HID - (HC - 1) * P
    HALF = INNER // 2
    G = H // 4
    QK_SCALE = 8.0

    with ExitStack() as ctx:
        def sb(name, shape):
            return ctx.enter_context(nc.sbuf_tensor("f_" + name, shape, F32))

        def sem(name):
            return shared["sems"].enter_context(nc.semaphore("f_" + name))

        wqkv = sb("wqkv", [P, KC, QKV])
        wo = sb("wo", [P, OC, D])
        w1 = sb("w1", [P, KC, 2 * HID])
        w2 = sb("w2", [P, HC, D])
        ln_g = sb("ln_g", [P, KC])
        ln_b = sb("ln_b", [P, KC])
        b1a = sb("b1a", [P, HC])
        b1g = sb("b1g", [P, HC])
        b2 = sb("b2", [P, D])
        qks = sb("qks", [P, 4, DH])
        rope = sb("rope", [P, TB, 4, DH])
        tab = sb("tab", [P, TB, 4, DH])
        band = sb("band", [P, 2, 2 * P])
        xin = sb("xin", [P, TB, D])
        xsT = sb("xsT", [P, KC, TB * P + 1])
        raw = sb("raw", [P, 8, HALF])
        sq = sb("sq", [P, 2, HALF])
        rot = sb("rot", [P, 2, 2, HALF])
        ss = sb("ss", [P, 2, 4 * 8])
        rn = sb("rn", [P, 2, 4 * 8])
        half_pow = sb("half_pow", [P, 4 * 8])
        rq8 = sb("rq8", [P, TB, H])
        qT = sb("qT", [P, H // 2, P])
        kT = sb("kT", [P, H // 2, (TB + 1) * P])
        v = sb("v", [P, TB, INNER])
        prob = sb("prob", [P, 12, 2 * P])
        mx = sb("mx", [P, 2, H])
        nb = sb("nb", [P, 2, H])
        sums = sb("sums", [P, 2, H])
        rs = sb("rs", [P, 2, H])
        pT = sb("pT", [P, 4, BANK])
        oT = sb("oT", [P, OC, P])
        xs = sb("xs", [P, TB, P])
        xn = sb("xn", [P, TB, D])
        xnT = sb("xnT", [P, KC, TB * P])
        stat = sb("stat", [P, TB, 12])
        mv = sb("mv", [P, TB, 2])
        rstd = sb("rstd", [P, 2, TB])
        x1 = sb("x1", [P, TB, D])
        hT = sb("hT", [P, HC, TB * P])

        w_attn = sem("w_attn")
        w_wo = sem("w_wo")
        w_ffn = sem("w_ffn")
        consts = sem("consts")
        pads = sem("pads")
        passed = sem("passed")
        tab_ready = sem("tab_ready")
        xin_ready = sem("xin_ready")
        sq_ready = sem("sq_ready")
        rot_ready = sem("rot_ready")
        rope_done = sem("rope_done")
        ss_ready = sem("ss_ready")
        ssm_ready = sem("ssm_ready")
        rn_ready = sem("rn_ready")
        qk_ready = sem("qk_ready")
        nb_ready = sem("nb_ready")
        exp_ready = sem("exp_ready")
        pv_done = sem("pv_done")
        rs_ready = sem("rs_ready")
        prob_ready = sem("prob_ready")
        x1_ready = sem("x1_ready")
        attn_weights = sem("attn_weights")
        wo_weights = sem("wo_weights")
        ffn_weights = sem("ffn_weights")
        xs_ready = sem("xs_ready")
        stat_ready = sem("stat_ready")
        mv_ready = sem("mv_ready")
        eps_ready = sem("eps_ready")
        rstd_ready = sem("rstd_ready")
        xn_ready = sem("xn_ready")
        x1b_ready = sem("x1b_ready")
        x_ready = sem("x_ready")
        h_ready = sem("h_ready")

        N = G * TB
        MLP = ("xs", "ln", "xn", "xnt", "f1", "f2")

        def project(t, parts):
            return [("qkv", t, i) for i in parts]

        dense = {0: project(2, (0, 1)), 1: project(2, (2, 3)) + [("pow", 2)], 2: project(2, (4, 5)),
                 3: [("norm", 2), ("f1", 0), ("f1", 1)],
                 4: project(3, (0, 1)), 5: project(3, (2, 3)) + [("pow", 3)], 6: project(3, (4, 5)),
                 7: [("norm", 3), ("wo", 0)],
                 8: [("f1", 2), ("f1", 3), ("xin",)], 10: [("f1", 4), ("f1", 5)], 11: [("wo", 1)],
                 12: [("f2", 0)], 13: [("f2", 1)], 14: [("f2", 2)], 15: [("wo", 2), ("tab",)],
                 16: [("xt",)], 17: [("f2", 3)]}

        def iteration():
            yield from [("xs",), *project(0, range(6)), ("ln",), ("pow", 0), *project(1, (0, 1)), ("xn",)]
            yield from [("norm", 0), *project(1, range(2, 6)), ("pow", 1), ("tr", 0), ("xnt",)]
            for n in range(N + 3):
                t, g = divmod(n, G)
                if n < N:
                    yield ("s", t, g)
                if 1 <= n <= N:
                    yield ("r", *divmod(n - 1, G))
                if n == 1:
                    yield ("norm", 1)
                if g == G - 1 and t + 1 < TB:
                    yield ("tr", t + 1)
                if 2 <= n <= N + 1:
                    yield ("pt", *divmod(n - 2, G))
                yield from dense.get(n, ())
                if n < N:
                    yield ("e", t, g)
                if 3 <= n:
                    yield ("pv", *divmod(n - 3, G))
            yield ("wo", TB - 1)

        ITS = L * NB
        phases = []
        every = list(iteration())
        for steps, first, end in (([("tab",), ("xt",)], -1, 0),
                                  ([step for step in every if step[0] not in MLP], 0, 1), (every, 1, ITS),
                                  ([step for step in every if step[0] in MLP], ITS, ITS + 1)):
            ps = Psum(shared, first)
            ring = {"p": 0, "t": 0}
            for step in steps:
                kind = step[0]
                if kind in ("xt", "tr", "xnt", "pt"):
                    for i in range(4 if kind == "tr" else 2):
                        ps.fill(step + (i,), 2 + ring["t"] % 2)
                        ring["t"] += 1
                elif kind == "s":
                    for i in range(2):
                        ps.fill(step + (i,), 4 + i)
                elif kind == "pv" and step[2] % 2 == 0:
                    ps.fill(("o", step[1], step[2] // 2), 6 + step[2] // 2 % 2)
                elif kind in ("qkv", "wo", "f2", "f1"):
                    for key in ((step + (1,), step + (0,)) if kind == "f1" else (step,)):
                        ps.fill(key, ring["p"] % 2)
                        ring["p"] += 1
            ps.finish(shared, end - first)
            phases.append((steps, ps, first, end))

        @contextmanager
        def each(engine, first, end):
            if end - first == 1:
                yield first
            else:
                with engine.Fori(first, end) as it:
                    yield it

        def mlp_of(it):
            return it - 1

        def unseen(t):
            return P - WINDOW if t else P

        NQ = 4 * TB
        NG = G * TB

        def heads(ap):
            return ap.rearrange("p (h d) -> p h d", d=DH)

        block = ctx.enter_context(nc.Block())

        @block.sync
        def _(sp):
            def load_attn(l):
                sp.dma_start(wqkv[:], w["Wqkv"][l].rearrange("(c p) n -> p c n", p=P)).then_inc(w_attn, 16)
                for i, name in enumerate(("q_scale", "q_swap", "k_scale", "k_swap")):
                    sp.dma_start(qks[:, i, :], w[name][l].partition_broadcast(P)).then_inc(w_attn, 16)

            def load_wo(l):
                sp.dma_start(wo[:], w["Wo"][l].rearrange("(c p) n -> p c n", p=P)).then_inc(w_wo, 16)

            def load_ffn(l):
                sp.dma_start(w1[:], w["W1"][l].rearrange("(c p) n -> p c n", p=P)).then_inc(w_ffn, 16)
                sp.dma_start(w2[:, 0:HC - 1, :],
                             w["W2"][l][0:(HC - 1) * P].rearrange("(c p) n -> p c n", p=P)).then_inc(w_ffn, 16)
                sp.dma_start(w2[0:HREM, HC - 1, :], w["W2"][l][(HC - 1) * P:HID]).then_inc(w_ffn, 16)
                sp.dma_start(ln_g[:], w["ln_g"][l]).then_inc(w_ffn, 16)
                sp.dma_start(ln_b[:], w["ln_b"][l]).then_inc(w_ffn, 16)
                sp.dma_start(b1a[:], w["b1a"][l]).then_inc(w_ffn, 16)
                sp.dma_start(b1g[:], w["b1g"][l]).then_inc(w_ffn, 16)
                sp.dma_start(b2[:], w["b2"][l].partition_broadcast(P)).then_inc(w_ffn, 16)

            def announce(l, which=("attn", "wo", "ffn")):
                if "attn" in which:
                    sp.wait_ge(w_attn, (l + 1) * 80)
                    sp.sem_inc(attn_weights, NB)
                if "wo" in which:
                    sp.wait_ge(w_wo, (l + 1) * 16)
                    sp.sem_inc(wo_weights, NB)
                if "ffn" in which:
                    sp.wait_ge(w_ffn, (l + 1) * 128)
                    sp.sem_inc(ffn_weights, NB)

            sp.dma_start(rope[:], tabs["rope"]).then_inc(consts, 16)
            sp.dma_start(band[:], tabs["band"]).then_inc(consts, 16)
            load_attn(0)
            load_ffn(0)
            load_wo(0)
            announce(0)
            ps = phases[2][1]
            with sp.Fori(1, L) as l:
                last = l * NB - 1
                key = ("qkv", TB - 1, 5)
                sp.wait_ge(ps.sem_filled(key), ps.count(key, last))
                load_attn(l)
                key = ("wo", TB - 1)
                sp.wait_ge(ps.sem_filled(key), ps.count(key, last))
                load_wo(l)
                announce(l, ("attn", "wo"))
                key = ("f2", TB - 1)
                sp.wait_ge(ps.sem_drained(key), ps.count(key, last + 1))
                load_ffn(l)
                announce(l, ("ffn",))
            sp.sem_inc(attn_weights, 1)

        @block.tensor
        def _(pe):
            def transposes(key, it, parts):
                pe.wait_ge(ps.sem_drained(key), ps.before(key, it))
                for n, (slot, src) in enumerate(parts):
                    mm = nc.tensor.transpose(ps.ap(key)[:, slot * P:(slot + 1) * P], src, ident[:])
                mm.then_inc(ps.sem_filled(key), 1)

            def wait_drained(key, it):
                pe.wait_ge(ps.sem_drained(key), ps.count(key, it))

            pe.wait_ge(pads, 1)
            for steps, ps, first, end in phases:
                with each(pe, first, end) as it:
                    for step in steps:
                        kind = step[0]
                        if kind == "xt":
                            pe.wait_ge(xin_ready, it + 2)
                            for c in range(KC):
                                transposes(("xt", c), it, [(t, xin[:, t, c * P:(c + 1) * P]) for t in range(TB)])
                        elif kind == "qkv":
                            t, i = step[1:]
                            if t == i == 0:
                                for c in range(KC):
                                    key = ("xt", c)
                                    pe.wait_ge(ps.sem_drained(key), ps.start(key, it))
                                pe.wait_ge(attn_weights, it + 1)
                            pe.wait_ge(ps.sem_drained(step), ps.before(step, it))
                            for c in range(KC):
                                mm = nc.tensor.matmul(ps.ap(step), xsT[:, c, t * P:(t + 1) * P],
                                                      wqkv[:, c, i * HALF:(i + 1) * HALF],
                                                      start=c == 0, stop=c == KC - 1)
                            mm.then_inc(ps.sem_filled(step), 1)
                        elif kind == "tr":
                            t = step[1]
                            for i in range(4):
                                s = 4 * t + i
                                if i < 2:
                                    pe.wait_ge(rope_done, it * NQ + s + 1)
                                else:
                                    pe.wait_ge(qk_ready, it * 2 * TB + 2 * t + i - 1)
                                transposes(step + (i,), it, [(n, raw[:, s % 8, n * P:(n + 1) * P]) for n in range(4)])
                        elif kind == "s":
                            t, g = step[1:]
                            if g % 2 == 0:
                                wait_drained(("tr", t, g // 2), it)
                                wait_drained(("tr", t, 2 + g // 2), it)
                            for i in range(2):
                                key = step + (i,)
                                pe.wait_ge(ps.sem_drained(key), ps.before(key, it))
                                rows = slice(i * DH, (i + 1) * DH)
                                for n in range(2):
                                    mm = nc.tensor.matmul(ps.ap(key)[:, n * 2 * P + unseen(t):(n + 1) * 2 * P],
                                                          qT[rows, 2 * g + n, :],
                                                          kT[rows, 2 * g + n, t * P + unseen(t):(t + 2) * P],
                                                          start=True, stop=True)
                                mm.then_inc(ps.sem_filled(key), 1)
                        elif kind == "pt":
                            t, g = step[1:]
                            pe.wait_ge(prob_ready, it * NG + t * G + g + 1)
                            for i in range(2):
                                parts = [(2 * n + k, prob[:, (4 * (t * G + g) + 2 * i + n) % 12, k * P:(k + 1) * P])
                                         for n in range(2) for k in range(2) if t or k]
                                transposes(step + (i,), it, parts)
                        elif kind == "pv":
                            t, g = step[1:]
                            okey = ("o", t, g // 2)
                            if g % 2 == 0:
                                pe.wait_ge(ps.sem_drained(okey), ps.before(okey, it))
                            for i in range(2):
                                wait_drained(("pt", t, g, i), it)
                                pair = 2 * g + i
                                slot = (2 * (t * G + g) + i) % 4
                                for k in range(2):
                                    for n in range(2):
                                        h = 2 * pair + n
                                        if t or k:
                                            mm = nc.tensor.matmul(
                                                ps.ap(okey)[n * DH:(n + 1) * DH, pair % 4 * P:(pair % 4 + 1) * P],
                                                v[:, t - 1 + k, h * DH:(h + 1) * DH],
                                                pT[:, slot, (2 * n + k) * P:(2 * n + k + 1) * P],
                                                start=(k == 0 or t == 0), stop=k == 1, skip_group_check=True)
                            mm.then_inc(pv_done, 1)
                            if g % 2 == 1:
                                pe.wait_ge(pv_done, it * NG + t * G + g + 1)
                                pe.sem_inc(ps.sem_filled(okey), 1)
                        elif kind == "wo":
                            t = step[1]
                            if t == 0:
                                pe.wait_ge(wo_weights, it + 1)
                            for i in range(2):
                                wait_drained(("o", t, i), it)
                            pe.wait_ge(ps.sem_drained(step), ps.before(step, it))
                            for c in range(OC):
                                mm = nc.tensor.matmul(ps.ap(step)[:, 0:D], oT[:, c, :], wo[:, c, :],
                                                      start=c == 0, stop=c == OC - 1)
                            mm.then_inc(ps.sem_filled(step), 1)
                        elif kind == "xnt":
                            for c in range(KC):
                                pe.wait_ge(xn_ready, mlp_of(it) + 1)
                                transposes(step + (c,), it, [(t, xn[:, t, c * P:(c + 1) * P]) for t in range(TB)])
                        elif kind == "f1":
                            ch = step[1]
                            if ch == 0:
                                pe.wait_ge(ffn_weights, mlp_of(it) + 1)
                                for c in range(KC):
                                    wait_drained(("xnt", c), it)
                            m = P if ch < HC - 1 else HREM
                            for i in (1, 0):
                                key = step + (i,)
                                pe.wait_ge(ps.sem_drained(key), ps.before(key, it))
                                for c in range(KC):
                                    at = i * HID + ch * P
                                    mm = nc.tensor.matmul(ps.ap(key)[0:m, :], w1[:, c, at:at + m], xnT[:, c, :],
                                                          start=c == 0, stop=c == KC - 1)
                                mm.then_inc(ps.sem_filled(key), 1)
                        elif kind == "f2":
                            t = step[1]
                            pe.wait_ge(ps.sem_drained(step), ps.before(step, it))
                            for c in range(HC):
                                if t == 0:
                                    pe.wait_ge(h_ready, mlp_of(it) * HC + c + 1)
                                m = P if c < HC - 1 else HREM
                                mm = nc.tensor.matmul(ps.ap(step)[:, 0:D], hT[0:m, c, t * P:(t + 1) * P],
                                                      w2[0:m, c, :], start=c == 0, stop=c == HC - 1)
                            mm.then_inc(ps.sem_filled(step), 1)

        def evacuate_probs(eng, copy, ps, step, it, i):
            t, g = step[1:]
            n = t * G + g
            key = step + (i,)
            if n >= 2:
                eng.wait_ge(pv_done, it * NG + n - 1)
            eng.wait_ge(ps.sem_filled(key), ps.count(key, it))
            first = 0 if t else 1
            src = ps.ap(key).rearrange("p (n k q) -> p n k q", n=2, k=2)[:, :, first:2, :]
            dst = pT[:, (2 * n + i) % 4, :].rearrange("p (n k q) -> p n k q", n=2, k=2)[:, :, first:2, :]
            copy(dst, src).then_inc(ps.sem_drained(key), 1)

        @block.scalar
        def _(act):
            def wait_filled(key, it):
                act.wait_ge(ps.sem_filled(key), ps.count(key, it))

            act.wait_ge(pads, 1)
            for steps, ps, first, end in phases:
                with each(act, first, end) as it:
                    for step in steps:
                        kind = step[0]
                        if kind == "xt":
                            for c in range(KC):
                                key = ("xt", c)
                                wait_filled(key, it)
                                nc.scalar.copy(xsT[:, c, c:c + TB * P], ps.ap(key)).then_inc(ps.sem_drained(key), 1)
                        elif kind == "qkv":
                            t, i = step[1:]
                            if i < 4 and t >= 2:
                                old = ("tr", t - 2, i)
                                wait_filled(old, it)
                            wait_filled(step, it)
                            if i < 4:
                                n = 4 * t + i
                                if n >= 2:
                                    act.wait_ge(ss_ready, it * NQ + n - 1)
                                nc.scalar.activation(sq[:, n % 2, :], ps.ap(step), ACT.Square).then_inc(sq_ready, 1)
                            dst = raw[:, (4 * t + i) % 8, :] if i < 4 else v[:, t, (i - 4) * HALF:(i - 3) * HALF]
                            nc.scalar.copy(dst, ps.ap(step)).then_inc(ps.sem_drained(step), 1)
                        elif kind == "tr":
                            t = step[1]
                            for i in range(4):
                                key = step + (i,)
                                wait_filled(key, it)
                                src = ps.ap(key).rearrange("p (n q) -> p n q", q=P)
                                n = 4 * (i % 2)
                                dst = qT[:, n:n + 4, :] if i < 2 else kT[:, n:n + 4, (t + 1) * P:(t + 2) * P]
                                nc.scalar.copy(dst, src).then_inc(ps.sem_drained(key), 1)
                        elif kind == "e":
                            t, g = step[1:]
                            act.wait_ge(nb_ready, it * NG + t * G + g + 1)
                            for n in range(4):
                                h = 4 * g + n
                                pr = prob[:, (4 * (t * G + g) + n) % 12, unseen(t):]
                                ex = nc.scalar.activation(pr, pr, ACT.Exp, bias=nb[:, t % 2, h:h + 1],
                                                          scale=rq8[:, t, h:h + 1],
                                                          accum_out=sums[:, t % 2, h:h + 1])
                            ex.then_inc(exp_ready, 1)
                        elif kind == "pt":
                            evacuate_probs(act, nc.scalar.copy, ps, step, it, 0)
                        elif kind == "pv":
                            t, g = step[1:]
                            if g % 2 == 1:
                                key = ("o", t, g // 2)
                                if t >= 1:
                                    wait_filled(("wo", t - 1), it)
                                wait_filled(key, it)
                                nc.scalar.copy(oT[:, 4 * (g // 2):4 * (g // 2) + 4, :],
                                               ps.ap(key).rearrange("p (n q) -> p n q", q=P)
                                               ).then_inc(ps.sem_drained(key), 1)
                        elif kind == "xs":
                            act.wait_ge(x1_ready, mlp_of(it) + 1)
                            act.dma_start(xs[1:P, :, :], x1[0:P - 1, :, P:D]).then_inc(xs_ready, 16)
                            act.dma_start(xs[0:1, 1:TB, :], x1[P - 1:P, 0:TB - 1, P:D]).then_inc(xs_ready, 16)
                        elif kind == "xnt":
                            act.wait_ge(ffn_weights, mlp_of(it) + 1)
                            for c in range(KC):
                                key = step + (c,)
                                wait_filled(key, it)
                                nc.scalar.activation(xnT[:, c, :], ps.ap(key), ACT.Identity, bias=ln_b[:, c:c + 1],
                                                     scale=ln_g[:, c:c + 1]).then_inc(ps.sem_drained(key), 1)
                        elif kind == "f1":
                            ch = step[1]
                            m = P if ch < HC - 1 else HREM
                            key = step + (1,)
                            wait_filled(key, it)
                            nc.scalar.activation(hT[0:m, ch, :], ps.ap(key)[0:m], ACT.Gelu,
                                                 bias=b1g[0:m, ch:ch + 1]).then_inc(ps.sem_drained(key), 1)

        @block.vector
        def _(dve):
            def wait_filled(key, it):
                dve.wait_ge(ps.sem_filled(key), ps.count(key, it))

            def wait_drained(key, it):
                dve.wait_ge(ps.sem_drained(key), ps.count(key, it))

            def evac(out, in_):
                return nc.vector.tensor_copy(out, in_)

            nc.vector.memset(kT[:, :, 0:P], 0.0)
            nc.vector.memset(prob[:, :, 0:P - WINDOW], 0.0)
            nc.vector.memset(xsT[:, 1, 0:1], 0.0)
            nc.vector.memset(xs[0:1, 0, :], 0.0)
            nc.vector.memset(half_pow[:], -0.5).then_inc(pads, 1)
            dve.wait_ge(consts, 32)
            for steps, ps, first, end in phases:
                with each(dve, first, end) as it:
                    for step in steps:
                        kind = step[0]
                        if kind == "qkv":
                            t, i = step[1:]
                            if i >= 4:
                                continue
                            if t == i == 0:
                                dve.wait_ge(tab_ready, it + 1)
                            n = 4 * t + i
                            wait_drained(step, it)
                            if n >= 2:
                                dve.wait_ge(rope_done, it * NQ + n - 1)
                            q = raw[:, n % 8, :]
                            kindq = 2 * (i // 2)
                            cos = tab[:, t:t + 1, kindq, :].broadcast_to([P, 8, DH])
                            sin = tab[:, t:t + 1, kindq + 1, :].broadcast_to([P, 8, DH])
                            nc.vector.tensor_tensor(heads(rot[:, n % 2, 0, :]), heads(q), cos, ALU.mult)
                            swapped = q.rearrange("p (h two d) -> p h two d", two=2, d=DH // 2)[:, :, ::-1, :]
                            nc.vector.tensor_tensor(
                                rot[:, n % 2, 1, :].rearrange("p (h two d) -> p h two d", two=2, d=DH // 2),
                                swapped, sin.rearrange("p h (two d) -> p h two d", two=2),
                                ALU.mult).then_inc(rot_ready, 1)
                            dve.wait_ge(sq_ready, it * NQ + n + 1)
                            nc.vector.tensor_reduce(ss[:, t % 2, 8 * i:8 * i + 8], heads(sq[:, n % 2, :]), AX.X,
                                                    ALU.add).then_inc(ss_ready, 1)
                        elif kind == "pow":
                            t = step[1]
                            dve.wait_ge(ss_ready, it * NQ + 4 * t + 4)
                            nc.vector.tensor_scalar(ss[:, t % 2, :], ss[:, t % 2, :], 1e-24, None,
                                                    ALU.max).then_inc(ssm_ready, 1)
                        elif kind == "norm":
                            t = step[1]
                            dve.wait_ge(rn_ready, it * TB + t + 1)
                            nc.vector.tensor_scalar(rq8[:, t, :], rn[:, t % 2, 0:H], QK_SCALE, None, ALU.mult)
                            for i in range(2, 4):
                                s = 4 * t + i
                                dve.wait_ge(rope_done, it * NQ + s + 1)
                                k = heads(raw[:, s % 8, :])
                                norm = rn[:, t % 2, 8 * i:8 * i + 8].unsqueeze(2).broadcast_to([P, 8, DH])
                                nc.vector.tensor_tensor(k, k, norm, ALU.mult).then_inc(qk_ready, 1)
                        elif kind == "s":
                            t, g = step[1:]
                            n = t * G + g
                            if n >= 3:
                                old = ("pt", (n - 3) // G, (n - 3) % G)
                                for i in range(2):
                                    wait_filled(old + (i,), it)
                            for i in range(2):
                                key = step + (i,)
                                wait_filled(key, it)
                                dve.sem_inc(passed, 1)
                                for j in range(2):
                                    h = 4 * g + 2 * j + i
                                    red = nc.vector.tensor_tensor_reduce(
                                        prob[:, (4 * n + 2 * j + i) % 12, unseen(t):],
                                        ps.ap(key)[:, j * 2 * P + unseen(t):(j + 1) * 2 * P],
                                        band[:, min(t, 1), unseen(t):], 1.0, LOWEST, ALU.add, ALU.max,
                                        mx[:, t % 2, h:h + 1])
                                red.then_inc(ps.sem_drained(key), 1)
                            for i in range(2):
                                wait_drained(step + (i,), it)
                            nc.vector.scalar_tensor_tensor(
                                out=nb[:, t % 2, 4 * g:4 * g + 4], in0=mx[:, t % 2, 4 * g:4 * g + 4], scalar=-1.0,
                                in1=rq8[:, t, 4 * g:4 * g + 4], op0=ALU.mult, op1=ALU.mult).then_inc(nb_ready, 1)
                        elif kind == "pt":
                            evacuate_probs(dve, evac, ps, step, it, 1)
                        elif kind == "r":
                            t, g = step[1:]
                            dve.wait_ge(exp_ready, it * NG + t * G + g + 1)
                            nc.vector.reciprocal(rs[:, t % 2, 4 * g:4 * g + 4],
                                                 sums[:, t % 2, 4 * g:4 * g + 4]).then_inc(rs_ready, 1)
                            dve.wait_ge(rs_ready, it * NG + t * G + g + 1)
                            for n in range(4):
                                h = 4 * g + n
                                pr = prob[:, (4 * (t * G + g) + n) % 12, unseen(t):]
                                ins = nc.vector.tensor_scalar(pr, pr, rs[:, t % 2, h:h + 1], None, ALU.mult)
                            ins.then_inc(prob_ready, 1)
                        elif kind == "wo":
                            t = step[1]
                            if t == 0 and first > 0:
                                dve.wait_ge(x1b_ready, mlp_of(it) + 1)
                            wait_filled(step, it)
                            nc.vector.tensor_tensor(x1[:, t, :], ps.ap(step)[:, 0:D],
                                                    x_all[:, it % NB * TB + t, :],
                                                    ALU.add).then_inc(ps.sem_drained(step), 1)
                            if t == TB - 1:
                                wait_drained(step, it)
                                dve.sem_inc(x1_ready, 1)
                        elif kind == "ln":
                            f = mlp_of(it)
                            dve.wait_ge(xs_ready, (f + 1) * 32)
                            for t in range(TB):
                                nc.vector.bn_stats(stat[:, t, 0:6], x1[:, t, 0:P])
                                ins = nc.vector.bn_stats(stat[:, t, 6:12], xs[:, t, :])
                            ins.then_inc(stat_ready, 1)
                            dve.wait_ge(stat_ready, f + 1)
                            dve.sem_inc(passed, 1)
                            for t in range(TB):
                                agg = nc.vector.bn_aggr(mv[:, t, :], stat[:, t, :])
                            agg.then_inc(mv_ready, 1)
                            dve.wait_ge(mv_ready, f + 1)
                            nc.vector.tensor_scalar(rstd[:, 0, :], mv[:, :, 1], LN_EPS, None,
                                                    ALU.add).then_inc(eps_ready, 1)
                        elif kind == "xn":
                            f = mlp_of(it)
                            dve.wait_ge(rstd_ready, f + 1)
                            for t in range(TB):
                                for c, src in enumerate((x1[:, t, 0:P], xs[:, t, :])):
                                    ins = nc.vector.tensor_scalar(xn[:, t, c * P:(c + 1) * P], src, mv[:, t, 0:1],
                                                                  rstd[:, 1, t:t + 1], ALU.subtract, ALU.mult)
                            ins.then_inc(xn_ready, 1)
                        elif kind == "f1":
                            ch = step[1]
                            m = P if ch < HC - 1 else HREM
                            f = mlp_of(it)
                            if ch == 0:
                                dve.wait_ge(ffn_weights, f + 1)
                            wait_filled(step + (0,), it)
                            wait_drained(step + (1,), it)
                            nc.vector.scalar_tensor_tensor(
                                out=hT[0:m, ch, :], in0=ps.ap(step + (0,))[0:m], scalar=b1a[0:m, ch:ch + 1],
                                in1=hT[0:m, ch, :], op0=ALU.add, op1=ALU.mult).then_inc(h_ready, 1)
                            dve.wait_ge(h_ready, f * HC + ch + 1)
                            dve.sem_inc(ps.sem_drained(step + (0,)), 1)
                        elif kind == "f2":
                            t = step[1]
                            if t == 0:
                                dve.wait_ge(x1b_ready, mlp_of(it) + 1)
                            wait_filled(step, it)
                            nc.vector.tensor_tensor(x_all[:, mlp_of(it) % NB * TB + t, :], ps.ap(step)[:, 0:D],
                                                    xn[:, t, :], ALU.add).then_inc(ps.sem_drained(step), 1)
                            if t == TB - 1:
                                wait_drained(step, it)
                                dve.sem_inc(x_ready, 1)

        @block.gpsimd
        def _(pool):
            pool.wait_ge(pads, 1)
            pool.wait_ge(consts, 32)

            def copy_x(it):
                nc.gpsimd.tensor_copy(xin[:], x_all[:, bass.ds(it % NB * TB, TB), :]).then_inc(xin_ready, 1)

            copy_x(0)
            pool.sem_inc(x_ready, NB - 1)
            for steps, ps, first, end in phases:
                with each(pool, first, end) as it:
                    for step in steps:
                        kind = step[0]
                        if kind == "xin":
                            pool.wait_ge(x_ready, it + 1)
                            copy_x(it + 1)
                        elif kind == "tab":
                            pool.wait_ge(attn_weights, it + 2)
                            for i in range(4):
                                ins = nc.gpsimd.tensor_tensor(tab[:, :, i, :], rope[:, :, i, :],
                                                              qks[:, i:i + 1, :].broadcast_to([P, TB, DH]), ALU.mult)
                            ins.then_inc(tab_ready, 1)
                        elif kind == "qkv":
                            t, i = step[1:]
                            if i >= 4:
                                continue
                            n = 4 * t + i
                            q = raw[:, n % 8, :]
                            pool.wait_ge(rot_ready, it * NQ + n + 1)
                            nc.gpsimd.tensor_tensor(q, rot[:, n % 2, 0, :], rot[:, n % 2, 1, :],
                                                    ALU.add).then_inc(rope_done, 1)
                        elif kind == "pow":
                            t = step[1]
                            pool.wait_ge(ssm_ready, it * TB + t + 1)
                            nc.gpsimd.tensor_tensor(rn[:, t % 2, :], ss[:, t % 2, :], half_pow[:],
                                                    ALU.pow).then_inc(rn_ready, 1)
                        elif kind == "ln":
                            f = mlp_of(it)
                            pool.wait_ge(eps_ready, f + 1)
                            nc.gpsimd.tensor_tensor(rstd[:, 1, :], rstd[:, 0, :], half_pow[:, 0:TB],
                                                    ALU.pow).then_inc(rstd_ready, 1)
                        elif kind == "xnt":
                            for c in range(KC):
                                key = step + (c,)
                                pool.wait_ge(ps.sem_filled(key), ps.count(key, it))
                            pool.wait_ge(ffn_weights, mlp_of(it) + 1)
                            nc.gpsimd.tensor_tensor(xn[:], x1[:], b2[:].unsqueeze(1).broadcast_to([P, TB, D]),
                                                    ALU.add).then_inc(x1b_ready, 1)


class Norm:

    def __init__(self, nc, shared, ctx, stage, y):
        self.nc, self.y, self.x_all, self.half_pow = nc, y, shared["x"], shared["half_pow"]
        self.tiles = y.shape[1]

        def sb(name, shape):
            return ctx.enter_context(nc.sbuf_tensor(f"{stage}_{name}", shape, F32))

        def sem(name):
            return shared["sems"].enter_context(nc.semaphore(f"{stage}_{name}"))

        self.stat = sb("stat", [P, self.tiles, 6])
        self.mv = sb("mv", [P, self.tiles, 2])
        self.rstd = sb("rstd", [P, 2, self.tiles])
        self.stat_ready = sem("stat_ready")
        self.mv_ready = sem("mv_ready")
        self.eps_ready = sem("eps_ready")
        self.rstd_ready = sem("rstd_ready")
        self.x_ready = sem("x_ready")
        self.passed = sem("passed")

    def vector(self, dve, it):
        nc, n = self.nc, self.tiles
        for t in range(n):
            ins = nc.vector.bn_stats(self.stat[:, t, :], self.y[:, t, :])
        ins.then_inc(self.stat_ready, 1)
        dve.wait_ge(self.stat_ready, it + 1)
        dve.sem_inc(self.passed, 1)
        for t in range(n):
            ins = nc.vector.bn_aggr(self.mv[:, t, :], self.stat[:, t, :])
        ins.then_inc(self.mv_ready, 1)
        dve.wait_ge(self.mv_ready, it + 1)
        nc.vector.tensor_scalar(self.rstd[:, 0, :], self.mv[:, :, 1], LN_EPS, None, ALU.add).then_inc(self.eps_ready, 1)
        dve.wait_ge(self.rstd_ready, it + 1)
        for t in range(n):
            ins = nc.vector.tensor_scalar(self.x_all[:, it * n + t, :], self.y[:, t, :], self.mv[:, t, 0:1],
                                          self.rstd[:, 1, t:t + 1], ALU.subtract, ALU.mult)
        ins.then_inc(self.x_ready, 1)

    def gpsimd(self, pool, it):
        pool.wait_ge(self.eps_ready, it + 1)
        self.nc.gpsimd.tensor_tensor(self.rstd[:, 1, :], self.rstd[:, 0, :], self.half_pow[:, 0:self.tiles],
                                     ALU.pow).then_inc(self.rstd_ready, 1)


def stage_wide_attention(nc, shared, stage, w, rope, cross):
    ident, x_all = shared["ident"], shared["x"]
    D = x_all.shape[2]
    TB = 4
    NB = x_all.shape[1] // TB
    S = TB * P
    KC = D // P
    scale = float(D) ** -0.5 if cross else 128.0 ** -0.5

    with ExitStack() as ctx:
        def sb(name, shape, dt=F32):
            return ctx.enter_context(nc.sbuf_tensor(f"{stage}_{name}", shape, dt))

        def sem(name):
            return shared["sems"].enter_context(nc.semaphore(f"{stage}_{name}"))

        ps = Psum(shared)
        xin = sb("xin", [P, TB, D])
        xb = sb("xb", [P, TB, D])
        xT = sb("xT", [P, KC, S])
        qT = sb("qT", [P, KC, S])
        kT = sb("kT", [P, KC, S])
        v = sb("v", [P, TB, D])
        prob = sb("prob", [P, 2, S])
        pT = sb("pT", [P, 2, S])
        mx = sb("mx", [P, TB])
        nb = sb("nb", [P, TB])
        sums = sb("sums", [P, TB])
        rs = sb("rs", [P, TB])
        y = sb("y", [P, TB, D])
        norm = Norm(nc, shared, ctx, stage, y)
        if cross:
            srcT = sb("srcT", [P, KC, S])
            mask_int = sb("mask_int", [P, S], mybir.dt.int32)
            keep = sb("keep", [P, S])
            gone = sb("gone", [P, S])
            add_mask = sb("add_mask", [P, TB, S])
        else:
            srcT = xT
        src_ready = sem("src_ready")
        mask_landed = sem("mask_landed")
        keep_ready = sem("keep_ready")
        gone_ready = sem("gone_ready")
        add_mask_ready = sem("add_mask_ready")
        weights_ready = sem("weights_ready")
        xin_ready = sem("xin_ready")
        xb_ready = sem("xb_ready")
        scaled_ready = sem("scaled_ready")
        mx_ready = sem("mx_ready")
        nb_ready = sem("nb_ready")
        exp_ready = sem("exp_ready")
        rs_ready = sem("rs_ready")
        y_ready = sem("y_ready")

        steps = [("xin",), ("xt",), ("q",), ("k",), ("v",)]
        for t in range(TB):
            steps.append(("s", t))
            if t >= 1:
                steps.append(("pt", t - 1))
            if t >= 1:
                steps.append(("pv", t - 1))
        steps += [("pt", TB - 1), ("pv", TB - 1), ("ln",)]
        banks = {"xt": (0, 1), "q": (2, 3), "k": (0, 1), "v": (2, 3)}
        for step in steps:
            kind = step[0]
            if kind in banks:
                for i in range(2):
                    ps.fill(step + (i,), banks[kind][i])
            elif kind == "s":
                ps.fill(step, 4 + step[1] % 2)
            elif kind == "pt":
                ps.fill(step, 0 + step[1] % 2)
            elif kind == "pv":
                ps.fill(step, 6 + step[1] % 2)

        ps.finish(shared, NB)

        block = ctx.enter_context(nc.Block())

        @block.sync
        def _(sp):
            if not cross:
                return
            with sp.Fori(0, NB) as it:
                key = ("s", 2)
                sp.wait_ge(ps.sem_filled(key), ps.last_time(key, it))
                sp.dma_start(srcT[:], w["ctxT"][it].rearrange("(c p) s -> p c s", p=P)).then_inc(src_ready, 16)
                sp.dma_start(mask_int[:], w["mask"][it].partition_broadcast(P)).then_inc(mask_landed, 16)

        @block.tensor
        def _(pe):
            def empty(key, it):
                pe.wait_ge(ps.sem_drained(key), ps.before(key, it))

            def drained(key, it):
                pe.wait_ge(ps.sem_drained(key), ps.count(key, it))

            pe.wait_ge(w["landed"], w["loads"])
            if rope is not None:
                pe.wait_ge(weights_ready, 1)
            with pe.Fori(0, NB) as it:
                for step in steps:
                    kind = step[0]
                    if kind == "xt":
                        pe.wait_ge(xin_ready, it + 1)
                        for c in range(KC):
                            key = step + (c,)
                            empty(key, it)
                            for t in range(TB):
                                mm = nc.tensor.transpose(ps.ap(key)[:, t * P:(t + 1) * P],
                                                         xin[:, t, c * P:(c + 1) * P], ident[:])
                            mm.then_inc(ps.sem_filled(key), 1)
                    elif kind in ("q", "k"):
                        if kind == "q":
                            for c in range(KC):
                                drained(("xt", c), it)
                        elif cross:
                            pe.wait_ge(src_ready, (it + 1) * 16)
                        for e in range(KC):
                            key = step + (e,)
                            empty(key, it)
                            for c in range(KC):
                                mm = nc.tensor.matmul(ps.ap(key), w["W" + kind][:, c, e * P:(e + 1) * P],
                                                      (xT if kind == "q" else srcT)[:, c, :],
                                                      start=c == 0, stop=c == KC - 1)
                            mm.then_inc(ps.sem_filled(key), 1)
                    elif kind == "v":
                        for i in range(2):
                            key = step + (i,)
                            empty(key, it)
                            for n in range(2):
                                t = 2 * i + n
                                for c in range(KC):
                                    mm = nc.tensor.matmul(ps.ap(key)[:, n * D:(n + 1) * D],
                                                          srcT[:, c, t * P:(t + 1) * P], w["Wv"][:, c, :],
                                                          start=c == 0, stop=c == KC - 1)
                            mm.then_inc(ps.sem_filled(key), 1)
                    elif kind == "s":
                        t = step[1]
                        if t == 0:
                            for e in range(KC):
                                drained(("q", e), it)
                                drained(("k", e), it)
                        empty(step, it)
                        for e in range(KC):
                            mm = nc.tensor.matmul(ps.ap(step), qT[:, e, t * P:(t + 1) * P], kT[:, e, :],
                                                  start=e == 0, stop=e == KC - 1)
                        mm.then_inc(ps.sem_filled(step), 1)
                    elif kind == "pt":
                        t = step[1]
                        pe.wait_ge(exp_ready, it * TB + t + 1)
                        empty(step, it)
                        for n in range(TB):
                            mm = nc.tensor.transpose(ps.ap(step)[:, n * P:(n + 1) * P],
                                                     prob[:, t % 2, n * P:(n + 1) * P], ident[:])
                        mm.then_inc(ps.sem_filled(step), 1)
                    elif kind == "pv":
                        t = step[1]
                        if t == 0:
                            for i in range(2):
                                drained(("v", i), it)
                        drained(("pt", t), it)
                        empty(step, it)
                        for n in range(TB):
                            mm = nc.tensor.matmul(ps.ap(step)[:, 0:D], pT[:, t % 2, n * P:(n + 1) * P], v[:, n, :],
                                                  start=n == 0, stop=n == TB - 1)
                        mm.then_inc(ps.sem_filled(step), 1)

        @block.scalar
        def _(act):
            def filled(key, it):
                act.wait_ge(ps.sem_filled(key), ps.count(key, it))

            with act.Fori(0, NB) as it:
                for step in steps:
                    kind = step[0]
                    if kind == "xin":
                        key = ("pv", 0)
                        act.wait_ge(ps.sem_drained(key), ps.last_time(key, it))
                        nc.scalar.copy(xin[:], x_all[:, bass.ds(it * TB, TB), :]).then_inc(xin_ready, 1)
                    elif kind == "xt":
                        for c in range(KC):
                            filled(step + (c,), it)
                            nc.scalar.copy(xT[:, c, :], ps.ap(step + (c,))).then_inc(ps.sem_drained(step + (c,)), 1)
                    elif kind == "v":
                        for i in range(2):
                            filled(step + (i,), it)
                            nc.scalar.copy(v[:, 2 * i:2 * i + 2, :], ps.ap(step + (i,)).rearrange(
                                "p (t d) -> p t d", d=D)).then_inc(ps.sem_drained(step + (i,)), 1)
                    elif kind == "s":
                        t = step[1]
                        act.wait_ge(nb_ready, it * TB + t + 1)
                        if t >= 2:
                            filled(("pt", t - 2), it)
                        if cross:
                            nc.scalar.activation(prob[:, t % 2, :], prob[:, t % 2, :], ACT.Exp, bias=nb[:, t:t + 1],
                                                 accum_out=sums[:, t:t + 1]).then_inc(exp_ready, 1)
                        else:
                            nc.scalar.activation(prob[:, t % 2, :], ps.ap(step), ACT.Exp, bias=nb[:, t:t + 1],
                                                 scale=scale, accum_out=sums[:, t:t + 1]).then_inc(exp_ready, 1)
                            act.wait_ge(exp_ready, it * TB + t + 1)
                            act.sem_inc(ps.sem_drained(step), 1)
                    elif kind == "pt":
                        t = step[1]
                        if t >= 2:
                            filled(("pv", t - 2), it)
                        filled(step, it)
                        nc.scalar.copy(pT[:, t % 2, :], ps.ap(step)).then_inc(ps.sem_drained(step), 1)

        @block.vector
        def _(dve):
            def filled(key, it):
                dve.wait_ge(ps.sem_filled(key), ps.count(key, it))

            dve.wait_ge(w["landed"], w["loads"])
            if rope is not None:
                for name in ("Wq", "Wk"):
                    plain = w[name + "_plain"][:].rearrange("p c (e two) -> p c e two", two=2)
                    out = w[name][:].rearrange("p c (e two) -> p c e two", two=2)
                    nc.vector.tensor_tensor(out[:, :, :, 0], plain[:, :, :, 0], plain[:, :, :, 1], ALU.subtract)
                    nc.vector.tensor_tensor(out[:, :, :, 1], plain[:, :, :, 1], plain[:, :, :, 0], ALU.add)
                for name in ("bq", "bk"):
                    ins = nc.vector.tensor_tensor(w[name + "_swap"][:], w[name + "_swap"][:], w["pair_sign"][:], ALU.mult)
                ins.then_inc(weights_ready, 1)
                dve.wait_ge(weights_ready, 1)
                for name in ("bq", "bk"):
                    ins = nc.vector.tensor_tensor(w[name][:], w[name][:], w[name + "_swap"][:], ALU.add)
                ins.then_inc(weights_ready, 1)
                dve.wait_ge(weights_ready, 2)
            with dve.Fori(0, NB) as it:
                for step in steps:
                    kind = step[0]
                    if kind in ("q", "k"):
                        dst = qT if kind == "q" else kT
                        for e in range(KC):
                            key = step + (e,)
                            filled(key, it)
                            bias = w["b" + kind][:, e:e + 1]
                            if rope is not None:
                                ins = nc.vector.scalar_tensor_tensor(out=dst[:, e, :], in0=ps.ap(key), scalar=bias,
                                                                     in1=rope[:, e, :], op0=ALU.add, op1=ALU.mult)
                            else:
                                ins = nc.vector.tensor_scalar(dst[:, e, :], ps.ap(key), bias, None, ALU.add)
                            ins.then_inc(ps.sem_drained(key), 1)
                        if kind == "q" and cross:
                            dve.wait_ge(mask_landed, (it + 1) * 16)
                            nc.vector.tensor_scalar(keep[:], mask_int[:], 0.0, None,
                                                    ALU.not_equal).then_inc(keep_ready, 1)
                            dve.wait_ge(keep_ready, it + 1)
                            nc.vector.tensor_scalar(gone[:], keep[:], 1e10, -1e10, ALU.mult,
                                                    ALU.add).then_inc(gone_ready, 1)
                            dve.wait_ge(gone_ready, it + 1)
                            nc.vector.tensor_tensor(add_mask[:], w["causal"][:],
                                                    gone[:].unsqueeze(1).broadcast_to([P, TB, S]),
                                                    ALU.add).then_inc(add_mask_ready, 1)
                            dve.wait_ge(add_mask_ready, it + 1)
                    elif kind == "s":
                        t = step[1]
                        filled(step, it)
                        if cross:
                            if t >= 2:
                                filled(("pt", t - 2), it)
                            nc.vector.scalar_tensor_tensor(out=prob[:, t % 2, :], in0=ps.ap(step), scalar=scale,
                                                           in1=keep[:], op0=ALU.mult,
                                                           op1=ALU.mult).then_inc(ps.sem_drained(step), 1)
                            dve.wait_ge(ps.sem_drained(step), ps.count(step, it))
                            dve.sem_inc(norm.passed, 1)
                            nc.vector.tensor_tensor_reduce(prob[:, t % 2, :], prob[:, t % 2, :], add_mask[:, t, :], 1.0,
                                                           LOWEST, ALU.add, ALU.max,
                                                           mx[:, t:t + 1]).then_inc(mx_ready, 1)
                        else:
                            nc.vector.reduce_max(mx[:, t:t + 1], ps.ap(step), AX.X).then_inc(mx_ready, 1)
                        dve.wait_ge(mx_ready, it * TB + t + 1)
                        nc.vector.tensor_scalar(nb[:, t:t + 1], mx[:, t:t + 1], -1.0 if cross else -scale, None,
                                                ALU.mult).then_inc(nb_ready, 1)
                    elif kind == "pv":
                        t = step[1]
                        dve.wait_ge(exp_ready, it * TB + t + 1)
                        nc.vector.reciprocal(rs[:, t:t + 1], sums[:, t:t + 1]).then_inc(rs_ready, 1)
                        if t == 0:
                            dve.wait_ge(xb_ready, it + 1)
                        dve.wait_ge(rs_ready, it * TB + t + 1)
                        filled(step, it)
                        nc.vector.scalar_tensor_tensor(out=y[:, t, :], in0=ps.ap(step)[:, 0:D], scalar=rs[:, t:t + 1],
                                                       in1=xb[:, t, :], op0=ALU.mult, op1=ALU.add).then_inc(y_ready, 1)
                        dve.wait_ge(y_ready, it * TB + t + 1)
                        dve.sem_inc(ps.sem_drained(step), 1)
                    elif kind == "ln":
                        norm.vector(dve, it)

        @block.gpsimd
        def _(pool):
            pool.wait_ge(w["landed"], w["loads"])
            with pool.Fori(0, NB) as it:
                key = ("pv", TB - 1)
                pool.wait_ge(ps.sem_drained(key), ps.last_time(key, it))
                pool.wait_ge(xin_ready, it + 1)
                for c in range(KC):
                    key = ("xt", c)
                    pool.wait_ge(ps.sem_filled(key), ps.count(key, it))
                nc.gpsimd.tensor_tensor(xb[:], xin[:], w["bv"][:].unsqueeze(1).broadcast_to([P, TB, D]),
                                        ALU.add).then_inc(xb_ready, 1)
                norm.gpsimd(pool, it)


def stage_moe(nc, shared, w):
    ident, x_all = shared["ident"], shared["x"]
    D = x_all.shape[2]
    TB = 4
    NB = x_all.shape[1] // TB
    S = TB * P
    KC = D // P
    E = w["Wr"].shape[2]
    HID = w["W1"].shape[3]
    HC = HID // P
    TOP_K = 2

    with ExitStack() as ctx:
        def sb(name, shape):
            return ctx.enter_context(nc.sbuf_tensor(f"m_{name}", shape, F32))

        def sem(name):
            return shared["sems"].enter_context(nc.semaphore(f"m_{name}"))

        ps = Psum(shared)
        xin = sb("xin", [P, TB, D])
        xT = sb("xT", [P, KC, S])
        logits = sb("logits", [P, TB, E])
        above = sb("above", [P, TB, E, E])
        equal = sb("equal", [P, TB, E, E])
        rank = sb("rank", [P, TB, E])
        top = sb("top", [P, TB])
        gates = sb("gates", [P, TB, E])
        total = sb("total", [P, TB])
        gT = sb("gT", [E, S])
        hT = sb("hT", [P, 2, HC, S])
        acc = sb("acc", [P, TB, D])
        norm = Norm(nc, shared, ctx, "m", acc)
        xin_ready = sem("xin_ready")
        routed = sem("routed")
        centred_ready = sem("centred_ready")
        exp_ready = sem("exp_ready")
        gates_ready = sem("gates_ready")
        acc_ready = sem("acc_ready")
        CHAIN = 10

        steps = [("xin",), ("xt",), ("route",), ("h", 0, 0), ("h", 0, 1), ("h", 0, 2), ("gt",), ("h", 0, 3)]
        steps += [("b2", t) for t in range(TB)]
        for e in range(1, E + 1):
            for c in range(HC):
                if e < E:
                    steps.append(("h", e, c))
                steps.append(("o", e - 1, c))
        steps.append(("ln",))
        ring = {"h": 0, "o": 0}
        for step in steps:
            kind = step[0]
            if kind == "xt":
                ps.fill(step + (0,), 0)
                ps.fill(step + (1,), 1)
            elif kind == "route":
                ps.fill(step, 2)
            elif kind == "gt":
                ps.fill(step, 3)
            elif kind == "h":
                ps.fill(step, (4, 5, 0, 1)[ring["h"] % 4])
                ring["h"] += 1
            elif kind in ("o", "b2"):
                ps.fill(step, (6, 7, 2, 3)[ring["o"] % 4])
                ring["o"] += 1

        ps.finish(shared, NB)

        block = ctx.enter_context(nc.Block())

        @block.tensor
        def _(pe):
            def empty(key, it):
                pe.wait_ge(ps.sem_drained(key), ps.before(key, it))

            def drained(key, it):
                pe.wait_ge(ps.sem_drained(key), ps.count(key, it))

            pe.wait_ge(w["landed"], w["loads"])
            with pe.Fori(0, NB) as it:
                for step in steps:
                    kind = step[0]
                    if kind == "xt":
                        pe.wait_ge(xin_ready, it + 1)
                        for c in range(KC):
                            key = step + (c,)
                            empty(key, it)
                            for t in range(TB):
                                mm = nc.tensor.transpose(ps.ap(key)[:, t * P:(t + 1) * P],
                                                         xin[:, t, c * P:(c + 1) * P], ident[:])
                            mm.then_inc(ps.sem_filled(key), 1)
                    elif kind == "route":
                        for c in range(KC):
                            drained(("xt", c), it)
                        empty(step, it)
                        for t in range(TB):
                            for c in range(KC):
                                mm = nc.tensor.matmul(ps.ap(step)[:, t * E:(t + 1) * E],
                                                      xT[:, c, t * P:(t + 1) * P], w["Wr"][:, c, :],
                                                      start=c == 0, stop=c == KC - 1)
                        mm.then_inc(ps.sem_filled(step), 1)
                    elif kind == "gt":
                        pe.wait_ge(gates_ready, it + 1)
                        empty(step, it)
                        for t in range(TB):
                            mm = nc.tensor.transpose(ps.ap(step)[0:E, t * P:(t + 1) * P], gates[:, t, :], ident[:])
                        mm.then_inc(ps.sem_filled(step), 1)
                    elif kind == "b2":
                        t = step[1]
                        drained(("gt",), it)
                        empty(step, it)
                        nc.tensor.matmul(ps.ap(step)[:, 0:D], gT[:, t * P:(t + 1) * P], w["b2"][:], start=True,
                                         stop=True).then_inc(ps.sem_filled(step), 1)
                    elif kind == "h":
                        e, ch = step[1:]
                        empty(step, it)
                        for c in range(KC):
                            mm = nc.tensor.matmul(ps.ap(step), w["W1"][:, e, c, ch * P:(ch + 1) * P], xT[:, c, :],
                                                  start=c == 0, stop=c == KC - 1)
                        mm.then_inc(ps.sem_filled(step), 1)
                    elif kind == "o":
                        e, t = step[1:]
                        if t == 0:
                            for c in range(HC):
                                drained(("h", e, c), it)
                        empty(step, it)
                        for c in range(HC):
                            mm = nc.tensor.matmul(ps.ap(step)[:, 0:D], hT[:, e % 2, c, t * P:(t + 1) * P],
                                                  w["W2"][:, e, c, :], start=c == 0, stop=c == HC - 1)
                        mm.then_inc(ps.sem_filled(step), 1)

        @block.scalar
        def _(act):
            def filled(key, it):
                act.wait_ge(ps.sem_filled(key), ps.count(key, it))

            act.wait_ge(w["landed"], w["loads"])
            with act.Fori(0, NB) as it:
                for step in steps:
                    kind = step[0]
                    if kind == "xin":
                        key = ("b2", TB - 1)
                        act.wait_ge(ps.sem_drained(key), ps.last_time(key, it))
                        nc.scalar.copy(xin[:], x_all[:, bass.ds(it * TB, TB), :]).then_inc(xin_ready, 1)
                    elif kind == "xt":
                        for c in range(KC):
                            filled(step + (c,), it)
                            nc.scalar.copy(xT[:, c, :], ps.ap(step + (c,))).then_inc(ps.sem_drained(step + (c,)), 1)
                    elif kind == "h":
                        e, ch = step[1:]
                        if e >= 2:
                            filled(("o", e - 2, TB - 1), it)
                        filled(step, it)
                        nc.scalar.activation(hT[:, e % 2, ch, :], ps.ap(step), ACT.Relu,
                                             bias=w["b1"][:, e, ch:ch + 1]).then_inc(ps.sem_drained(step), 1)
                        if (e, ch) == (0, 0):
                            act.wait_ge(centred_ready, it + 1)
                            nc.scalar.activation(gates[:], gates[:], ACT.Exp).then_inc(exp_ready, 1)
                    elif kind == "gt":
                        filled(step, it)
                        nc.scalar.copy(gT[:], ps.ap(step)[0:E, :]).then_inc(ps.sem_drained(step), 1)

        @block.vector
        def _(dve):
            def filled(key, it):
                dve.wait_ge(ps.sem_filled(key), ps.count(key, it))

            dve.wait_ge(w["landed"], w["loads"])
            with dve.Fori(0, NB) as it:
                for step in steps:
                    kind = step[0]
                    if kind == "route":
                        done = [0]

                        def chained(ins):
                            done[0] += 1
                            ins.then_inc(routed, 1)
                            dve.wait_ge(routed, it * CHAIN + done[0])

                        filled(step, it)
                        nc.vector.tensor_tensor(logits[:], ps.ap(step)[:, 0:TB * E].rearrange(
                            "p (t e) -> p t e", e=E), w["br"][:].unsqueeze(1).broadcast_to([P, TB, E]),
                            ALU.add).then_inc(ps.sem_drained(step), 1)
                        dve.wait_ge(ps.sem_drained(step), ps.count(step, it))
                        mine = logits[:].unsqueeze(3).broadcast_to([P, TB, E, E])
                        other = logits[:].unsqueeze(2).broadcast_to([P, TB, E, E])
                        for t in range(TB):
                            nc.vector.tensor_tensor(above[:, t], other[:, t], mine[:, t], ALU.is_gt)
                            ins = nc.vector.tensor_tensor(equal[:, t], other[:, t], mine[:, t], ALU.is_equal)
                        chained(ins)
                        chained(nc.vector.tensor_tensor(equal[:], equal[:],
                                                        w["before"][:].unsqueeze(1).broadcast_to([P, TB, E, E]),
                                                        ALU.mult))
                        chained(nc.vector.tensor_tensor(above[:], above[:], equal[:], ALU.add))
                        nc.vector.tensor_reduce(rank[:], above[:], AX.X, ALU.add)
                        chained(nc.vector.tensor_reduce(top[:], logits[:], AX.X, ALU.max))
                        nc.vector.tensor_tensor(gates[:], logits[:], top[:].unsqueeze(2).broadcast_to([P, TB, E]),
                                                ALU.subtract).then_inc(centred_ready, 1)
                        chained(nc.vector.tensor_scalar(rank[:], rank[:], TOP_K - 0.5, None, ALU.is_lt))
                        dve.wait_ge(exp_ready, it + 1)
                        chained(nc.vector.tensor_tensor(gates[:], gates[:], rank[:], ALU.mult))
                        chained(nc.vector.tensor_reduce(total[:], gates[:], AX.X, ALU.add))
                        chained(nc.vector.reciprocal(total[:], total[:]))
                        chained(nc.vector.tensor_tensor(gates[:], gates[:],
                                                        total[:].unsqueeze(2).broadcast_to([P, TB, E]), ALU.mult))
                        dve.sem_inc(gates_ready, 1)
                        done[0] += 1
                        dve.sem_inc(routed, 1)
                        assert done[0] == CHAIN, done
                    elif kind == "b2":
                        t = step[1]
                        filled(step, it)
                        nc.vector.tensor_tensor(acc[:, t, :], ps.ap(step)[:, 0:D], xin[:, t, :],
                                                ALU.add).then_inc(acc_ready, 1)
                        dve.wait_ge(acc_ready, it * TB + t + 1)
                        dve.sem_inc(ps.sem_drained(step), 1)
                    elif kind == "o":
                        e, t = step[1:]
                        before = ("o", e - 1, t) if e else ("b2", t)
                        dve.wait_ge(ps.sem_drained(before), ps.count(before, it))
                        filled(step, it)
                        nc.vector.scalar_tensor_tensor(out=acc[:, t, :], in0=ps.ap(step)[:, 0:D],
                                                       scalar=gates[:, t, e:e + 1], in1=acc[:, t, :], op0=ALU.mult,
                                                       op1=ALU.add).then_inc(ps.sem_drained(step), 1)
                    elif kind == "ln":
                        for t in range(TB):
                            key = ("o", E - 1, t)
                            dve.wait_ge(ps.sem_drained(key), ps.count(key, it))
                        norm.vector(dve, it)

        @block.gpsimd
        def _(pool):
            with pool.Fori(0, NB) as it:
                norm.gpsimd(pool, it)


def stage_head_attention(nc, shared, stage, w, cross):
    ident, x_all = shared["ident"], shared["x"]
    D = x_all.shape[2]
    TB = 4
    NB = x_all.shape[1] // TB
    S = TB * P
    KC = D // P
    H, DH, ROWS = 16, 16, 32
    HPC = P // ROWS
    QC = H // HPC
    scale = float(DH) ** -0.5

    with ExitStack() as ctx:
        def sb(name, shape, dt=F32):
            return ctx.enter_context(nc.sbuf_tensor(f"{stage}_{name}", shape, dt))

        def sem(name):
            return shared["sems"].enter_context(nc.semaphore(f"{stage}_{name}"))

        ps = Psum(shared)
        xin = sb("xin", [P, TB, D])
        xT = sb("xT", [P, KC, S])
        qT = sb("qT", [P, H, S])
        kT = sb("kT", [P, QC, S])
        v = sb("v", [P, TB, H, ROWS])
        prob = sb("prob", [P, 4, S])
        pT = sb("pT", [P, 2 * HPC, S])
        mx = sb("mx", [P, 2, H])
        nb = sb("nb", [P, 2, H])
        o_raw = sb("o_raw", [P, QC * P])
        inv_sum = sb("inv_sum", [P, QC * P])
        oT = sb("oT", [P, QC * P])
        y = sb("y", [P, TB, D])
        norm = Norm(nc, shared, ctx, stage, y)
        srcT = sb("srcT", [P, KC, S]) if cross else xT
        mask_int = sb("mask_int", [P, TB, S], mybir.dt.int32) if cross else None
        add_mask = sb("add_mask", [P, TB, S]) if cross else w["causal"]
        src_ready = sem("src_ready")
        mask_landed = sem("mask_landed")
        masked = sem("masked")
        mask_ready = sem("mask_ready")
        xin_ready = sem("xin_ready")
        nb_ready = sem("nb_ready")
        exp_ready = sem("exp_ready")
        pads = sem("pads")
        inverted = sem("inverted")
        o_ready = sem("o_ready")
        y_ready = sem("y_ready")

        units = [(t, h) for t in range(TB) for h in range(H)]
        N = len(units)
        steps = [("xin",), ("xt",), ("q",), ("k",), ("v",)]
        for n in range(N + 3):
            if n < N:
                steps.append(("s", n))
            if 2 <= n < N + 2:
                steps.append(("pt", n - 2))
            if n >= HPC + 2 and n % HPC == 2:
                g = n // HPC - 1
                steps.append(("pv", g))
                if g % QC == QC - 1:
                    steps.append(("den", g // QC))
            if n % H == HPC + 1 and n > H:
                steps.append(("wo", n // H - 1))
        steps += [("wo", TB - 1), ("ln",)]
        for step in steps:
            kind = step[0]
            if kind in ("xt", "v"):
                for i in range(2):
                    ps.fill(step + (i,), i)
            elif kind in ("q", "k"):
                for i in range(QC):
                    ps.fill(step + (i,), 2 + i)
            elif kind == "s":
                ps.fill(step, (4, 5, 0)[step[1] % 3])
            elif kind == "pt":
                ps.fill(step, 2 + step[1] % 2)
            elif kind == "pv" and step[1] % QC == 0:
                ps.fill(("o", step[1] // QC), 6 + step[1] // QC % 2)
            elif kind in ("den", "wo"):
                ps.fill(step, 1)

        def keys(t):
            return S if cross else (t + 1) * P

        ps.finish(shared, NB)

        block = ctx.enter_context(nc.Block())

        @block.sync
        def _(sp):
            if not cross:
                return
            with sp.Fori(0, NB) as it:
                key = ("s", H)
                sp.wait_ge(ps.sem_filled(key), ps.last_time(key, it))
                sp.dma_start(srcT[:], w["ctxT"][it].rearrange("(c p) s -> p c s", p=P)).then_inc(src_ready, 16)
                sp.dma_start(mask_int[:], w["mask"][it].rearrange("(t p) s -> p t s", p=P)).then_inc(mask_landed, 16)

        @block.tensor
        def _(pe):
            def empty(key, it):
                pe.wait_ge(ps.sem_drained(key), ps.before(key, it))

            def drained(key, it):
                pe.wait_ge(ps.sem_drained(key), ps.count(key, it))

            pe.wait_ge(w["landed"], w["loads"])
            pe.wait_ge(pads, 1)
            with pe.Fori(0, NB) as it:
                for step in steps:
                    kind = step[0]
                    if kind == "xt":
                        pe.wait_ge(xin_ready, it + 1)
                        for c in range(KC):
                            key = step + (c,)
                            empty(key, it)
                            for t in range(TB):
                                mm = nc.tensor.transpose(ps.ap(key)[:, t * P:(t + 1) * P],
                                                         xin[:, t, c * P:(c + 1) * P], ident[:])
                            mm.then_inc(ps.sem_filled(key), 1)
                    elif kind in ("q", "k"):
                        if kind == "q":
                            for c in range(KC):
                                drained(("xt", c), it)
                        elif cross:
                            pe.wait_ge(src_ready, (it + 1) * 16)
                        for e in range(QC):
                            key = step + (e,)
                            empty(key, it)
                            for c in range(KC):
                                mm = nc.tensor.matmul(ps.ap(key), w["W" + kind][:, c, e * P:(e + 1) * P],
                                                      (xT if kind == "q" else srcT)[:, c, :],
                                                      start=c == 0, stop=c == KC - 1)
                            mm.then_inc(ps.sem_filled(key), 1)
                    elif kind == "v":
                        for i in range(2):
                            key = step + (i,)
                            empty(key, it)
                            for n in range(2):
                                t = 2 * i + n
                                for c in range(KC):
                                    mm = nc.tensor.matmul(ps.ap(key)[:, n * D:(n + 1) * D],
                                                          srcT[:, c, t * P:(t + 1) * P], w["Wv"][:, c, :],
                                                          start=c == 0, stop=c == KC - 1)
                            mm.then_inc(ps.sem_filled(key), 1)
                    elif kind == "s":
                        n = step[1]
                        t, h = units[n]
                        if t == 0 and h % HPC == 0:
                            drained(("q", h // HPC), it)
                            drained(("k", h // HPC), it)
                        empty(step, it)
                        nc.tensor.matmul(ps.ap(step)[:, 0:keys(t)], qT[:, h, t * P:(t + 1) * P],
                                         kT[:, h // HPC, 0:keys(t)], start=True,
                                         stop=True).then_inc(ps.sem_filled(step), 1)
                    elif kind == "pt":
                        n = step[1]
                        t, h = units[n]
                        pe.wait_ge(exp_ready, it * N + n + 1)
                        empty(step, it)
                        for k in range(keys(t) // P):
                            mm = nc.tensor.transpose(ps.ap(step)[:, k * P:(k + 1) * P],
                                                     prob[:, n % 4, k * P:(k + 1) * P], ident[:])
                        mm.then_inc(ps.sem_filled(step), 1)
                    elif kind == "pv":
                        t, g = divmod(step[1], QC)
                        if step[1] == 0:
                            for i in range(2):
                                drained(("v", i), it)
                        for j in range(HPC - 2, HPC):
                            drained(("pt", HPC * step[1] + j), it)
                        okey = ("o", t)
                        if g == 0:
                            empty(okey, it)
                        for k in range(keys(t) // P):
                            for j in range(HPC):
                                rows = slice(j * ROWS, (j + 1) * ROWS)
                                mm = nc.tensor.matmul(ps.ap(okey)[rows, g * P:(g + 1) * P],
                                                      v[:, k, HPC * g + j, :],
                                                      pT[:, HPC * (g % 2) + j, k * P:(k + 1) * P],
                                                      start=k == 0, stop=k == keys(t) // P - 1,
                                                      tile_position=(0, j * ROWS))
                        if g == QC - 1:
                            mm.then_inc(ps.sem_filled(okey), 1)
                    elif kind == "den":
                        drained(("o", step[1]), it)
                        empty(step, it)
                        nc.tensor.matmul(ps.ap(step), w["spread"][:], o_raw[:], start=True,
                                         stop=True).then_inc(ps.sem_filled(step), 1)
                    elif kind == "wo":
                        t = step[1]
                        pe.wait_ge(o_ready, it * TB + t + 1)
                        empty(step, it)
                        for g in range(QC):
                            mm = nc.tensor.matmul(ps.ap(step)[:, 0:D], oT[:, g * P:(g + 1) * P], w["Wo"][:, g, :],
                                                  start=g == 0, stop=g == QC - 1)
                        mm.then_inc(ps.sem_filled(step), 1)

        def copy_probs(eng, copy, n, it):
            t, h = units[n]
            key = ("pt", n)
            eng.wait_ge(ps.sem_filled(key), ps.count(key, it))
            copy(pT[:, n % (2 * HPC), 0:keys(t)], ps.ap(key)[:, 0:keys(t)]).then_inc(ps.sem_drained(key), 1)

        def copy_queries(eng, e, it):
            key = ("q", e)
            eng.wait_ge(ps.sem_filled(key), ps.count(key, it))
            for j in range(HPC):
                rows = slice(j * ROWS, (j + 1) * ROWS)
                out, src = qT[rows, HPC * e + j, :], ps.ap(key)[rows]
                if eng is nc.scalar:
                    if cross:
                        ins = nc.scalar.activation(out, src, ACT.Identity, bias=w["bq"][rows, e:e + 1])
                    else:
                        ins = nc.scalar.copy(out, src)
                elif cross:
                    ins = nc.vector.tensor_scalar(out, src, w["bq"][rows, e:e + 1], None, ALU.add)
                else:
                    ins = nc.vector.tensor_copy(out, src)
            ins.then_inc(ps.sem_drained(key), 1)

        def on_scalar(n):
            return n % 3 == 0

        @block.scalar
        def _(act):
            def filled(key, it):
                act.wait_ge(ps.sem_filled(key), ps.count(key, it))

            act.wait_ge(w["landed"], w["loads"])
            act.wait_ge(pads, 1)
            with act.Fori(0, NB) as it:
                for step in steps:
                    kind = step[0]
                    if kind == "xin":
                        key = ("wo", TB - 1)
                        act.wait_ge(ps.sem_drained(key), ps.last_time(key, it))
                        nc.scalar.copy(xin[:], x_all[:, bass.ds(it * TB, TB), :]).then_inc(xin_ready, 1)
                    elif kind == "xt":
                        for c in range(KC):
                            filled(step + (c,), it)
                            nc.scalar.copy(xT[:, c, :], ps.ap(step + (c,))).then_inc(ps.sem_drained(step + (c,)), 1)
                    elif kind == "q":
                        for e in range(QC // 2, QC):
                            copy_queries(nc.scalar, e, it)
                    elif kind == "k":
                        for e in range(QC):
                            key = step + (e,)
                            filled(key, it)
                            if cross:
                                ins = nc.scalar.activation(kT[:, e, :], ps.ap(key), ACT.Identity,
                                                           bias=w["bk"][:, e:e + 1])
                            else:
                                ins = nc.scalar.copy(kT[:, e, :], ps.ap(key))
                            ins.then_inc(ps.sem_drained(key), 1)
                    elif kind == "s":
                        n = step[1]
                        t, h = units[n]
                        act.wait_ge(nb_ready, it * N + n + 1)
                        pr = prob[:, n % 4, 0:keys(t)]
                        nc.scalar.activation(pr, pr, ACT.Exp, bias=nb[:, t % 2, h:h + 1],
                                             scale=scale).then_inc(exp_ready, 1)
                    elif kind == "pt" and on_scalar(step[1]):
                        copy_probs(act, nc.scalar.copy, step[1], it)
                    elif kind == "den":
                        t = step[1]
                        if t:
                            filled(("wo", t - 1), it)
                        filled(("o", t), it)
                        nc.scalar.copy(o_raw[:], ps.ap(("o", t))).then_inc(ps.sem_drained(("o", t)), 1)

        @block.vector
        def _(dve):
            def filled(key, it):
                dve.wait_ge(ps.sem_filled(key), ps.count(key, it))

            nc.vector.memset(qT[:], 0.0)
            nc.vector.memset(v[:, :, :, DH + 1:ROWS], 0.0)
            nc.vector.memset(v[:, :, :, DH:DH + 1], 1.0).then_inc(pads, 1)
            dve.wait_ge(w["landed"], w["loads"])
            dve.wait_ge(pads, 1)
            with dve.Fori(0, NB) as it:
                for step in steps:
                    kind = step[0]
                    if kind == "q":
                        for e in range(QC // 2):
                            copy_queries(nc.vector, e, it)
                    elif kind == "v":
                        for i in range(2):
                            key = step + (i,)
                            filled(key, it)
                            out = v[:, 2 * i:2 * i + 2, :, 0:DH]
                            src = ps.ap(key).rearrange("p (t h d) -> p t h d", t=2, d=DH)
                            if cross:
                                bv = w["bv"][:].rearrange("p (h d) -> p h d", d=DH)
                                ins = nc.vector.tensor_tensor(out, src, bv.unsqueeze(1).broadcast_to(
                                    [P, 2, H, DH]), ALU.add)
                            else:
                                ins = nc.vector.tensor_copy(out, src)
                            ins.then_inc(ps.sem_drained(key), 1)
                        if cross:
                            dve.wait_ge(mask_landed, (it + 1) * 16)
                            nc.vector.tensor_scalar(add_mask[:], mask_int[:], 0.0, MASKED, ALU.is_equal,
                                                    ALU.mult).then_inc(mask_ready, 1)
                            dve.wait_ge(mask_ready, it + 1)
                    elif kind == "s":
                        n = step[1]
                        t, h = units[n]
                        if n >= 4:
                            filled(("pt", n - 4), it)
                        filled(step, it)
                        dve.sem_inc(norm.passed, 1)
                        nc.vector.tensor_tensor_reduce(prob[:, n % 4, 0:keys(t)], ps.ap(step)[:, 0:keys(t)],
                                                       add_mask[:, t, 0:keys(t)], 1.0, LOWEST, ALU.add, ALU.max,
                                                       mx[:, t % 2, h:h + 1]).then_inc(ps.sem_drained(step), 1)
                        dve.wait_ge(ps.sem_drained(step), ps.count(step, it))
                        nc.vector.tensor_scalar(nb[:, t % 2, h:h + 1], mx[:, t % 2, h:h + 1], -scale, None,
                                                ALU.mult).then_inc(nb_ready, 1)
                    elif kind == "pt" and not on_scalar(step[1]):
                        copy_probs(dve, nc.vector.tensor_copy, step[1], it)
                    elif kind == "den":
                        t = step[1]
                        filled(step, it)
                        nc.vector.reciprocal(inv_sum[:], ps.ap(step)).then_inc(ps.sem_drained(step), 1)
                        if t:
                            filled(("wo", t - 1), it)
                        dve.wait_ge(ps.sem_drained(step), ps.count(step, it))
                        nc.vector.tensor_tensor(oT[:], o_raw[:], inv_sum[:], ALU.mult).then_inc(o_ready, 1)
                    elif kind == "wo":
                        t = step[1]
                        filled(step, it)
                        nc.vector.tensor_tensor(y[:, t, :], ps.ap(step)[:, 0:D], xin[:, t, :],
                                                ALU.add).then_inc(ps.sem_drained(step), 1)
                        dve.wait_ge(ps.sem_drained(step), ps.count(step, it))
                        dve.sem_inc(y_ready, 1)
                    elif kind == "ln":
                        if cross:
                            for t in range(TB):
                                ins = nc.vector.tensor_tensor(y[:, t, :], y[:, t, :], w["bo"][:], ALU.add)
                            ins.then_inc(masked, 1)
                            dve.wait_ge(masked, it + 1)
                        norm.vector(dve, it)

        @block.gpsimd
        def _(pool):
            with pool.Fori(0, NB) as it:
                norm.gpsimd(pool, it)


def mk_decoder(nc, ins, out):
    B, S, D = ins["x"].shape
    TILES = B * S // P
    scratch = nc.dram_tensor("x_before_mlp", [P, TILES, D], F32, kind="Internal").ap()
    with ExitStack() as ctx:
        def sb(c, name, shape, dt=F32):
            return c.enter_context(nc.sbuf_tensor(name, shape, dt))

        psum = ctx.enter_context(nc.psum_tensor("psum", [P, PSUM_BANKS, BANK], F32))
        ident = sb(ctx, "ident", [P, P])
        half_pow = sb(ctx, "half_pow", [P, 32])
        x_all = sb(ctx, "x_all", [P, TILES, D])
        shared = {"psum": psum, "ident": ident, "x": x_all, "half_pow": half_pow}
        landed = {n: ctx.enter_context(nc.semaphore("landed_" + n)) for n in ("x", "a0", "x0", "moe", "a1", "x1")}
        shared["sems"] = ctx
        for n in ("filled", "drained"):
            shared[n] = [ctx.enter_context(nc.semaphore(f"bank{b}_{n}")) for b in range(PSUM_BANKS)]
        shared["contents"] = [8] * PSUM_BANKS
        made = ctx.enter_context(nc.semaphore("made"))
        saved = ctx.enter_context(nc.semaphore("saved"))

        with ExitStack() as attention:
            loads = []
            place = attention

            def weight(stage, name, shape, src):
                t = sb(place, f"w_{stage}_{name}", shape)
                loads.append((stage, t[:], src))
                return t

            def chunks(ap):
                return ap.rearrange("(c p) n -> p c n", p=P)

            ORDER = ("a0", "x0", "moe", "a1", "x1")
            a0, x0, moe, a1, x1 = {}, {}, {}, {}, {}
            KC = D // P
            for st, d, pre in (("a1", a1, "L1_attn_"), ("x1", x1, "L1_xattn_")):
                for n in ("Wq", "Wk"):
                    d[n] = weight(st, n, [P, KC, 2 * D], chunks(ins[pre + n]))
                d["Wv"] = weight(st, "Wv", [P, KC, D], chunks(ins[pre + "Wv"]))
                d["Wo"] = weight(st, "Wo", [P, 2 * KC, D], chunks(ins[pre + "Wo"]))
            x0["causal"] = weight("x0", "causal", [P, S // P, S], ins["causal"])
            a1["causal"] = x0["causal"]
            a1["spread"] = x1["spread"] = weight("a1", "spread", [P, P], ins["spread"])
            for n in ("bq", "bk"):
                x1[n] = weight("x1", n, [P, 4], ins["L1_xattn_" + n])
            for n in ("bv", "bo"):
                x1[n] = weight("x1", n, [P, D], ins["L1_xattn_" + n].partition_broadcast(P))
            x1["ctxT"], x1["mask"] = ins["ctxT"], ins["mask_BxSxS2_ik0"]
            place = ctx.enter_context(ExitStack())
            for n in ("Wq", "Wk"):
                a0[n + "_plain"] = weight("a0", n, [P, KC, D], chunks(ins["L0_attn_" + n]))
                a0[n] = sb(place, "w_a0_turned_" + n, [P, KC, D])
            a0["Wv"] = weight("a0", "Wv", [P, KC, D], chunks(ins["L0_attn_Wv"]))
            for n in ("bq", "bk", "bq_swap", "bk_swap"):
                a0[n] = weight("a0", n, [P, KC], ins["L0_attn_" + n])
            a0["pair_sign"] = weight("a0", "pair_sign", [P, KC], ins["pair_sign"])
            a0["bv"] = weight("a0", "bv", [P, D], ins["L0_attn_bv"].partition_broadcast(P))
            rope = weight("a0", "rope", [P, KC, S], ins["rope_pairs"])
            for n in ("Wq", "Wk", "Wv"):
                x0[n] = weight("x0", n, [P, KC, D], chunks(ins["L0_xattn_" + n]))
            for n in ("bq", "bk"):
                x0[n] = weight("x0", n, [P, KC], ins["L0_xattn_" + n])
            x0["bv"] = weight("x0", "bv", [P, D], ins["L0_xattn_bv"].partition_broadcast(P))
            x0["ctxT"] = ins["ctxT"]
            x0["mask"] = ins["mask_Bx1xS2_ik0"].rearrange("b a s -> b (a s)")
            E, _, HID = ins["L0_ffn_W1"].shape
            moe["Wr"] = weight("moe", "Wr", [P, KC, E], chunks(ins["L0_ffn_Wr"]))
            moe["br"] = weight("moe", "br", [P, E], ins["L0_ffn_br"].partition_broadcast(P))
            moe["before"] = weight("moe", "before", [P, E, E], ins["before"].rearrange(
                "e f -> (e f)").partition_broadcast(P).rearrange("p (e f) -> p e f", e=E))
            moe["b1"] = weight("moe", "b1", [P, E, HID // P], ins["L0_ffn_b1"])
            moe["b2"] = weight("moe", "b2", [E, D], ins["L0_ffn_b2"])
            moe["W1"] = weight("moe", "W1", [P, E, KC, HID], ins["L0_ffn_W1"].rearrange("e (c p) n -> p e c n", p=P))
            moe["W2"] = weight("moe", "W2", [P, E, HID // P, D],
                               ins["L0_ffn_W2"].rearrange("e (c p) n -> p e c n", p=P))
            for st, d in (("a0", a0), ("x0", x0), ("moe", moe), ("a1", a1), ("x1", x1)):
                d["landed"], d["loads"] = landed[st], 16 * sum(1 for s, _, _ in loads if s == st)

            with nc.Block() as block:
                @block.sync
                def _(sp):
                    sp.dma_start(ident[:], ins["ident"]).then_inc(landed["x"], 16)
                    sp.dma_start(x_all[:], ins["x"].rearrange("b (t p) d -> p (b t) d", p=P)
                                 ).then_inc(landed["x"], 16)
                    for st, dst, src in sorted(loads, key=lambda load: ORDER.index(load[0])):
                        sp.dma_start(dst, src).then_inc(landed[st], 16)
                    sp.wait_ge(landed["x"], 32)

                @block.vector
                def _(dve):
                    for bank in range(PSUM_BANKS):
                        dve.sem_inc(shared["filled"][bank], 8)
                        dve.sem_inc(shared["drained"][bank], 8)
                    nc.vector.memset(half_pow[:], -0.5).then_inc(made, 1)
                    dve.wait_ge(made, 1)

            stage_wide_attention(nc, shared, "a0", a0, rope, cross=False)
            stage_wide_attention(nc, shared, "x0", x0, None, cross=True)
            stage_moe(nc, shared, moe)
            place.close()
            stage_head_attention(nc, shared, "a1", a1, cross=False)
            stage_head_attention(nc, shared, "x1", x1, cross=True)

        with nc.Block() as block:
            @block.sync
            def _(sp):
                sp.dma_start(scratch, x_all[:]).then_inc(saved, 16)
                sp.wait_ge(saved, 16)
        stage_l1_ffn(nc, shared, ins, ins)
        stage_final(nc, shared, scratch, out)


def stage_final(nc, shared, scratch, out):
    x_all = shared["x"]
    _, TILES, D = x_all.shape
    TB = 4
    NB = TILES // TB
    with ExitStack() as ctx:
        x_old = ctx.enter_context(nc.sbuf_tensor("x_old", [P, TILES, D], F32))
        y = ctx.enter_context(nc.sbuf_tensor("z_y", [P, TILES, D], F32))
        norm = Norm(nc, shared, ctx, "z", y)
        old_landed = ctx.enter_context(nc.semaphore("z_old_landed"))
        summed = ctx.enter_context(nc.semaphore("z_summed"))
        stored = ctx.enter_context(nc.semaphore("z_stored"))
        out_v = out.rearrange("b (t p) d -> p (b t) d", p=P)
        with nc.Block() as block:
            @block.sync
            def _(sp):
                sp.dma_start(x_old[:], scratch).then_inc(old_landed, 16)
                sp.wait_ge(norm.x_ready, 1)
                sp.dma_start(out_v, x_all[:]).then_inc(stored, 16)
                sp.wait_ge(stored, 16)

            @block.vector
            def _(dve):
                dve.wait_ge(old_landed, 16)
                nc.vector.tensor_tensor(y[:], x_old[:], x_all[:], ALU.add).then_inc(summed, 1)
                dve.wait_ge(summed, 1)
                norm.vector(dve, 0)

            @block.gpsimd
            def _(pool):
                norm.gpsimd(pool, 0)


def tables():
    import numpy as np

    f32 = np.float32
    S, D, E, DH = 512, 256, 8, 64
    t = {"ident": np.eye(P, dtype=f32)}
    pos = np.arange(S, dtype=f32)
    inv = (f32(10000.0) ** (np.arange(0, 128, 2, dtype=f32) / f32(128))).astype(f32)
    rad = (pos[:, None] / inv).astype(f32)
    sincos = np.repeat(np.stack((np.sin(rad), np.cos(rad)), axis=-1).reshape(S, -1), 2, axis=-1)
    t["rope_pairs"] = sincos.T.reshape(D // P, P, S).transpose(1, 0, 2)
    t["pair_sign"] = np.where(np.arange(P) % 2 == 0, -1, 1)[:, None] * np.ones((1, D // P))
    q, k = np.arange(S)[:, None], np.arange(S)[None]
    tiled = lambda a: a.reshape(S // P, P, S).transpose(1, 0, 2)
    t["causal"] = tiled(np.where(k > q, -1e10, 0.0))
    row = np.arange(P)
    t["spread"] = np.where(row[:, None] == row[None] // 32 * 32 + 16, 1.0, 0.0)
    t["before"] = np.where(np.arange(E)[None] < np.arange(E)[:, None], 1.0, 0.0)
    half = np.arange(0, DH, 2, dtype=f32)
    freq = (f32(1.0) / f32(10000.0) ** (half / f32(DH))).astype(f32)
    ang = np.concatenate([pos[:, None] * freq[None]] * 2, -1).astype(f32)
    base = ((half + f32(0.4 * DH)) / f32(1.4 * DH)).astype(f32)
    power = ((pos - S // 2) / 32).astype(f32)
    sc = (base[None] ** power[:, None]).astype(f32)
    sc = np.concatenate([sc, sc], -1)
    sign = np.where(np.arange(DH) < DH // 2, -1, 1).astype(f32)
    cos, sin = np.cos(ang), np.sin(ang) * sign
    inv_sc = (f32(1.0) / sc).astype(f32)
    t["rope"] = np.stack([cos * sc, sin * sc, cos * inv_sc, sin * inv_sc], 1).reshape(S // P, P, 4, DH).transpose(
        1, 0, 2, 3)
    p, j = np.arange(P)[:, None], np.arange(2 * P)[None]
    near = (P + p - j >= 0) & (P + p - j <= 64)
    t["band"] = np.stack([np.where(near & (j >= P), 0.0, -1e30), np.where(near, 0.0, -1e30)], 1)
    return {n: np.ascontiguousarray(a, dtype=f32) for n, a in t.items()}


def lay_out(inputs):
    import numpy as np

    a = {n: np.asarray(v) for n, v in inputs.items()}
    D = a["x"].shape[-1]
    g = {n: a[n] for n in ("x", "mask_Bx1xS2_ik0", "mask_BxSxS2_ik0")}
    g["ctxT"] = a["ctx_1024"].transpose(0, 2, 1)

    def columns(v, chunks):
        out = np.zeros(v.shape[:-1] + (chunks * P,), v.dtype)
        out[..., :v.shape[-1]] = v
        return out.reshape(v.shape[:-1] + (chunks, P)).swapaxes(-1, -2)

    def spaced(v):
        out = np.zeros(v.shape[:-1] + (D // 16, 32), v.dtype)
        out[..., :16] = v.reshape(v.shape[:-1] + (D // 16, 16))
        return out.reshape(v.shape[:-1] + (2 * D,))

    for n in ("Wq", "Wk", "Wv"):
        g["L0_attn_" + n] = a["L0_attn_" + n].T
        g["L0_xattn_" + n] = a["L0_xattn_" + n].T
    for n in ("bq", "bk"):
        g["L0_attn_" + n] = columns(a["L0_attn_" + n], D // P)
        g["L0_attn_" + n + "_swap"] = columns(a["L0_attn_" + n].reshape(-1, 2)[:, ::-1].reshape(-1), D // P)
        g["L0_xattn_" + n] = columns(a["L0_xattn_" + n], D // P)
    for n in ("L0_attn_bv", "L0_xattn_bv", "L0_ffn_Wr", "L0_ffn_br", "L0_ffn_W1", "L0_ffn_W2", "L0_ffn_b2",
              "L1_xattn_bv", "L1_xattn_bo"):
        g[n] = a[n]
    g["L0_ffn_b1"] = columns(a["L0_ffn_b1"], a["L0_ffn_b1"].shape[1] // P).transpose(1, 0, 2)
    for pre in ("L1_attn_", "L1_xattn_"):
        for n in ("Wq", "Wk"):
            g[pre + n] = spaced(a[pre + n].T)
        g[pre + "Wv"] = a[pre + "Wv"].T
        g[pre + "Wo"] = spaced(a[pre + "Wo"]).T
    for n in ("bq", "bk"):
        g["L1_xattn_" + n] = columns(spaced(a["L1_xattn_" + n]), 2 * D // P)
    for n in ("Wqkv", "Wo", "W1", "W2", "b2"):
        g[n] = a["L1_ffn_" + n]
    for n in ("q", "k"):
        s = a[f"L1_ffn_{n}_scale"]
        g[n + "_scale"] = s
        g[n + "_swap"] = np.concatenate([s[:, s.shape[1] // 2:], s[:, :s.shape[1] // 2]], 1)
    for n in ("ln_g", "ln_b"):
        g[n] = columns(a["L1_ffn_" + n], D // P)
    hid = a["L1_ffn_W2"].shape[1]
    g["b1a"] = columns(a["L1_ffn_b1"][:, :hid], -(-hid // P))
    g["b1g"] = columns(a["L1_ffn_b1"][:, hid:], -(-hid // P))
    return {n: np.ascontiguousarray(v) for n, v in g.items()}


def kernel(**inputs):
    import concourse.bacc as _bacc
    from concourse import mybir as _mybir
    from concourse.bass_utils import run_bass_kernel_spmd as _run

    nc = _bacc.Bacc("TRN2", target_bir_lowering=False, num_devices=1)
    laid = lay_out(inputs)
    laid.update(tables())
    arrays = {f"in_{n}": v for n, v in laid.items()}
    ins = {n: nc.dram_tensor(f"in_{n}", v.shape, _mybir.dt.from_np(v.dtype), kind="ExternalInput").ap()
           for n, v in laid.items()}
    out = nc.dram_tensor("out", laid["x"].shape, F32, kind="ExternalOutput").ap()
    mk_decoder(nc, ins, out)
    r = _run(nc, [arrays], core_ids=[0])
    return r.results[0]["out"]
```

```python
from contextlib import ExitStack, contextmanager

import concourse.bass as bass
from concourse import mybir

P = 128
F32 = mybir.dt.float32
ALU = mybir.AluOpType
ACT = mybir.ActivationFunctionType
AX = mybir.AxisListType
PSUM_BANKS = 8
BANK = 512
LOWEST = -3.0e38
LN_EPS = 1e-5
MASKED = -1.0e30


class Psum:

    def __init__(self, shared, first=0):
        self.first = first
        self.tensor, self.filled, self.drained = shared["psum"], shared["filled"], shared["drained"]
        self.earlier = shared["contents"]
        self.bank, self.number, self.per = {}, {}, [0] * PSUM_BANKS

    def fill(self, key, bank):
        assert key not in self.bank, key
        self.bank[key], self.number[key] = bank, self.per[bank] + 1
        self.per[bank] += 1

    def finish(self, shared, iterations):
        shared["contents"] = [n + iterations * m for n, m in zip(self.earlier, self.per)]

    def ap(self, key):
        return self.tensor[:, self.bank[key], :]

    def sem_filled(self, key):
        return self.filled[self.bank[key]]

    def sem_drained(self, key):
        return self.drained[self.bank[key]]

    def start(self, key, it):
        b = self.bank[key]
        return it * self.per[b] + (self.earlier[b] - self.first * self.per[b])

    def before(self, key, it):
        return self.start(key, it) + (self.number[key] - 1)

    def last_time(self, key, it):
        assert self.earlier[self.bank[key]] + self.number[key] > self.per[self.bank[key]]
        return self.start(key, it) + (self.number[key] - self.per[self.bank[key]])

    def count(self, key, it):
        return self.start(key, it) + self.number[key]


class MlpStageWeights:

    def __init__(self, nc, ctx, shared, w, tabs):
        L, D, QKV = w["Wqkv"].shape
        INNER, HID, TB, DH = QKV // 3, w["W2"].shape[1], 4, 64
        KC, OC, HC = D // P, INNER // P, -(-HID // P)
        HREM = HID - (HC - 1) * P

        def sb(name, shape):
            return ctx.enter_context(nc.sbuf_tensor("f_" + name, shape, F32, side="right"))

        def sem(name):
            return shared["sems"].enter_context(nc.semaphore("f_" + name))

        self.source, self.tabs, self.HC, self.HREM, self.HID = w, tabs, HC, HREM, HID
        self.wqkv = sb("wqkv", [P, KC, QKV])
        self.wo = sb("wo", [P, OC, D])
        self.ln_g = sb("ln_g", [P, KC])
        self.ln_b = sb("ln_b", [P, KC])
        self.b1a = sb("b1a", [P, HC])
        self.b1g = sb("b1g", [P, HC])
        self.b2 = sb("b2", [P, D])
        self.qks = sb("qks", [P, 4, DH])
        self.rope = sb("rope", [P, TB, 4, DH])
        self.band = sb("band", [P, 2, 2 * P])
        self.w_attn = sem("w_attn")
        self.w_wo = sem("w_wo")
        self.w_ffn = sem("w_ffn")
        self.consts = sem("consts")

    def load_first(self, sp):
        sp.dma_start(self.rope[:], self.tabs["rope"]).then_inc(self.consts, 16)
        sp.dma_start(self.band[:], self.tabs["band"]).then_inc(self.consts, 16)
        self.load_attn(sp, 0)
        self.load_wo(sp, 0)

    def place_mlp(self, nc, ctx):
        _, KC, _ = self.wqkv.shape
        D = self.wo.shape[2]
        self.w1 = ctx.enter_context(nc.sbuf_tensor("f_w1", [P, KC, 2 * self.HID], F32))
        self.w2 = ctx.enter_context(nc.sbuf_tensor("f_w2", [P, self.HC, D], F32))

    def load_attn(self, sp, l):
        w = self.source
        sp.dma_start(self.wqkv[:], w["Wqkv"][l].rearrange("(c p) n -> p c n", p=P)).then_inc(self.w_attn, 16)
        for i, name in enumerate(("q_scale", "q_swap", "k_scale", "k_swap")):
            sp.dma_start(self.qks[:, i, :], w[name][l].partition_broadcast(P)).then_inc(self.w_attn, 16)

    def load_wo(self, sp, l):
        sp.dma_start(self.wo[:], self.source["Wo"][l].rearrange("(c p) n -> p c n", p=P)).then_inc(self.w_wo, 16)

    def load_ffn(self, sp, l):
        w, full = self.source, (self.HC - 1) * P
        sp.dma_start(self.w1[:], w["W1"][l].rearrange("(c p) n -> p c n", p=P)).then_inc(self.w_ffn, 16)
        sp.dma_start(self.w2[:, 0:self.HC - 1, :],
                     w["W2"][l][0:full].rearrange("(c p) n -> p c n", p=P)).then_inc(self.w_ffn, 16)
        sp.dma_start(self.w2[0:self.HREM, self.HC - 1, :], w["W2"][l][full:self.HID]).then_inc(self.w_ffn, 16)
        sp.dma_start(self.ln_g[:], w["ln_g"][l]).then_inc(self.w_ffn, 16)
        sp.dma_start(self.ln_b[:], w["ln_b"][l]).then_inc(self.w_ffn, 16)
        sp.dma_start(self.b1a[:], w["b1a"][l]).then_inc(self.w_ffn, 16)
        sp.dma_start(self.b1g[:], w["b1g"][l]).then_inc(self.w_ffn, 16)
        sp.dma_start(self.b2[:], w["b2"][l].partition_broadcast(P)).then_inc(self.w_ffn, 16)


def stage_l1_ffn(nc, shared, weights, before):
    ident, x_all = shared["ident"], shared["x"]
    w = weights.source
    L, D, QKV = w["Wqkv"].shape
    INNER = QKV // 3
    HID = w["W2"].shape[1]
    H, DH = 16, 64
    WINDOW = 64
    TB = 4
    NB = x_all.shape[1] // TB
    KC = D // P
    OC = INNER // P
    HC = -(-HID // P)
    HREM = HID - (HC - 1) * P
    HALF = INNER // 2
    G = H // 4
    QK_SCALE = 8.0

    with ExitStack() as ctx:
        def sb(name, shape):
            return ctx.enter_context(nc.sbuf_tensor("f_" + name, shape, F32))

        def sem(name):
            return shared["sems"].enter_context(nc.semaphore("f_" + name))

        tab = sb("tab", [P, TB, 4, DH])
        weights.place_mlp(nc, ctx)
        wqkv, wo, w1, w2 = weights.wqkv, weights.wo, weights.w1, weights.w2
        ln_g, ln_b, b1a, b1g, b2 = weights.ln_g, weights.ln_b, weights.b1a, weights.b1g, weights.b2
        qks, rope, band = weights.qks, weights.rope, weights.band
        w_attn, w_wo, w_ffn, consts = weights.w_attn, weights.w_wo, weights.w_ffn, weights.consts
        xin = sb("xin", [P, TB, D])
        xsT = sb("xsT", [P, KC, TB * P + 1])
        raw = sb("raw", [P, 8, HALF])
        sq = sb("sq", [P, 2, HALF])
        rot = sb("rot", [P, 2, 2, HALF])
        ss = sb("ss", [P, 2, 4 * 8])
        rn = sb("rn", [P, 2, 4 * 8])
        half_pow = sb("half_pow", [P, 4 * 8])
        rq8 = sb("rq8", [P, TB, H])
        qT = sb("qT", [P, H // 2, P])
        kT = sb("kT", [P, H // 2, (TB + 1) * P])
        v = sb("v", [P, TB, INNER])
        prob = sb("prob", [P, 12, 2 * P])
        mx = sb("mx", [P, 2, H])
        nb = sb("nb", [P, 2, H])
        sums = sb("sums", [P, 2, H])
        rs = sb("rs", [P, 2, H])
        pT = sb("pT", [P, 4, BANK])
        oT = sb("oT", [P, OC, P])
        xs = sb("xs", [P, TB, P])
        xn = sb("xn", [P, TB, D])
        xnT = sb("xnT", [P, KC, TB * P])
        stat = sb("stat", [P, TB, 12])
        mv = sb("mv", [P, TB, 2])
        rstd = sb("rstd", [P, 2, TB])
        x1 = sb("x1", [P, TB, D])
        hT = sb("hT", [P, HC, TB * P])

        pads = sem("pads")
        saved = sem("saved")
        passed = sem("passed")
        tab_ready = sem("tab_ready")
        xin_ready = sem("xin_ready")
        sq_ready = sem("sq_ready")
        rot_ready = sem("rot_ready")
        rope_done = sem("rope_done")
        ss_ready = sem("ss_ready")
        ssm_ready = sem("ssm_ready")
        rn_ready = sem("rn_ready")
        qk_ready = sem("qk_ready")
        nb_ready = sem("nb_ready")
        exp_ready = sem("exp_ready")
        rs_ready = sem("rs_ready")
        prob_ready = sem("prob_ready")
        x1_ready = sem("x1_ready")
        attn_weights = sem("attn_weights")
        wo_weights = sem("wo_weights")
        ffn_weights = sem("ffn_weights")
        xs_ready = sem("xs_ready")
        stat_ready = sem("stat_ready")
        mv_ready = sem("mv_ready")
        eps_ready = sem("eps_ready")
        rstd_ready = sem("rstd_ready")
        xn_ready = sem("xn_ready")
        x1b_ready = sem("x1b_ready")
        x_ready = sem("x_ready")
        h_ready = sem("h_ready")

        N = G * TB
        MLP = ("xs", "ln", "xn", "xnt", "f1", "f2")

        def project(t, parts):
            return [("qkv", t, i) for i in parts]

        dense = {0: project(2, (0, 4)), 1: project(2, (1, 5)), 2: project(2, (2,)),
                 3: project(2, (3,)) + [("pow", 2), ("f1", 0)],
                 4: [("f1", 1)] + project(3, (0,)), 5: project(3, (1, 4)) + [("norm", 2)], 6: project(3, (2, 5)),
                 7: project(3, (3,)) + [("pow", 3), ("wo", 0)],
                 8: [("f1", 2), ("f1", 3), ("xin",)], 9: [("norm", 3)], 10: [("f1", 4), ("f1", 5)], 11: [("wo", 1)],
                 12: [("f2", 0)], 13: [("f2", 1)], 14: [("f2", 2)], 15: [("wo", 2), ("tab",)],
                 16: [("xt",)]}

        def iteration():
            yield from [("xs",), *project(0, range(6)), ("ln",), ("pow", 0), *project(1, (0, 1)), ("xn",)]
            yield from [("norm", 0), *project(1, range(2, 6)), ("pow", 1), ("tr", 0), ("xnt",)]
            for n in range(N + 3):
                t, g = divmod(n, G)
                turn = g == G - 1 and t + 1 < TB
                if n < N:
                    yield ("s", t, g)
                if turn:
                    yield from [("tr", t + 1), ("e", t, g - 1)]
                if 1 <= n <= N:
                    yield ("r", *divmod(n - 1, G))
                if n == 1:
                    yield ("norm", 1)
                if 2 <= n <= N + 1:
                    yield ("pt", *divmod(n - 2, G))
                yield from dense.get(n, ())
                if n < N and (g != G - 2 or t + 1 == TB):
                    yield ("e", t, g)
                if 3 <= n:
                    yield ("pv", *divmod(n - 3, G))
            yield ("f2", 3)
            yield ("wo", TB - 1)

        ITS = L * NB
        phases = []
        every = list(iteration())
        for steps, first, end in (([("tab",), ("xt",)], -1, 0),
                                  ([step for step in every if step[0] not in MLP], 0, 1), (every, 1, ITS),
                                  ([step for step in every if step[0] in MLP], ITS, ITS + 1)):
            ps = Psum(shared, first)
            ring = {"p": 0, "t": 0}
            for step in steps:
                kind = step[0]
                if kind in ("xt", "tr", "xnt", "pt"):
                    for i in range(4 if kind == "tr" else 2):
                        ps.fill(step + (i,), 2 + ring["t"] % 2)
                        ring["t"] += 1
                elif kind == "s":
                    for i in range(2):
                        ps.fill(step + (i,), 4 + i)
                elif kind == "pv" and step[2] % 2 == 0:
                    ps.fill(("o", step[1], step[2] // 2), 6 + step[2] // 2 % 2)
                elif kind in ("qkv", "wo", "f2", "f1"):
                    for key in ((step + (1,), step + (0,)) if kind == "f1" else (step,)):
                        ps.fill(key, ring["p"] % 2)
                        ring["p"] += 1
            ps.finish(shared, end - first)
            phases.append((steps, ps, first, end))

        @contextmanager
        def each(engine, first, end):
            if end - first == 1:
                yield first
            else:
                with engine.Fori(first, end) as it:
                    yield it

        def mlp_of(it):
            return it - 1

        def unseen(t):
            return P - WINDOW if t else P

        NQ = 4 * TB
        NG = G * TB

        def heads(ap):
            return ap.rearrange("p (h d) -> p h d", d=DH)

        block = ctx.enter_context(nc.Block())

        @block.sync
        def _(sp):
            def announce(l, which=("attn", "wo", "ffn")):
                if "attn" in which:
                    sp.wait_ge(w_attn, (l + 1) * 80)
                    sp.sem_inc(attn_weights, NB)
                if "wo" in which:
                    sp.wait_ge(w_wo, (l + 1) * 16)
                    sp.sem_inc(wo_weights, NB)
                if "ffn" in which:
                    sp.wait_ge(w_ffn, (l + 1) * 128)
                    sp.sem_inc(ffn_weights, NB)

            weights.load_ffn(sp, 0)
            sp.dma_start(before, x_all[:]).then_inc(saved, 16)
            announce(0)
            ps = phases[2][1]
            with sp.Fori(1, L) as l:
                last = l * NB - 1
                key = [step for step in every if step[0] == "qkv"][-1]
                sp.wait_ge(ps.sem_filled(key), ps.count(key, last))
                weights.load_attn(sp, l)
                key = ("wo", TB - 1)
                sp.wait_ge(ps.sem_filled(key), ps.count(key, last))
                weights.load_wo(sp, l)
                announce(l, ("attn", "wo"))
                key = ("f2", TB - 1)
                sp.wait_ge(ps.sem_drained(key), ps.count(key, last + 1))
                weights.load_ffn(sp, l)
                announce(l, ("ffn",))
            sp.sem_inc(attn_weights, 1)

        @block.tensor
        def _(pe):
            def transposes(key, it, parts):
                pe.wait_ge(ps.sem_drained(key), ps.before(key, it))
                for n, (slot, src) in enumerate(parts):
                    mm = nc.tensor.transpose(ps.ap(key)[:, slot * P:(slot + 1) * P], src, ident[:])
                mm.then_inc(ps.sem_filled(key), 1)

            def wait_drained(key, it):
                pe.wait_ge(ps.sem_drained(key), ps.count(key, it))

            pe.wait_ge(pads, 1)
            for steps, ps, first, end in phases:
                with each(pe, first, end) as it:
                    for step in steps:
                        kind = step[0]
                        if kind == "xt":
                            pe.wait_ge(xin_ready, it + 2)
                            for c in range(KC):
                                transposes(("xt", c), it, [(t, xin[:, t, c * P:(c + 1) * P]) for t in range(TB)])
                        elif kind == "qkv":
                            t, i = step[1:]
                            if t == i == 0:
                                for c in range(KC):
                                    key = ("xt", c)
                                    pe.wait_ge(ps.sem_drained(key), ps.start(key, it))
                                pe.wait_ge(attn_weights, it + 1)
                            pe.wait_ge(ps.sem_drained(step), ps.before(step, it))
                            for c in range(KC):
                                mm = nc.tensor.matmul(ps.ap(step), xsT[:, c, t * P:(t + 1) * P],
                                                      wqkv[:, c, i * HALF:(i + 1) * HALF],
                                                      start=c == 0, stop=c == KC - 1)
                            mm.then_inc(ps.sem_filled(step), 1)
                        elif kind == "tr":
                            t = step[1]
                            for i in range(4):
                                s = 4 * t + i
                                if i < 2:
                                    pe.wait_ge(rope_done, it * NQ + s + 1)
                                else:
                                    pe.wait_ge(qk_ready, it * 2 * TB + 2 * t + i - 1)
                                transposes(step + (i,), it, [(n, raw[:, s % 8, n * P:(n + 1) * P]) for n in range(4)])
                        elif kind == "s":
                            t, g = step[1:]
                            if g % 2 == 0:
                                wait_drained(("tr", t, g // 2), it)
                                wait_drained(("tr", t, 2 + g // 2), it)
                            for i in range(2):
                                key = step + (i,)
                                pe.wait_ge(ps.sem_drained(key), ps.before(key, it))
                                rows = slice(i * DH, (i + 1) * DH)
                                for n in range(2):
                                    mm = nc.tensor.matmul(ps.ap(key)[:, n * 2 * P + unseen(t):(n + 1) * 2 * P],
                                                          qT[rows, 2 * g + n, :],
                                                          kT[rows, 2 * g + n, t * P + unseen(t):(t + 2) * P],
                                                          start=True, stop=True)
                                mm.then_inc(ps.sem_filled(key), 1)
                        elif kind == "pt":
                            t, g = step[1:]
                            pe.wait_ge(prob_ready, it * NG + t * G + g + 1)
                            for i in range(2):
                                parts = [(2 * n + k, prob[:, (4 * (t * G + g) + 2 * i + n) % 12, k * P:(k + 1) * P])
                                         for n in range(2) for k in range(2) if t or k]
                                transposes(step + (i,), it, parts)
                        elif kind == "pv":
                            t, g = step[1:]
                            okey = ("o", t, g // 2)
                            if g % 2 == 0:
                                pe.wait_ge(ps.sem_drained(okey), ps.before(okey, it))
                            for i in range(2):
                                wait_drained(("pt", t, g, i), it)
                                pair = 2 * g + i
                                slot = (2 * (t * G + g) + i) % 4
                                for k in range(2):
                                    for n in range(2):
                                        h = 2 * pair + n
                                        if t or k:
                                            mm = nc.tensor.matmul(
                                                ps.ap(okey)[n * DH:(n + 1) * DH, pair % 4 * P:(pair % 4 + 1) * P],
                                                v[:, t - 1 + k, h * DH:(h + 1) * DH],
                                                pT[:, slot, (2 * n + k) * P:(2 * n + k + 1) * P],
                                                start=(k == 0 or t == 0), stop=k == 1, skip_group_check=True)
                            if g % 2 == 1:
                                mm.then_inc(ps.sem_filled(okey), 1)
                        elif kind == "wo":
                            t = step[1]
                            if t == 0:
                                pe.wait_ge(wo_weights, it + 1)
                            for i in range(2):
                                wait_drained(("o", t, i), it)
                            pe.wait_ge(ps.sem_drained(step), ps.before(step, it))
                            for c in range(OC):
                                mm = nc.tensor.matmul(ps.ap(step)[:, 0:D], oT[:, c, :], wo[:, c, :],
                                                      start=c == 0, stop=c == OC - 1)
                            mm.then_inc(ps.sem_filled(step), 1)
                        elif kind == "xnt":
                            for c in range(KC):
                                pe.wait_ge(xn_ready, mlp_of(it) + 1)
                                transposes(step + (c,), it, [(t, xn[:, t, c * P:(c + 1) * P]) for t in range(TB)])
                        elif kind == "f1":
                            ch = step[1]
                            if ch == 0:
                                pe.wait_ge(ffn_weights, mlp_of(it) + 1)
                                for c in range(KC):
                                    wait_drained(("xnt", c), it)
                            m = P if ch < HC - 1 else HREM
                            for i in (1, 0):
                                key = step + (i,)
                                pe.wait_ge(ps.sem_drained(key), ps.before(key, it))
                                for c in range(KC):
                                    at = i * HID + ch * P
                                    mm = nc.tensor.matmul(ps.ap(key)[0:m, :], w1[:, c, at:at + m], xnT[:, c, :],
                                                          start=c == 0, stop=c == KC - 1)
                                mm.then_inc(ps.sem_filled(key), 1)
                        elif kind == "f2":
                            t = step[1]
                            pe.wait_ge(ps.sem_drained(step), ps.before(step, it))
                            for c in range(HC):
                                if t == 0:
                                    pe.wait_ge(h_ready, mlp_of(it) * HC + c + 1)
                                m = P if c < HC - 1 else HREM
                                mm = nc.tensor.matmul(ps.ap(step)[:, 0:D], hT[0:m, c, t * P:(t + 1) * P],
                                                      w2[0:m, c, :], start=c == 0, stop=c == HC - 1)
                            mm.then_inc(ps.sem_filled(step), 1)

        def evacuate_probs(eng, copy, ps, step, it, i):
            t, g = step[1:]
            n = t * G + g
            key = step + (i,)
            eng.wait_ge(ps.sem_filled(key), ps.count(key, it))
            first = 0 if t else 1
            src = ps.ap(key).rearrange("p (n k q) -> p n k q", n=2, k=2)[:, :, first:2, :]
            dst = pT[:, (2 * n + i) % 4, :].rearrange("p (n k q) -> p n k q", n=2, k=2)[:, :, first:2, :]
            copy(dst, src).then_inc(ps.sem_drained(key), 1)

        @block.scalar
        def _(act):
            def wait_filled(key, it):
                act.wait_ge(ps.sem_filled(key), ps.count(key, it))

            act.wait_ge(pads, 1)
            for steps, ps, first, end in phases:
                with each(act, first, end) as it:
                    for step in steps:
                        kind = step[0]
                        if kind == "xt":
                            for c in range(KC):
                                key = ("xt", c)
                                wait_filled(key, it)
                                nc.scalar.copy(xsT[:, c, c:c + TB * P], ps.ap(key)).then_inc(ps.sem_drained(key), 1)
                        elif kind == "qkv":
                            t, i = step[1:]
                            if i < 4 and t >= 2:
                                old = ("tr", t - 2, i)
                                wait_filled(old, it)
                            wait_filled(step, it)
                            if i < 4:
                                n = 4 * t + i
                                if n >= 2:
                                    act.wait_ge(ss_ready, it * NQ + n - 1)
                                nc.scalar.activation(sq[:, n % 2, :], ps.ap(step), ACT.Square).then_inc(sq_ready, 1)
                            dst = raw[:, (4 * t + i) % 8, :] if i < 4 else v[:, t, (i - 4) * HALF:(i - 3) * HALF]
                            nc.scalar.copy(dst, ps.ap(step)).then_inc(ps.sem_drained(step), 1)
                        elif kind == "tr":
                            t = step[1]
                            for i in range(4):
                                key = step + (i,)
                                wait_filled(key, it)
                                src = ps.ap(key).rearrange("p (n q) -> p n q", q=P)
                                n = 4 * (i % 2)
                                dst = qT[:, n:n + 4, :] if i < 2 else kT[:, n:n + 4, (t + 1) * P:(t + 2) * P]
                                nc.scalar.copy(dst, src).then_inc(ps.sem_drained(key), 1)
                        elif kind == "e":
                            t, g = step[1:]
                            act.wait_ge(nb_ready, it * NG + t * G + g + 1)
                            for n in range(4):
                                h = 4 * g + n
                                pr = prob[:, (4 * (t * G + g) + n) % 12, unseen(t):]
                                ex = nc.scalar.activation(pr, pr, ACT.Exp, bias=nb[:, t % 2, h:h + 1],
                                                          scale=rq8[:, t, h:h + 1],
                                                          accum_out=sums[:, t % 2, h:h + 1])
                            ex.then_inc(exp_ready, 1)
                        elif kind == "pt":
                            evacuate_probs(act, nc.scalar.copy, ps, step, it, 0)
                        elif kind == "pv":
                            t, g = step[1:]
                            if g % 2 == 1:
                                key = ("o", t, g // 2)
                                if t >= 1:
                                    wait_filled(("wo", t - 1), it)
                                wait_filled(key, it)
                                nc.scalar.copy(oT[:, 4 * (g // 2):4 * (g // 2) + 4, :],
                                               ps.ap(key).rearrange("p (n q) -> p n q", q=P)
                                               ).then_inc(ps.sem_drained(key), 1)
                        elif kind == "xs":
                            act.wait_ge(x1_ready, mlp_of(it) + 1)
                            act.dma_start(xs[1:P, :, :], x1[0:P - 1, :, P:D]).then_inc(xs_ready, 16)
                            act.dma_start(xs[0:1, 1:TB, :], x1[P - 1:P, 0:TB - 1, P:D]).then_inc(xs_ready, 16)
                        elif kind == "xnt":
                            act.wait_ge(ffn_weights, mlp_of(it) + 1)
                            for c in range(KC):
                                key = step + (c,)
                                wait_filled(key, it)
                                nc.scalar.activation(xnT[:, c, :], ps.ap(key), ACT.Identity, bias=ln_b[:, c:c + 1],
                                                     scale=ln_g[:, c:c + 1]).then_inc(ps.sem_drained(key), 1)
                        elif kind == "f1":
                            ch = step[1]
                            m = P if ch < HC - 1 else HREM
                            key = step + (1,)
                            wait_filled(key, it)
                            nc.scalar.activation(hT[0:m, ch, :], ps.ap(key)[0:m], ACT.Gelu,
                                                 bias=b1g[0:m, ch:ch + 1]).then_inc(ps.sem_drained(key), 1)

        @block.vector
        def _(dve):
            def wait_filled(key, it):
                dve.wait_ge(ps.sem_filled(key), ps.count(key, it))

            def wait_drained(key, it):
                dve.wait_ge(ps.sem_drained(key), ps.count(key, it))

            def evac(out, in_):
                return nc.vector.tensor_copy(out, in_)

            nc.vector.memset(kT[:, :, 0:P], 0.0)
            nc.vector.memset(prob[:, :, 0:P - WINDOW], 0.0)
            nc.vector.memset(xsT[:, 1, 0:1], 0.0)
            nc.vector.memset(xs[0:1, 0, :], 0.0)
            nc.vector.memset(half_pow[:], -0.5).then_inc(pads, 1)
            dve.wait_ge(consts, 32)
            dve.wait_ge(saved, 16)
            for steps, ps, first, end in phases:
                with each(dve, first, end) as it:
                    for step in steps:
                        kind = step[0]
                        if kind == "qkv":
                            t, i = step[1:]
                            if i >= 4:
                                continue
                            if t == i == 0:
                                dve.wait_ge(tab_ready, it + 1)
                            n = 4 * t + i
                            wait_drained(step, it)
                            if n >= 2:
                                dve.wait_ge(rope_done, it * NQ + n - 1)
                            q = raw[:, n % 8, :]
                            kindq = 2 * (i // 2)
                            cos = tab[:, t:t + 1, kindq, :].broadcast_to([P, 8, DH])
                            sin = tab[:, t:t + 1, kindq + 1, :].broadcast_to([P, 8, DH])
                            nc.vector.tensor_tensor(heads(rot[:, n % 2, 0, :]), heads(q), cos, ALU.mult)
                            swapped = q.rearrange("p (h two d) -> p h two d", two=2, d=DH // 2)[:, :, ::-1, :]
                            nc.vector.tensor_tensor(
                                rot[:, n % 2, 1, :].rearrange("p (h two d) -> p h two d", two=2, d=DH // 2),
                                swapped, sin.rearrange("p h (two d) -> p h two d", two=2),
                                ALU.mult).then_inc(rot_ready, 1)
                            dve.wait_ge(sq_ready, it * NQ + n + 1)
                            nc.vector.tensor_reduce(ss[:, t % 2, 8 * i:8 * i + 8], heads(sq[:, n % 2, :]), AX.X,
                                                    ALU.add).then_inc(ss_ready, 1)
                        elif kind == "pow":
                            t = step[1]
                            dve.wait_ge(ss_ready, it * NQ + 4 * t + 4)
                            nc.vector.tensor_scalar(ss[:, t % 2, :], ss[:, t % 2, :], 1e-24, None,
                                                    ALU.max).then_inc(ssm_ready, 1)
                        elif kind == "norm":
                            t = step[1]
                            dve.wait_ge(rn_ready, it * TB + t + 1)
                            nc.vector.tensor_scalar(rq8[:, t, :], rn[:, t % 2, 0:H], QK_SCALE, None, ALU.mult)
                            for i in range(2, 4):
                                s = 4 * t + i
                                dve.wait_ge(rope_done, it * NQ + s + 1)
                                k = heads(raw[:, s % 8, :])
                                norm = rn[:, t % 2, 8 * i:8 * i + 8].unsqueeze(2).broadcast_to([P, 8, DH])
                                nc.vector.tensor_tensor(k, k, norm, ALU.mult).then_inc(qk_ready, 1)
                        elif kind == "s":
                            t, g = step[1:]
                            n = t * G + g
                            if n >= 3:
                                old = ("pt", (n - 3) // G, (n - 3) % G)
                                for i in range(2):
                                    wait_filled(old + (i,), it)
                            for i in range(2):
                                key = step + (i,)
                                wait_filled(key, it)
                                dve.sem_inc(passed, 1)
                                for j in range(2):
                                    h = 4 * g + 2 * j + i
                                    red = nc.vector.tensor_tensor_reduce(
                                        prob[:, (4 * n + 2 * j + i) % 12, unseen(t):],
                                        ps.ap(key)[:, j * 2 * P + unseen(t):(j + 1) * 2 * P],
                                        band[:, min(t, 1), unseen(t):], 1.0, LOWEST, ALU.add, ALU.max,
                                        mx[:, t % 2, h:h + 1])
                                red.then_inc(ps.sem_drained(key), 1)
                            for i in range(2):
                                wait_drained(step + (i,), it)
                            nc.vector.scalar_tensor_tensor(
                                out=nb[:, t % 2, 4 * g:4 * g + 4], in0=mx[:, t % 2, 4 * g:4 * g + 4], scalar=-1.0,
                                in1=rq8[:, t, 4 * g:4 * g + 4], op0=ALU.mult, op1=ALU.mult).then_inc(nb_ready, 1)
                        elif kind == "pt":
                            evacuate_probs(dve, evac, ps, step, it, 1)
                        elif kind == "r":
                            t, g = step[1:]
                            dve.wait_ge(exp_ready, it * NG + t * G + g + 1)
                            nc.vector.reciprocal(rs[:, t % 2, 4 * g:4 * g + 4],
                                                 sums[:, t % 2, 4 * g:4 * g + 4]).then_inc(rs_ready, 1)
                            dve.wait_ge(rs_ready, it * NG + t * G + g + 1)
                            for n in range(4):
                                h = 4 * g + n
                                pr = prob[:, (4 * (t * G + g) + n) % 12, unseen(t):]
                                ins = nc.vector.tensor_scalar(pr, pr, rs[:, t % 2, h:h + 1], None, ALU.mult)
                            ins.then_inc(prob_ready, 1)
                        elif kind == "wo":
                            t = step[1]
                            if t == 0 and first > 0:
                                dve.wait_ge(x1b_ready, mlp_of(it) + 1)
                            wait_filled(step, it)
                            nc.vector.tensor_tensor(x1[:, t, :], ps.ap(step)[:, 0:D],
                                                    x_all[:, it % NB * TB + t, :],
                                                    ALU.add).then_inc(ps.sem_drained(step), 1)
                            if t == TB - 1:
                                wait_drained(step, it)
                                dve.sem_inc(x1_ready, 1)
                        elif kind == "ln":
                            f = mlp_of(it)
                            dve.wait_ge(xs_ready, (f + 1) * 32)
                            for t in range(TB):
                                nc.vector.bn_stats(stat[:, t, 0:6], x1[:, t, 0:P])
                                ins = nc.vector.bn_stats(stat[:, t, 6:12], xs[:, t, :])
                            ins.then_inc(stat_ready, 1)
                            dve.wait_ge(stat_ready, f + 1)
                            dve.sem_inc(passed, 1)
                            for t in range(TB):
                                agg = nc.vector.bn_aggr(mv[:, t, :], stat[:, t, :])
                            agg.then_inc(mv_ready, 1)
                            dve.wait_ge(mv_ready, f + 1)
                            nc.vector.tensor_scalar(rstd[:, 0, :], mv[:, :, 1], LN_EPS, None,
                                                    ALU.add).then_inc(eps_ready, 1)
                        elif kind == "xn":
                            f = mlp_of(it)
                            dve.wait_ge(rstd_ready, f + 1)
                            for t in range(TB):
                                for c, src in enumerate((x1[:, t, 0:P], xs[:, t, :])):
                                    ins = nc.vector.tensor_scalar(xn[:, t, c * P:(c + 1) * P], src, mv[:, t, 0:1],
                                                                  rstd[:, 1, t:t + 1], ALU.subtract, ALU.mult)
                            ins.then_inc(xn_ready, 1)
                        elif kind == "f1":
                            ch = step[1]
                            m = P if ch < HC - 1 else HREM
                            f = mlp_of(it)
                            if ch == 0:
                                dve.wait_ge(ffn_weights, f + 1)
                            wait_filled(step + (0,), it)
                            wait_drained(step + (1,), it)
                            nc.vector.scalar_tensor_tensor(
                                out=hT[0:m, ch, :], in0=ps.ap(step + (0,))[0:m], scalar=b1a[0:m, ch:ch + 1],
                                in1=hT[0:m, ch, :], op0=ALU.add, op1=ALU.mult).then_inc(h_ready, 1)
                            dve.wait_ge(h_ready, f * HC + ch + 1)
                            dve.sem_inc(ps.sem_drained(step + (0,)), 1)
                        elif kind == "f2":
                            t = step[1]
                            if t == 0:
                                dve.wait_ge(x1b_ready, mlp_of(it) + 1)
                            wait_filled(step, it)
                            nc.vector.tensor_tensor(x_all[:, mlp_of(it) % NB * TB + t, :], ps.ap(step)[:, 0:D],
                                                    xn[:, t, :], ALU.add).then_inc(ps.sem_drained(step), 1)
                            if t == TB - 1:
                                wait_drained(step, it)
                                dve.sem_inc(x_ready, 1)

        @block.gpsimd
        def _(pool):
            pool.wait_ge(pads, 1)
            pool.wait_ge(consts, 32)

            def copy_x(it):
                nc.gpsimd.tensor_copy(xin[:], x_all[:, bass.ds(it % NB * TB, TB), :]).then_inc(xin_ready, 1)

            copy_x(0)
            pool.sem_inc(x_ready, NB - 1)
            for steps, ps, first, end in phases:
                with each(pool, first, end) as it:
                    for step in steps:
                        kind = step[0]
                        if kind == "xin":
                            pool.wait_ge(x_ready, it + 1)
                            copy_x(it + 1)
                        elif kind == "tab":
                            pool.wait_ge(attn_weights, it + 2)
                            for i in range(4):
                                ins = nc.gpsimd.tensor_tensor(tab[:, :, i, :], rope[:, :, i, :],
                                                              qks[:, i:i + 1, :].broadcast_to([P, TB, DH]), ALU.mult)
                            ins.then_inc(tab_ready, 1)
                        elif kind == "qkv":
                            t, i = step[1:]
                            if i >= 4:
                                continue
                            n = 4 * t + i
                            q = raw[:, n % 8, :]
                            pool.wait_ge(rot_ready, it * NQ + n + 1)
                            nc.gpsimd.tensor_tensor(q, rot[:, n % 2, 0, :], rot[:, n % 2, 1, :],
                                                    ALU.add).then_inc(rope_done, 1)
                        elif kind == "pow":
                            t = step[1]
                            pool.wait_ge(ssm_ready, it * TB + t + 1)
                            nc.gpsimd.tensor_tensor(rn[:, t % 2, :], ss[:, t % 2, :], half_pow[:],
                                                    ALU.pow).then_inc(rn_ready, 1)
                        elif kind == "ln":
                            f = mlp_of(it)
                            pool.wait_ge(eps_ready, f + 1)
                            nc.gpsimd.tensor_tensor(rstd[:, 1, :], rstd[:, 0, :], half_pow[:, 0:TB],
                                                    ALU.pow).then_inc(rstd_ready, 1)
                        elif kind == "xnt":
                            for c in range(KC):
                                key = step + (c,)
                                pool.wait_ge(ps.sem_filled(key), ps.count(key, it))
                            pool.wait_ge(ffn_weights, mlp_of(it) + 1)
                            nc.gpsimd.tensor_tensor(xn[:], x1[:], b2[:].unsqueeze(1).broadcast_to([P, TB, D]),
                                                    ALU.add).then_inc(x1b_ready, 1)


class Norm:

    def __init__(self, nc, shared, ctx, stage, y):
        self.nc, self.y, self.x_all, self.half_pow = nc, y, shared["x"], shared["half_pow"]
        self.tiles = y.shape[1]

        def sb(name, shape):
            return ctx.enter_context(nc.sbuf_tensor(f"{stage}_{name}", shape, F32))

        def sem(name):
            return shared["sems"].enter_context(nc.semaphore(f"{stage}_{name}"))

        self.stat = sb("stat", [P, self.tiles, 6])
        self.mv = sb("mv", [P, self.tiles, 2])
        self.rstd = sb("rstd", [P, 2, self.tiles])
        self.stat_ready = sem("stat_ready")
        self.mv_ready = sem("mv_ready")
        self.eps_ready = sem("eps_ready")
        self.rstd_ready = sem("rstd_ready")
        self.x_ready = sem("x_ready")
        self.passed = sem("passed")

    def vector(self, dve, it):
        nc, n = self.nc, self.tiles
        for t in range(n):
            ins = nc.vector.bn_stats(self.stat[:, t, :], self.y[:, t, :])
        ins.then_inc(self.stat_ready, 1)
        dve.wait_ge(self.stat_ready, it + 1)
        dve.sem_inc(self.passed, 1)
        for t in range(n):
            ins = nc.vector.bn_aggr(self.mv[:, t, :], self.stat[:, t, :])
        ins.then_inc(self.mv_ready, 1)
        dve.wait_ge(self.mv_ready, it + 1)
        nc.vector.tensor_scalar(self.rstd[:, 0, :], self.mv[:, :, 1], LN_EPS, None, ALU.add).then_inc(self.eps_ready, 1)
        dve.wait_ge(self.rstd_ready, it + 1)
        for t in range(n):
            ins = nc.vector.tensor_scalar(self.x_all[:, it * n + t, :], self.y[:, t, :], self.mv[:, t, 0:1],
                                          self.rstd[:, 1, t:t + 1], ALU.subtract, ALU.mult)
        ins.then_inc(self.x_ready, 1)

    def gpsimd(self, pool, it):
        pool.wait_ge(self.eps_ready, it + 1)
        self.nc.gpsimd.tensor_tensor(self.rstd[:, 1, :], self.rstd[:, 0, :], self.half_pow[:, 0:self.tiles],
                                     ALU.pow).then_inc(self.rstd_ready, 1)


def stage_wide_attention(nc, shared, stage, w, rope, cross):
    ident, x_all = shared["ident"], shared["x"]
    D = x_all.shape[2]
    TB = 4
    NB = x_all.shape[1] // TB
    S = TB * P
    KC = D // P
    scale = float(D) ** -0.5 if cross else 128.0 ** -0.5

    with ExitStack() as ctx:
        def sb(name, shape, dt=F32):
            return ctx.enter_context(nc.sbuf_tensor(f"{stage}_{name}", shape, dt))

        def sem(name):
            return shared["sems"].enter_context(nc.semaphore(f"{stage}_{name}"))

        ps = Psum(shared)
        xin = sb("xin", [P, TB, D])
        xb = sb("xb", [P, TB, D])
        xT = sb("xT", [P, KC, S])
        qT = sb("qT", [P, KC, S])
        kT = sb("kT", [P, KC, S])
        v = sb("v", [P, TB, D])
        prob = sb("prob", [P, 2, S])
        pT = sb("pT", [P, 2, S])
        mx = sb("mx", [P, TB])
        nb = sb("nb", [P, TB])
        sums = sb("sums", [P, TB])
        rs = sb("rs", [P, TB])
        y = sb("y", [P, TB, D])
        norm = Norm(nc, shared, ctx, stage, y)
        if cross:
            srcT = sb("srcT", [P, KC, S])
            mask_int = sb("mask_int", [P, S], mybir.dt.int32)
            keep = sb("keep", [P, S])
            gone = sb("gone", [P, S])
            add_mask = sb("add_mask", [P, TB, S])
        else:
            srcT = xT
        src_ready = sem("src_ready")
        mask_landed = sem("mask_landed")
        keep_ready = sem("keep_ready")
        gone_ready = sem("gone_ready")
        add_mask_ready = sem("add_mask_ready")
        weights_ready = sem("weights_ready")
        xin_ready = sem("xin_ready")
        xb_ready = sem("xb_ready")
        mx_ready = sem("mx_ready")
        nb_ready = sem("nb_ready")
        exp_ready = sem("exp_ready")
        rs_ready = sem("rs_ready")
        y_ready = sem("y_ready")

        steps = [("xin",), ("xt",), ("q",), ("k",), ("v",)]
        for t in range(TB):
            steps.append(("s", t))
            if t >= 1:
                steps.append(("pt", t - 1))
            if t >= 1:
                steps.append(("pv", t - 1))
        steps += [("pt", TB - 1), ("pv", TB - 1), ("ln",)]
        banks = {"xt": (0, 1), "q": (2, 3), "k": (0, 1), "v": (2, 3)}
        for step in steps:
            kind = step[0]
            if kind in banks:
                for i in range(2):
                    ps.fill(step + (i,), banks[kind][i])
            elif kind == "s":
                ps.fill(step, 4 + step[1] % 2)
            elif kind == "pt":
                ps.fill(step, 0 + step[1] % 2)
            elif kind == "pv":
                ps.fill(step, 6 + step[1] % 2)

        ps.finish(shared, NB)

        block = ctx.enter_context(nc.Block())

        @block.sync
        def _(sp):
            if not cross:
                return
            with sp.Fori(0, NB) as it:
                key = ("s", 2)
                sp.wait_ge(ps.sem_filled(key), ps.last_time(key, it))
                sp.dma_start(srcT[:], w["ctxT"][it].rearrange("(c p) s -> p c s", p=P)).then_inc(src_ready, 16)
                sp.dma_start(mask_int[:], w["mask"][it].partition_broadcast(P)).then_inc(mask_landed, 16)

        @block.tensor
        def _(pe):
            def empty(key, it):
                pe.wait_ge(ps.sem_drained(key), ps.before(key, it))

            def drained(key, it):
                pe.wait_ge(ps.sem_drained(key), ps.count(key, it))

            pe.wait_ge(w["landed"], w["loads"])
            if rope is not None:
                pe.wait_ge(weights_ready, 1)
            with pe.Fori(0, NB) as it:
                for step in steps:
                    kind = step[0]
                    if kind == "xt":
                        pe.wait_ge(xin_ready, it + 1)
                        for c in range(KC):
                            key = step + (c,)
                            empty(key, it)
                            for t in range(TB):
                                mm = nc.tensor.transpose(ps.ap(key)[:, t * P:(t + 1) * P],
                                                         xin[:, t, c * P:(c + 1) * P], ident[:])
                            mm.then_inc(ps.sem_filled(key), 1)
                    elif kind in ("q", "k"):
                        if kind == "q":
                            for c in range(KC):
                                drained(("xt", c), it)
                        elif cross:
                            pe.wait_ge(src_ready, (it + 1) * 16)
                        for e in range(KC):
                            key = step + (e,)
                            empty(key, it)
                            for c in range(KC):
                                mm = nc.tensor.matmul(ps.ap(key), w["W" + kind][:, c, e * P:(e + 1) * P],
                                                      (xT if kind == "q" else srcT)[:, c, :],
                                                      start=c == 0, stop=c == KC - 1)
                            mm.then_inc(ps.sem_filled(key), 1)
                    elif kind == "v":
                        for i in range(2):
                            key = step + (i,)
                            empty(key, it)
                            for n in range(2):
                                t = 2 * i + n
                                for c in range(KC):
                                    mm = nc.tensor.matmul(ps.ap(key)[:, n * D:(n + 1) * D],
                                                          srcT[:, c, t * P:(t + 1) * P], w["Wv"][:, c, :],
                                                          start=c == 0, stop=c == KC - 1)
                            mm.then_inc(ps.sem_filled(key), 1)
                    elif kind == "s":
                        t = step[1]
                        if t == 0:
                            for e in range(KC):
                                drained(("q", e), it)
                                drained(("k", e), it)
                        empty(step, it)
                        for e in range(KC):
                            mm = nc.tensor.matmul(ps.ap(step), qT[:, e, t * P:(t + 1) * P], kT[:, e, :],
                                                  start=e == 0, stop=e == KC - 1)
                        mm.then_inc(ps.sem_filled(step), 1)
                    elif kind == "pt":
                        t = step[1]
                        pe.wait_ge(exp_ready, it * TB + t + 1)
                        empty(step, it)
                        for n in range(TB):
                            mm = nc.tensor.transpose(ps.ap(step)[:, n * P:(n + 1) * P],
                                                     prob[:, t % 2, n * P:(n + 1) * P], ident[:])
                        mm.then_inc(ps.sem_filled(step), 1)
                    elif kind == "pv":
                        t = step[1]
                        if t == 0:
                            for i in range(2):
                                drained(("v", i), it)
                        drained(("pt", t), it)
                        empty(step, it)
                        for n in range(TB):
                            mm = nc.tensor.matmul(ps.ap(step)[:, 0:D], pT[:, t % 2, n * P:(n + 1) * P], v[:, n, :],
                                                  start=n == 0, stop=n == TB - 1)
                        mm.then_inc(ps.sem_filled(step), 1)

        @block.scalar
        def _(act):
            def filled(key, it):
                act.wait_ge(ps.sem_filled(key), ps.count(key, it))

            with act.Fori(0, NB) as it:
                for step in steps:
                    kind = step[0]
                    if kind == "xin":
                        key = ("pv", 0)
                        act.wait_ge(ps.sem_drained(key), ps.last_time(key, it))
                        nc.scalar.copy(xin[:], x_all[:, bass.ds(it * TB, TB), :]).then_inc(xin_ready, 1)
                    elif kind == "xt":
                        for c in range(KC):
                            filled(step + (c,), it)
                            nc.scalar.copy(xT[:, c, :], ps.ap(step + (c,))).then_inc(ps.sem_drained(step + (c,)), 1)
                    elif kind == "v":
                        for i in range(2):
                            filled(step + (i,), it)
                            nc.scalar.copy(v[:, 2 * i:2 * i + 2, :], ps.ap(step + (i,)).rearrange(
                                "p (t d) -> p t d", d=D)).then_inc(ps.sem_drained(step + (i,)), 1)
                    elif kind == "s":
                        t = step[1]
                        act.wait_ge(nb_ready, it * TB + t + 1)
                        if t >= 2:
                            filled(("pt", t - 2), it)
                        if cross:
                            nc.scalar.activation(prob[:, t % 2, :], prob[:, t % 2, :], ACT.Exp, bias=nb[:, t:t + 1],
                                                 accum_out=sums[:, t:t + 1]).then_inc(exp_ready, 1)
                        else:
                            nc.scalar.activation(prob[:, t % 2, :], ps.ap(step), ACT.Exp, bias=nb[:, t:t + 1],
                                                 scale=scale, accum_out=sums[:, t:t + 1]).then_inc(exp_ready, 1)
                            act.wait_ge(exp_ready, it * TB + t + 1)
                            act.sem_inc(ps.sem_drained(step), 1)
                    elif kind == "pt":
                        t = step[1]
                        if t >= 2:
                            filled(("pv", t - 2), it)
                        filled(step, it)
                        nc.scalar.copy(pT[:, t % 2, :], ps.ap(step)).then_inc(ps.sem_drained(step), 1)

        @block.vector
        def _(dve):
            def filled(key, it):
                dve.wait_ge(ps.sem_filled(key), ps.count(key, it))

            dve.wait_ge(w["landed"], w["loads"])
            if rope is not None:
                for name in ("Wq", "Wk"):
                    plain = w[name + "_plain"][:].rearrange("p c (e two) -> p c e two", two=2)
                    out = w[name][:].rearrange("p c (e two) -> p c e two", two=2)
                    nc.vector.tensor_tensor(out[:, :, :, 0], plain[:, :, :, 0], plain[:, :, :, 1], ALU.subtract)
                    nc.vector.tensor_tensor(out[:, :, :, 1], plain[:, :, :, 1], plain[:, :, :, 0], ALU.add)
                for name in ("bq", "bk"):
                    swap = w[name + "_swap"]
                    ins = nc.vector.tensor_tensor(swap[:], swap[:], w["pair_sign"][:], ALU.mult)
                ins.then_inc(weights_ready, 1)
                dve.wait_ge(weights_ready, 1)
                for name in ("bq", "bk"):
                    ins = nc.vector.tensor_tensor(w[name][:], w[name][:], w[name + "_swap"][:], ALU.add)
                ins.then_inc(weights_ready, 1)
                dve.wait_ge(weights_ready, 2)
            with dve.Fori(0, NB) as it:
                for step in steps:
                    kind = step[0]
                    if kind in ("q", "k"):
                        dst = qT if kind == "q" else kT
                        for e in range(KC):
                            key = step + (e,)
                            filled(key, it)
                            bias = w["b" + kind][:, e:e + 1]
                            if rope is not None:
                                ins = nc.vector.scalar_tensor_tensor(out=dst[:, e, :], in0=ps.ap(key), scalar=bias,
                                                                     in1=rope[:, e, :], op0=ALU.add, op1=ALU.mult)
                            else:
                                ins = nc.vector.tensor_scalar(dst[:, e, :], ps.ap(key), bias, None, ALU.add)
                            ins.then_inc(ps.sem_drained(key), 1)
                        if kind == "q" and cross:
                            dve.wait_ge(mask_landed, (it + 1) * 16)
                            nc.vector.tensor_scalar(keep[:], mask_int[:], 0.0, None,
                                                    ALU.not_equal).then_inc(keep_ready, 1)
                            dve.wait_ge(keep_ready, it + 1)
                            nc.vector.tensor_scalar(gone[:], keep[:], 1e10, -1e10, ALU.mult,
                                                    ALU.add).then_inc(gone_ready, 1)
                            dve.wait_ge(gone_ready, it + 1)
                            nc.vector.tensor_tensor(add_mask[:], w["causal"][:],
                                                    gone[:].unsqueeze(1).broadcast_to([P, TB, S]),
                                                    ALU.add).then_inc(add_mask_ready, 1)
                            dve.wait_ge(add_mask_ready, it + 1)
                    elif kind == "s":
                        t = step[1]
                        filled(step, it)
                        if cross:
                            if t >= 2:
                                filled(("pt", t - 2), it)
                            nc.vector.scalar_tensor_tensor(out=prob[:, t % 2, :], in0=ps.ap(step), scalar=scale,
                                                           in1=keep[:], op0=ALU.mult,
                                                           op1=ALU.mult).then_inc(ps.sem_drained(step), 1)
                            dve.wait_ge(ps.sem_drained(step), ps.count(step, it))
                            dve.sem_inc(norm.passed, 1)
                            nc.vector.tensor_tensor_reduce(prob[:, t % 2, :], prob[:, t % 2, :], add_mask[:, t, :], 1.0,
                                                           LOWEST, ALU.add, ALU.max,
                                                           mx[:, t:t + 1]).then_inc(mx_ready, 1)
                        else:
                            nc.vector.reduce_max(mx[:, t:t + 1], ps.ap(step), AX.X).then_inc(mx_ready, 1)
                        dve.wait_ge(mx_ready, it * TB + t + 1)
                        nc.vector.tensor_scalar(nb[:, t:t + 1], mx[:, t:t + 1], -1.0 if cross else -scale, None,
                                                ALU.mult).then_inc(nb_ready, 1)
                    elif kind == "pv":
                        t = step[1]
                        dve.wait_ge(exp_ready, it * TB + t + 1)
                        nc.vector.reciprocal(rs[:, t:t + 1], sums[:, t:t + 1]).then_inc(rs_ready, 1)
                        if t == 0:
                            dve.wait_ge(xb_ready, it + 1)
                        dve.wait_ge(rs_ready, it * TB + t + 1)
                        filled(step, it)
                        nc.vector.scalar_tensor_tensor(out=y[:, t, :], in0=ps.ap(step)[:, 0:D], scalar=rs[:, t:t + 1],
                                                       in1=xb[:, t, :], op0=ALU.mult, op1=ALU.add).then_inc(y_ready, 1)
                        dve.wait_ge(y_ready, it * TB + t + 1)
                        dve.sem_inc(ps.sem_drained(step), 1)
                    elif kind == "ln":
                        norm.vector(dve, it)

        @block.gpsimd
        def _(pool):
            pool.wait_ge(w["landed"], w["loads"])
            with pool.Fori(0, NB) as it:
                key = ("pv", TB - 1)
                pool.wait_ge(ps.sem_drained(key), ps.last_time(key, it))
                pool.wait_ge(xin_ready, it + 1)
                for c in range(KC):
                    key = ("xt", c)
                    pool.wait_ge(ps.sem_filled(key), ps.count(key, it))
                nc.gpsimd.tensor_tensor(xb[:], xin[:], w["bv"][:].unsqueeze(1).broadcast_to([P, TB, D]),
                                        ALU.add).then_inc(xb_ready, 1)
                norm.gpsimd(pool, it)


def stage_moe(nc, shared, w):
    ident, x_all = shared["ident"], shared["x"]
    D = x_all.shape[2]
    TB = 4
    NB = x_all.shape[1] // TB
    S = TB * P
    KC = D // P
    E = w["Wr"].shape[2]
    HID = w["W1"].shape[3]
    HC = HID // P
    TOP_K = 2

    with ExitStack() as ctx:
        def sb(name, shape):
            return ctx.enter_context(nc.sbuf_tensor(f"m_{name}", shape, F32))

        def sem(name):
            return shared["sems"].enter_context(nc.semaphore(f"m_{name}"))

        ps = Psum(shared)
        xin = sb("xin", [P, TB, D])
        xT = sb("xT", [P, KC, S])
        logits = sb("logits", [P, TB, E])
        above = sb("above", [P, TB, E, E])
        equal = sb("equal", [P, TB, E, E])
        rank = sb("rank", [P, TB, E])
        top = sb("top", [P, TB])
        gates = sb("gates", [P, TB, E])
        total = sb("total", [P, TB])
        gT = sb("gT", [E, S])
        hT = sb("hT", [P, 2, HC, S])
        acc = sb("acc", [P, TB, D])
        norm = Norm(nc, shared, ctx, "m", acc)
        xin_ready = sem("xin_ready")
        routed = sem("routed")
        centred_ready = sem("centred_ready")
        exp_ready = sem("exp_ready")
        gates_ready = sem("gates_ready")
        acc_ready = sem("acc_ready")
        CHAIN = 10

        steps = [("xin",), ("xt",), ("route",), ("h", 0, 0), ("h", 0, 1), ("h", 0, 2), ("gt",), ("h", 0, 3)]
        steps += [("b2", t) for t in range(TB)]
        for e in range(1, E + 1):
            for c in range(HC):
                if e < E:
                    steps.append(("h", e, c))
                steps.append(("o", e - 1, c))
        steps.append(("ln",))
        ring = {"h": 0, "o": 0}
        for step in steps:
            kind = step[0]
            if kind == "xt":
                ps.fill(step + (0,), 0)
                ps.fill(step + (1,), 1)
            elif kind == "route":
                ps.fill(step, 2)
            elif kind == "gt":
                ps.fill(step, 3)
            elif kind == "h":
                ps.fill(step, (4, 5, 0, 1)[ring["h"] % 4])
                ring["h"] += 1
            elif kind in ("o", "b2"):
                ps.fill(step, (6, 7, 2, 3)[ring["o"] % 4])
                ring["o"] += 1

        ps.finish(shared, NB)

        block = ctx.enter_context(nc.Block())

        @block.tensor
        def _(pe):
            def empty(key, it):
                pe.wait_ge(ps.sem_drained(key), ps.before(key, it))

            def drained(key, it):
                pe.wait_ge(ps.sem_drained(key), ps.count(key, it))

            pe.wait_ge(w["landed"], w["loads"])
            with pe.Fori(0, NB) as it:
                for step in steps:
                    kind = step[0]
                    if kind == "xt":
                        pe.wait_ge(xin_ready, it + 1)
                        for c in range(KC):
                            key = step + (c,)
                            empty(key, it)
                            for t in range(TB):
                                mm = nc.tensor.transpose(ps.ap(key)[:, t * P:(t + 1) * P],
                                                         xin[:, t, c * P:(c + 1) * P], ident[:])
                            mm.then_inc(ps.sem_filled(key), 1)
                    elif kind == "route":
                        for c in range(KC):
                            drained(("xt", c), it)
                        empty(step, it)
                        for t in range(TB):
                            for c in range(KC):
                                mm = nc.tensor.matmul(ps.ap(step)[:, t * E:(t + 1) * E],
                                                      xT[:, c, t * P:(t + 1) * P], w["Wr"][:, c, :],
                                                      start=c == 0, stop=c == KC - 1)
                        mm.then_inc(ps.sem_filled(step), 1)
                    elif kind == "gt":
                        pe.wait_ge(gates_ready, it + 1)
                        empty(step, it)
                        for t in range(TB):
                            mm = nc.tensor.transpose(ps.ap(step)[0:E, t * P:(t + 1) * P], gates[:, t, :], ident[:])
                        mm.then_inc(ps.sem_filled(step), 1)
                    elif kind == "b2":
                        t = step[1]
                        drained(("gt",), it)
                        empty(step, it)
                        nc.tensor.matmul(ps.ap(step)[:, 0:D], gT[:, t * P:(t + 1) * P], w["b2"][:], start=True,
                                         stop=True).then_inc(ps.sem_filled(step), 1)
                    elif kind == "h":
                        e, ch = step[1:]
                        empty(step, it)
                        for c in range(KC):
                            mm = nc.tensor.matmul(ps.ap(step), w["W1"][:, e, c, ch * P:(ch + 1) * P], xT[:, c, :],
                                                  start=c == 0, stop=c == KC - 1)
                        mm.then_inc(ps.sem_filled(step), 1)
                    elif kind == "o":
                        e, t = step[1:]
                        if t == 0:
                            for c in range(HC):
                                drained(("h", e, c), it)
                        empty(step, it)
                        for c in range(HC):
                            mm = nc.tensor.matmul(ps.ap(step)[:, 0:D], hT[:, e % 2, c, t * P:(t + 1) * P],
                                                  w["W2"][:, e, c, :], start=c == 0, stop=c == HC - 1)
                        mm.then_inc(ps.sem_filled(step), 1)

        @block.scalar
        def _(act):
            def filled(key, it):
                act.wait_ge(ps.sem_filled(key), ps.count(key, it))

            act.wait_ge(w["landed"], w["loads"])
            with act.Fori(0, NB) as it:
                for step in steps:
                    kind = step[0]
                    if kind == "xin":
                        key = ("b2", TB - 1)
                        act.wait_ge(ps.sem_drained(key), ps.last_time(key, it))
                        nc.scalar.copy(xin[:], x_all[:, bass.ds(it * TB, TB), :]).then_inc(xin_ready, 1)
                    elif kind == "xt":
                        for c in range(KC):
                            filled(step + (c,), it)
                            nc.scalar.copy(xT[:, c, :], ps.ap(step + (c,))).then_inc(ps.sem_drained(step + (c,)), 1)
                    elif kind == "h":
                        e, ch = step[1:]
                        if e >= 2:
                            filled(("o", e - 2, TB - 1), it)
                        filled(step, it)
                        nc.scalar.activation(hT[:, e % 2, ch, :], ps.ap(step), ACT.Relu,
                                             bias=w["b1"][:, e, ch:ch + 1]).then_inc(ps.sem_drained(step), 1)
                        if (e, ch) == (0, 0):
                            act.wait_ge(centred_ready, it + 1)
                            nc.scalar.activation(gates[:], gates[:], ACT.Exp).then_inc(exp_ready, 1)
                    elif kind == "gt":
                        filled(step, it)
                        nc.scalar.copy(gT[:], ps.ap(step)[0:E, :]).then_inc(ps.sem_drained(step), 1)

        @block.vector
        def _(dve):
            def filled(key, it):
                dve.wait_ge(ps.sem_filled(key), ps.count(key, it))

            dve.wait_ge(w["landed"], w["loads"])
            with dve.Fori(0, NB) as it:
                for step in steps:
                    kind = step[0]
                    if kind == "route":
                        done = [0]

                        def chained(ins):
                            done[0] += 1
                            ins.then_inc(routed, 1)
                            dve.wait_ge(routed, it * CHAIN + done[0])

                        filled(step, it)
                        nc.vector.tensor_tensor(logits[:], ps.ap(step)[:, 0:TB * E].rearrange(
                            "p (t e) -> p t e", e=E), w["br"][:].unsqueeze(1).broadcast_to([P, TB, E]),
                            ALU.add).then_inc(ps.sem_drained(step), 1)
                        dve.wait_ge(ps.sem_drained(step), ps.count(step, it))
                        mine = logits[:].unsqueeze(3).broadcast_to([P, TB, E, E])
                        other = logits[:].unsqueeze(2).broadcast_to([P, TB, E, E])
                        for t in range(TB):
                            nc.vector.tensor_tensor(above[:, t], other[:, t], mine[:, t], ALU.is_gt)
                            ins = nc.vector.tensor_tensor(equal[:, t], other[:, t], mine[:, t], ALU.is_equal)
                        chained(ins)
                        chained(nc.vector.tensor_tensor(equal[:], equal[:],
                                                        w["before"][:].unsqueeze(1).broadcast_to([P, TB, E, E]),
                                                        ALU.mult))
                        chained(nc.vector.tensor_tensor(above[:], above[:], equal[:], ALU.add))
                        nc.vector.tensor_reduce(rank[:], above[:], AX.X, ALU.add)
                        chained(nc.vector.tensor_reduce(top[:], logits[:], AX.X, ALU.max))
                        nc.vector.tensor_tensor(gates[:], logits[:], top[:].unsqueeze(2).broadcast_to([P, TB, E]),
                                                ALU.subtract).then_inc(centred_ready, 1)
                        chained(nc.vector.tensor_scalar(rank[:], rank[:], TOP_K - 0.5, None, ALU.is_lt))
                        dve.wait_ge(exp_ready, it + 1)
                        chained(nc.vector.tensor_tensor(gates[:], gates[:], rank[:], ALU.mult))
                        chained(nc.vector.tensor_reduce(total[:], gates[:], AX.X, ALU.add))
                        chained(nc.vector.reciprocal(total[:], total[:]))
                        chained(nc.vector.tensor_tensor(gates[:], gates[:],
                                                        total[:].unsqueeze(2).broadcast_to([P, TB, E]), ALU.mult))
                        dve.sem_inc(gates_ready, 1)
                        done[0] += 1
                        dve.sem_inc(routed, 1)
                        assert done[0] == CHAIN, done
                    elif kind == "b2":
                        t = step[1]
                        filled(step, it)
                        nc.vector.tensor_tensor(acc[:, t, :], ps.ap(step)[:, 0:D], xin[:, t, :],
                                                ALU.add).then_inc(acc_ready, 1)
                        dve.wait_ge(acc_ready, it * TB + t + 1)
                        dve.sem_inc(ps.sem_drained(step), 1)
                    elif kind == "o":
                        e, t = step[1:]
                        before = ("o", e - 1, t) if e else ("b2", t)
                        dve.wait_ge(ps.sem_drained(before), ps.count(before, it))
                        filled(step, it)
                        nc.vector.scalar_tensor_tensor(out=acc[:, t, :], in0=ps.ap(step)[:, 0:D],
                                                       scalar=gates[:, t, e:e + 1], in1=acc[:, t, :], op0=ALU.mult,
                                                       op1=ALU.add).then_inc(ps.sem_drained(step), 1)
                    elif kind == "ln":
                        for t in range(TB):
                            key = ("o", E - 1, t)
                            dve.wait_ge(ps.sem_drained(key), ps.count(key, it))
                        norm.vector(dve, it)

        @block.gpsimd
        def _(pool):
            with pool.Fori(0, NB) as it:
                norm.gpsimd(pool, it)


def stage_head_attention(nc, shared, stage, w, cross, preload=None):
    ident, x_all = shared["ident"], shared["x"]
    D = x_all.shape[2]
    TB = 4
    NB = x_all.shape[1] // TB
    S = TB * P
    KC = D // P
    H, DH, ROWS = 16, 16, 32
    HPC = P // ROWS
    QC = H // HPC
    scale = float(DH) ** -0.5

    with ExitStack() as ctx:
        def sb(name, shape, dt=F32):
            return ctx.enter_context(nc.sbuf_tensor(f"{stage}_{name}", shape, dt))

        def sem(name):
            return shared["sems"].enter_context(nc.semaphore(f"{stage}_{name}"))

        xin = sb("xin", [P, TB, D])
        xT = sb("xT", [P, KC, S])
        qT = sb("qT", [P, H, S])
        kT = sb("kT", [P, QC, S])
        v = sb("v", [P, TB, H, ROWS])
        prob = sb("prob", [P, 4, S])
        pT = sb("pT", [P, 2 * HPC, S])
        mx = sb("mx", [P, 2, H])
        nb = sb("nb", [P, 2, H])
        sums = sb("sums", [P, 2, H])
        rs = sb("rs", [P, H])
        rs_wide = sb("rs_wide", [P, H * ROWS])
        o_raw = sb("o_raw", [P, QC * P])
        oT = sb("oT", [P, QC * P])
        y = sb("y", [P, TB, D])
        norm = Norm(nc, shared, ctx, stage, y)
        srcT = sb("srcT", [P, KC, S]) if cross else xT
        mask_int = sb("mask_int", [P, TB, S], mybir.dt.int32) if cross else None
        add_mask = sb("add_mask", [P, TB, S]) if cross else w["causal"]
        src_ready = sem("src_ready")
        mask_landed = sem("mask_landed")
        masked = sem("masked")
        mask_ready = sem("mask_ready")
        xin_ready = sem("xin_ready")
        nb_ready = sem("nb_ready")
        exp_ready = sem("exp_ready")
        pads = sem("pads")
        o_ready = sem("o_ready")
        inverted = sem("inverted")
        rs_ready = sem("rs_ready")
        o_copied = sem("o_copied")

        units = [(t, h) for t in range(TB) for h in range(H)]
        N = len(units)
        def project_next():
            return [("xin",), ("xt",), *[("q", e) for e in range(QC)], *[("k", e) for e in range(QC)], ("v",)]

        def batch(before, more):
            ahead = {N - H: ("xin",), N - H // 2: ("xt",), N: ("q", 0), N + 1: ("q", 2), N + 2: ("k", 0)}
            for n in range(N + 3):
                if n < N:
                    yield ("s", n)
                if 2 <= n < N + 2:
                    yield ("pt", n - 2)
                if more and n in ahead:
                    step = ahead[n]
                    yield step
                    if step[0] in ("q", "k"):
                        yield (step[0], step[1] + 1)
                if n >= HPC + 2 and n % HPC == 2:
                    g = n // HPC - 1
                    yield ("pv", g)
                    if g % QC == QC - 1:
                        yield ("den", g // QC)
                if n % H == HPC and n > H:
                    yield ("div", n // H - 1)
                if n % H == HPC + 1 and n > H:
                    yield ("wo", n // H - 1)
                if n == HPC and before:
                    yield ("ln", -1)
            yield ("div", TB - 1)
            if more:
                yield from [("k", 2), ("k", 3), ("v",)]
            yield ("wo", TB - 1)
            if not more:
                yield ("ln", 0)

        phases = []
        for steps, first, end in ((project_next(), -1, 0), (list(batch(False, True)), 0, 1),
                                  (list(batch(True, True)), 1, NB - 1), (list(batch(True, False)), NB - 1, NB)):
            ps = Psum(shared, first)
            dense = N if first >= 0 else 0
            for step in steps:
                kind = step[0]
                if kind == "xt":
                    for c in range(KC):
                        ps.fill(step + (c,), 1)
                elif kind in ("q", "k"):
                    ps.fill(step, (4, 5, 0)[dense % 3])
                    dense += 1
                elif kind == "v":
                    for i in range(2):
                        ps.fill(step + (i,), (4, 5, 0)[dense % 3])
                        dense += 1
                elif kind == "s":
                    ps.fill(step, (4, 5, 0)[step[1] % 3])
                elif kind == "pt":
                    ps.fill(step, 2 + step[1] % 2)
                elif kind == "pv" and step[1] % QC == 0:
                    ps.fill(("o", step[1] // QC), 6 + step[1] // QC % 2)
                elif kind in ("den", "wo"):
                    ps.fill(step, 1)
            ps.finish(shared, end - first)
            phases.append((steps, ps, first, end))

        @contextmanager
        def each(engine, first, end):
            if end - first == 1:
                yield first
            else:
                with engine.Fori(first, end) as it:
                    yield it

        def keys(t):
            return S if cross else (t + 1) * P

        block = ctx.enter_context(nc.Block())

        @block.sync
        def _(sp):
            if preload:
                preload(sp)
            if not cross:
                return

            def load(b):
                sp.dma_start(srcT[:], w["ctxT"][b].rearrange("(c p) s -> p c s", p=P)).then_inc(src_ready, 16)
                sp.dma_start(mask_int[:], w["mask"][b].rearrange("(t p) s -> p t s", p=P)).then_inc(mask_landed, 16)

            load(0)
            with sp.Fori(1, NB) as b:
                sp.wait_ge(mask_ready, b)
                load(b)

        @block.tensor
        def _(pe):
            def empty(key, it):
                pe.wait_ge(ps.sem_drained(key), ps.before(key, it))

            def drained(key, it):
                pe.wait_ge(ps.sem_drained(key), ps.count(key, it))

            pe.wait_ge(w["landed"], w["loads"])
            for steps, ps, first, end in phases:
                with each(pe, first, end) as it:
                    for step in steps:
                        kind = step[0]
                        if kind == "xt":
                            pe.wait_ge(xin_ready, it + 2)
                            for c in range(KC):
                                key = step + (c,)
                                empty(key, it)
                                for t in range(TB):
                                    mm = nc.tensor.transpose(ps.ap(key)[:, t * P:(t + 1) * P],
                                                             xin[:, t, c * P:(c + 1) * P], ident[:])
                                mm.then_inc(ps.sem_filled(key), 1)
                        elif kind in ("q", "k"):
                            e = step[1]
                            if step == ("q", 0):
                                drained(("xt", KC - 1), it)
                            elif step == ("k", 0) and cross:
                                pe.wait_ge(src_ready, (it + 2) * 16)
                            empty(step, it)
                            for c in range(KC):
                                mm = nc.tensor.matmul(ps.ap(step), w["W" + kind][:, c, e * P:(e + 1) * P],
                                                      (xT if kind == "q" else srcT)[:, c, :],
                                                      start=c == 0, stop=c == KC - 1)
                            mm.then_inc(ps.sem_filled(step), 1)
                        elif kind == "v":
                            for i in range(2):
                                key = step + (i,)
                                empty(key, it)
                                for n in range(2):
                                    t = 2 * i + n
                                    for c in range(KC):
                                        mm = nc.tensor.matmul(ps.ap(key)[:, n * D:(n + 1) * D],
                                                              srcT[:, c, t * P:(t + 1) * P], w["Wv"][:, c, :],
                                                              start=c == 0, stop=c == KC - 1)
                                mm.then_inc(ps.sem_filled(key), 1)
                        elif kind == "s":
                            n = step[1]
                            t, h = units[n]
                            if n == 0:
                                for key in (("s", 1), ("s", 2)):
                                    pe.wait_ge(ps.sem_drained(key), ps.start(key, it))
                            empty(step, it)
                            nc.tensor.matmul(ps.ap(step)[:, 0:keys(t)], qT[:, h, t * P:(t + 1) * P],
                                             kT[:, h // HPC, 0:keys(t)], start=True,
                                             stop=True).then_inc(ps.sem_filled(step), 1)
                        elif kind == "pt":
                            n = step[1]
                            t, h = units[n]
                            pe.wait_ge(exp_ready, it * N + n + 1)
                            empty(step, it)
                            for k in range(keys(t) // P):
                                mm = nc.tensor.transpose(ps.ap(step)[:, k * P:(k + 1) * P],
                                                         prob[:, n % 4, k * P:(k + 1) * P], ident[:])
                            mm.then_inc(ps.sem_filled(step), 1)
                        elif kind == "pv":
                            t, g = divmod(step[1], QC)
                            for j in range(HPC - 2, HPC):
                                drained(("pt", HPC * step[1] + j), it)
                            okey = ("o", t)
                            if g == 0:
                                empty(okey, it)
                            for k in range(keys(t) // P):
                                for j in range(HPC):
                                    rows = slice(j * ROWS, (j + 1) * ROWS)
                                    mm = nc.tensor.matmul(ps.ap(okey)[rows, g * P:(g + 1) * P],
                                                          v[:, k, HPC * g + j, :],
                                                          pT[:, HPC * (g % 2) + j, k * P:(k + 1) * P],
                                                          start=k == 0, stop=k == keys(t) // P - 1,
                                                          tile_position=(0, j * ROWS))
                            if g == QC - 1:
                                mm.then_inc(ps.sem_filled(okey), 1)
                        elif kind == "den":
                            pe.wait_ge(rs_ready, it * TB + step[1] + 1)
                            empty(step, it)
                            for g in range(QC):
                                mm = nc.tensor.matmul(ps.ap(step)[:, g * P:(g + 1) * P],
                                                      rs_wide[:, g * P:(g + 1) * P], ident[:], start=True, stop=True)
                            mm.then_inc(ps.sem_filled(step), 1)
                        elif kind == "wo":
                            t = step[1]
                            pe.wait_ge(o_ready, it * TB + t + 1)
                            empty(step, it)
                            for g in range(QC):
                                mm = nc.tensor.matmul(ps.ap(step)[:, 0:D], oT[:, g * P:(g + 1) * P], w["Wo"][:, g, :],
                                                      start=g == 0, stop=g == QC - 1)
                            mm.then_inc(ps.sem_filled(step), 1)

        def copy_probs(eng, copy, ps, n, it):
            t, h = units[n]
            key = ("pt", n)
            eng.wait_ge(ps.sem_filled(key), ps.count(key, it))
            copy(pT[:, n % (2 * HPC), 0:keys(t)], ps.ap(key)[:, 0:keys(t)]).then_inc(ps.sem_drained(key), 1)

        def copy_queries(waits, eng, ps, step, it):
            e = step[1]
            if ps.first < 0:
                waits.wait_ge(pads, 2)
            waits.wait_ge(ps.sem_filled(step), ps.count(step, it))
            for j in range(HPC):
                rows = slice(j * ROWS, (j + 1) * ROWS)
                out, src = qT[rows, HPC * e + j, :], ps.ap(step)[rows]
                if eng is nc.scalar:
                    if cross:
                        ins = nc.scalar.activation(out, src, ACT.Identity, bias=w["bq"][rows, e:e + 1])
                    else:
                        ins = nc.scalar.copy(out, src)
                elif cross:
                    ins = nc.vector.tensor_scalar(out, src, w["bq"][rows, e:e + 1], None, ALU.add)
                else:
                    ins = nc.vector.tensor_copy(out, src)
            ins.then_inc(ps.sem_drained(step), 1)

        def on_scalar(n):
            return n % 2 == 0

        @block.scalar
        def _(act):
            def filled(key, it):
                act.wait_ge(ps.sem_filled(key), ps.count(key, it))

            act.wait_ge(w["landed"], w["loads"])
            for steps, ps, first, end in phases:
                with each(act, first, end) as it:
                    for step in steps:
                        kind = step[0]
                        if kind == "xt":
                            for c in range(KC):
                                filled(step + (c,), it)
                                nc.scalar.copy(xT[:, c, :], ps.ap(step + (c,))).then_inc(ps.sem_drained(step + (c,)), 1)
                        elif kind == "q" and step[1] % 2 == 1:
                            copy_queries(act, nc.scalar, ps, step, it)
                        elif kind == "k":
                            e = step[1]
                            filled(step, it)
                            if cross:
                                ins = nc.scalar.activation(kT[:, e, :], ps.ap(step), ACT.Identity,
                                                           bias=w["bk"][:, e:e + 1])
                            else:
                                ins = nc.scalar.copy(kT[:, e, :], ps.ap(step))
                            ins.then_inc(ps.sem_drained(step), 1)
                        elif kind == "s":
                            n = step[1]
                            t, h = units[n]
                            act.wait_ge(nb_ready, it * N + n + 1)
                            pr = prob[:, n % 4, 0:keys(t)]
                            nc.scalar.activation(pr, pr, ACT.Exp, bias=nb[:, t % 2, h:h + 1],
                                                 scale=scale,
                                                 accum_out=sums[:, t % 2, h:h + 1]).then_inc(exp_ready, 1)
                        elif kind == "pt" and on_scalar(step[1]):
                            copy_probs(act, nc.scalar.copy, ps, step[1], it)
                        elif kind == "den":
                            t = step[1]
                            if t:
                                filled(("wo", t - 1), it)
                            filled(("o", t), it)
                            nc.scalar.copy(o_raw[:], ps.ap(("o", t))).then_inc(ps.sem_drained(("o", t)), 1)
                            act.wait_ge(ps.sem_drained(("o", t)), ps.count(("o", t), it))
                            act.sem_inc(o_copied, 1)

        @block.vector
        def _(dve):
            def filled(key, it):
                dve.wait_ge(ps.sem_filled(key), ps.count(key, it))

            nc.vector.memset(v[:, :, :, DH:ROWS], 0.0)
            nc.vector.memset(qT[:, 0:H // 2, :], 0.0).then_inc(pads, 1)
            dve.wait_ge(w["landed"], w["loads"])
            for steps, ps, first, end in phases:
                with each(dve, first, end) as it:
                    for step in steps:
                        kind = step[0]
                        if kind == "q" and step[1] % 2 == 0:
                            copy_queries(dve, nc.vector, ps, step, it)
                        elif kind == "v":
                            for i in range(2):
                                key = step + (i,)
                                filled(key, it)
                                out = v[:, 2 * i:2 * i + 2, :, 0:DH]
                                src = ps.ap(key).rearrange("p (t h d) -> p t h d", t=2, d=DH)
                                if cross:
                                    bv = w["bv"][:].rearrange("p (h d) -> p h d", d=DH)
                                    ins = nc.vector.tensor_tensor(out, src, bv.unsqueeze(1).broadcast_to(
                                        [P, 2, H, DH]), ALU.add)
                                else:
                                    ins = nc.vector.tensor_copy(out, src)
                                ins.then_inc(ps.sem_drained(key), 1)
                            if cross:
                                dve.wait_ge(mask_landed, (it + 2) * 16)
                                nc.vector.tensor_scalar(add_mask[:], mask_int[:], 0.0, MASKED, ALU.is_equal,
                                                        ALU.mult).then_inc(mask_ready, 1)
                                dve.wait_ge(mask_ready, it + 2)
                        elif kind == "s":
                            n = step[1]
                            t, h = units[n]
                            if n >= 4:
                                filled(("pt", n - 4), it)
                            filled(step, it)
                            dve.sem_inc(norm.passed, 1)
                            nc.vector.tensor_tensor_reduce(prob[:, n % 4, 0:keys(t)], ps.ap(step)[:, 0:keys(t)],
                                                           add_mask[:, t, 0:keys(t)], 1.0, LOWEST, ALU.add, ALU.max,
                                                           mx[:, t % 2, h:h + 1]).then_inc(ps.sem_drained(step), 1)
                            dve.wait_ge(ps.sem_drained(step), ps.count(step, it))
                            nc.vector.tensor_scalar(nb[:, t % 2, h:h + 1], mx[:, t % 2, h:h + 1], -scale, None,
                                                    ALU.mult).then_inc(nb_ready, 1)
                        elif kind == "pt" and not on_scalar(step[1]):
                            copy_probs(dve, nc.vector.tensor_copy, ps, step[1], it)
                        elif kind == "den":
                            t = step[1]
                            dve.wait_ge(exp_ready, it * N + H * (t + 1))
                            nc.vector.reciprocal(rs[:], sums[:, t % 2, :]).then_inc(inverted, 1)
                            dve.wait_ge(inverted, it * TB + t + 1)
                            nc.vector.tensor_copy(rs_wide[:].rearrange("p (h r) -> p h r", r=ROWS),
                                                  rs[:].unsqueeze(2).broadcast_to([P, H, ROWS])).then_inc(rs_ready, 1)
                        elif kind == "div":
                            t = step[1]
                            key = ("den", t)
                            if t:
                                filled(("wo", t - 1), it)
                            dve.wait_ge(o_copied, it * TB + t + 1)
                            filled(key, it)
                            dve.sem_inc(norm.passed, 1)
                            nc.vector.tensor_tensor(oT[:], o_raw[:], ps.ap(key),
                                                    ALU.mult).then_inc(ps.sem_drained(key), 1)
                            dve.wait_ge(ps.sem_drained(key), ps.count(key, it))
                            dve.sem_inc(o_ready, 1)
                        elif kind == "wo":
                            t = step[1]
                            filled(step, it)
                            nc.vector.tensor_tensor(y[:, t, :], ps.ap(step)[:, 0:D], x_all[:, it * TB + t, :],
                                                    ALU.add).then_inc(ps.sem_drained(step), 1)
                        elif kind == "ln":
                            key = ("wo", TB - 1)
                            done = it + step[1]
                            dve.wait_ge(ps.sem_drained(key), ps.start(key, it) if step[1] else ps.count(key, it))
                            dve.sem_inc(norm.passed, 1)
                            if cross:
                                for t in range(TB):
                                    ins = nc.vector.tensor_tensor(y[:, t, :], y[:, t, :], w["bo"][:], ALU.add)
                                ins.then_inc(masked, 1)
                                dve.wait_ge(masked, done + 1)
                            norm.vector(dve, done)

        @block.gpsimd
        def _(pool):
            for steps, ps, first, end in phases:
                with each(pool, first, end) as it:
                    for step in steps:
                        if step[0] == "xin":
                            key = ("xt", KC - 1)
                            pool.wait_ge(ps.sem_filled(key), ps.start(key, it))
                            nc.gpsimd.tensor_copy(xin[:], x_all[:, bass.ds((it + 1) * TB, TB), :]
                                                  ).then_inc(xin_ready, 1)
                            if first < 0:
                                nc.gpsimd.memset(qT[:, H // 2:H, :], 0.0).then_inc(pads, 1)
                        elif step[0] == "ln":
                            norm.gpsimd(pool, it + step[1])


def mk_decoder(nc, ins, out):
    B, S, D = ins["x"].shape
    TILES = B * S // P
    scratch = nc.dram_tensor("x_before_mlp", [P, TILES, D], F32, kind="Internal").ap()
    with ExitStack() as ctx:
        def sb(c, name, shape, dt=F32):
            return c.enter_context(nc.sbuf_tensor(name, shape, dt))

        psum = ctx.enter_context(nc.psum_tensor("psum", [P, PSUM_BANKS, BANK], F32))
        ident = sb(ctx, "ident", [P, P])
        half_pow = sb(ctx, "half_pow", [P, 32])
        x_all = sb(ctx, "x_all", [P, TILES, D])
        shared = {"psum": psum, "ident": ident, "x": x_all, "half_pow": half_pow}
        landed = {n: ctx.enter_context(nc.semaphore("landed_" + n)) for n in ("x", "a0", "x0", "moe", "a1", "x1")}
        shared["sems"] = ctx
        for n in ("filled", "drained"):
            shared[n] = [ctx.enter_context(nc.semaphore(f"bank{b}_{n}")) for b in range(PSUM_BANKS)]
        shared["contents"] = [8] * PSUM_BANKS
        made = ctx.enter_context(nc.semaphore("made"))

        with ExitStack() as attention:
            loads = []
            place = attention

            def weight(stage, name, shape, src):
                t = sb(place, f"w_{stage}_{name}", shape)
                loads.append((stage, t[:], src))
                return t

            def chunks(ap):
                return ap.rearrange("(c p) n -> p c n", p=P)

            ORDER = ("a0", "x0", "moe", "a1", "x1")
            a0, x0, moe, a1, x1 = {}, {}, {}, {}, {}
            KC = D // P
            for st, d, pre in (("a1", a1, "L1_attn_"), ("x1", x1, "L1_xattn_")):
                for n in ("Wq", "Wk"):
                    d[n] = weight(st, n, [P, KC, 2 * D], chunks(ins[pre + n]))
                d["Wv"] = weight(st, "Wv", [P, KC, D], chunks(ins[pre + "Wv"]))
                d["Wo"] = weight(st, "Wo", [P, 2 * KC, D], chunks(ins[pre + "Wo"]))
            x0["causal"] = weight("x0", "causal", [P, S // P, S], ins["causal"])
            a1["causal"] = x0["causal"]
            for n in ("bq", "bk"):
                x1[n] = weight("x1", n, [P, 4], ins["L1_xattn_" + n])
            for n in ("bv", "bo"):
                x1[n] = weight("x1", n, [P, D], ins["L1_xattn_" + n].partition_broadcast(P))
            x1["ctxT"], x1["mask"] = ins["ctxT"], ins["mask_BxSxS2_ik0"]
            place = ctx.enter_context(ExitStack())
            for n in ("Wq", "Wk"):
                a0[n + "_plain"] = weight("a0", n, [P, KC, D], chunks(ins["L0_attn_" + n]))
                a0[n] = sb(place, "w_a0_turned_" + n, [P, KC, D])
            a0["Wv"] = weight("a0", "Wv", [P, KC, D], chunks(ins["L0_attn_Wv"]))
            for n in ("bq", "bk", "bq_swap", "bk_swap"):
                a0[n] = weight("a0", n, [P, KC], ins["L0_attn_" + n])
            a0["pair_sign"] = weight("a0", "pair_sign", [P, KC], ins["pair_sign"])
            a0["bv"] = weight("a0", "bv", [P, D], ins["L0_attn_bv"].partition_broadcast(P))
            rope = weight("a0", "rope", [P, KC, S], ins["rope_pairs"])
            for n in ("Wq", "Wk", "Wv"):
                x0[n] = weight("x0", n, [P, KC, D], chunks(ins["L0_xattn_" + n]))
            for n in ("bq", "bk"):
                x0[n] = weight("x0", n, [P, KC], ins["L0_xattn_" + n])
            x0["bv"] = weight("x0", "bv", [P, D], ins["L0_xattn_bv"].partition_broadcast(P))
            x0["ctxT"] = ins["ctxT"]
            x0["mask"] = ins["mask_Bx1xS2_ik0"].rearrange("b a s -> b (a s)")
            E, _, HID = ins["L0_ffn_W1"].shape
            moe["Wr"] = weight("moe", "Wr", [P, KC, E], chunks(ins["L0_ffn_Wr"]))
            moe["br"] = weight("moe", "br", [P, E], ins["L0_ffn_br"].partition_broadcast(P))
            moe["before"] = weight("moe", "before", [P, E, E], ins["before"].rearrange(
                "e f -> (e f)").partition_broadcast(P).rearrange("p (e f) -> p e f", e=E))
            moe["b1"] = weight("moe", "b1", [P, E, HID // P], ins["L0_ffn_b1"])
            moe["b2"] = weight("moe", "b2", [E, D], ins["L0_ffn_b2"])
            moe["W1"] = weight("moe", "W1", [P, E, KC, HID], ins["L0_ffn_W1"].rearrange("e (c p) n -> p e c n", p=P))
            moe["W2"] = weight("moe", "W2", [P, E, HID // P, D],
                               ins["L0_ffn_W2"].rearrange("e (c p) n -> p e c n", p=P))
            for st, d in (("a0", a0), ("x0", x0), ("moe", moe), ("a1", a1), ("x1", x1)):
                d["landed"], d["loads"] = landed[st], 16 * sum(1 for s, _, _ in loads if s == st)

            with nc.Block() as block:
                @block.sync
                def _(sp):
                    sp.dma_start(ident[:], ins["ident"]).then_inc(landed["x"], 16)
                    sp.dma_start(x_all[:], ins["x"].rearrange("b (t p) d -> p (b t) d", p=P)
                                 ).then_inc(landed["x"], 16)
                    for st, dst, src in sorted(loads, key=lambda load: ORDER.index(load[0])):
                        sp.dma_start(dst, src).then_inc(landed[st], 16)
                    sp.wait_ge(landed["x"], 32)

                @block.vector
                def _(dve):
                    for bank in range(PSUM_BANKS):
                        dve.sem_inc(shared["filled"][bank], 8)
                        dve.sem_inc(shared["drained"][bank], 8)
                    nc.vector.memset(half_pow[:], -0.5).then_inc(made, 1)
                    dve.wait_ge(made, 1)

            stage_wide_attention(nc, shared, "a0", a0, rope, cross=False)
            stage_wide_attention(nc, shared, "x0", x0, None, cross=True)
            stage_moe(nc, shared, moe)
            place.close()
            far = ctx.enter_context(ExitStack())
            mlp_weights = MlpStageWeights(nc, far, shared, ins, ins)
            stage_head_attention(nc, shared, "a1", a1, cross=False, preload=mlp_weights.load_first)
            stage_head_attention(nc, shared, "x1", x1, cross=True)

        stage_l1_ffn(nc, shared, mlp_weights, scratch)
        far.close()
        stage_final(nc, shared, scratch, out)


def stage_final(nc, shared, scratch, out):
    x_all = shared["x"]
    _, TILES, D = x_all.shape
    TB = 4
    NB = TILES // TB
    with ExitStack() as ctx:
        x_old = ctx.enter_context(nc.sbuf_tensor("x_old", [P, TILES, D], F32))
        y = ctx.enter_context(nc.sbuf_tensor("z_y", [P, TILES, D], F32))
        norm = Norm(nc, shared, ctx, "z", y)
        old_landed = ctx.enter_context(nc.semaphore("z_old_landed"))
        summed = ctx.enter_context(nc.semaphore("z_summed"))
        stored = ctx.enter_context(nc.semaphore("z_stored"))
        out_v = out.rearrange("b (t p) d -> p (b t) d", p=P)
        with nc.Block() as block:
            @block.sync
            def _(sp):
                sp.dma_start(x_old[:], scratch).then_inc(old_landed, 16)
                sp.wait_ge(norm.x_ready, 1)
                sp.dma_start(out_v, x_all[:]).then_inc(stored, 16)
                sp.wait_ge(stored, 16)

            @block.vector
            def _(dve):
                dve.wait_ge(old_landed, 16)
                nc.vector.tensor_tensor(y[:], x_old[:], x_all[:], ALU.add).then_inc(summed, 1)
                dve.wait_ge(summed, 1)
                norm.vector(dve, 0)

            @block.gpsimd
            def _(pool):
                norm.gpsimd(pool, 0)


def tables():
    import numpy as np

    f32 = np.float32
    S, D, E, DH = 512, 256, 8, 64
    t = {"ident": np.eye(P, dtype=f32)}
    pos = np.arange(S, dtype=f32)
    inv = (f32(10000.0) ** (np.arange(0, 128, 2, dtype=f32) / f32(128))).astype(f32)
    rad = (pos[:, None] / inv).astype(f32)
    sincos = np.repeat(np.stack((np.sin(rad), np.cos(rad)), axis=-1).reshape(S, -1), 2, axis=-1)
    t["rope_pairs"] = sincos.T.reshape(D // P, P, S).transpose(1, 0, 2)
    t["pair_sign"] = np.where(np.arange(P) % 2 == 0, -1, 1)[:, None] * np.ones((1, D // P))
    q, k = np.arange(S)[:, None], np.arange(S)[None]
    tiled = lambda a: a.reshape(S // P, P, S).transpose(1, 0, 2)
    t["causal"] = tiled(np.where(k > q, -1e10, 0.0))
    t["before"] = np.where(np.arange(E)[None] < np.arange(E)[:, None], 1.0, 0.0)
    half = np.arange(0, DH, 2, dtype=f32)
    freq = (f32(1.0) / f32(10000.0) ** (half / f32(DH))).astype(f32)
    ang = np.concatenate([pos[:, None] * freq[None]] * 2, -1).astype(f32)
    base = ((half + f32(0.4 * DH)) / f32(1.4 * DH)).astype(f32)
    power = ((pos - S // 2) / 32).astype(f32)
    sc = (base[None] ** power[:, None]).astype(f32)
    sc = np.concatenate([sc, sc], -1)
    sign = np.where(np.arange(DH) < DH // 2, -1, 1).astype(f32)
    cos, sin = np.cos(ang), np.sin(ang) * sign
    inv_sc = (f32(1.0) / sc).astype(f32)
    t["rope"] = np.stack([cos * sc, sin * sc, cos * inv_sc, sin * inv_sc], 1).reshape(S // P, P, 4, DH).transpose(
        1, 0, 2, 3)
    p, j = np.arange(P)[:, None], np.arange(2 * P)[None]
    near = (P + p - j >= 0) & (P + p - j <= 64)
    t["band"] = np.stack([np.where(near & (j >= P), 0.0, -1e30), np.where(near, 0.0, -1e30)], 1)
    return {n: np.ascontiguousarray(a, dtype=f32) for n, a in t.items()}


def lay_out(inputs):
    import numpy as np

    a = {n: np.asarray(v) for n, v in inputs.items()}
    D = a["x"].shape[-1]
    g = {n: a[n] for n in ("x", "mask_Bx1xS2_ik0", "mask_BxSxS2_ik0")}
    g["ctxT"] = a["ctx_1024"].transpose(0, 2, 1)

    def columns(v, chunks):
        out = np.zeros(v.shape[:-1] + (chunks * P,), v.dtype)
        out[..., :v.shape[-1]] = v
        return out.reshape(v.shape[:-1] + (chunks, P)).swapaxes(-1, -2)

    def spaced(v):
        out = np.zeros(v.shape[:-1] + (D // 16, 32), v.dtype)
        out[..., :16] = v.reshape(v.shape[:-1] + (D // 16, 16))
        return out.reshape(v.shape[:-1] + (2 * D,))

    for n in ("Wq", "Wk", "Wv"):
        g["L0_attn_" + n] = a["L0_attn_" + n].T
        g["L0_xattn_" + n] = a["L0_xattn_" + n].T
    for n in ("bq", "bk"):
        g["L0_attn_" + n] = columns(a["L0_attn_" + n], D // P)
        g["L0_attn_" + n + "_swap"] = columns(a["L0_attn_" + n].reshape(-1, 2)[:, ::-1].reshape(-1), D // P)
        g["L0_xattn_" + n] = columns(a["L0_xattn_" + n], D // P)
    for n in ("L0_attn_bv", "L0_xattn_bv", "L0_ffn_Wr", "L0_ffn_br", "L0_ffn_W1", "L0_ffn_W2", "L0_ffn_b2",
              "L1_xattn_bv", "L1_xattn_bo"):
        g[n] = a[n]
    g["L0_ffn_b1"] = columns(a["L0_ffn_b1"], a["L0_ffn_b1"].shape[1] // P).transpose(1, 0, 2)
    for pre in ("L1_attn_", "L1_xattn_"):
        for n in ("Wq", "Wk"):
            g[pre + n] = spaced(a[pre + n].T)
        g[pre + "Wv"] = a[pre + "Wv"].T
        g[pre + "Wo"] = spaced(a[pre + "Wo"]).T
    for n in ("bq", "bk"):
        g["L1_xattn_" + n] = columns(spaced(a["L1_xattn_" + n]), 2 * D // P)
    for n in ("Wqkv", "Wo", "W1", "W2", "b2"):
        g[n] = a["L1_ffn_" + n]
    for n in ("q", "k"):
        s = a[f"L1_ffn_{n}_scale"]
        g[n + "_scale"] = s
        g[n + "_swap"] = np.concatenate([s[:, s.shape[1] // 2:], s[:, :s.shape[1] // 2]], 1)
    for n in ("ln_g", "ln_b"):
        g[n] = columns(a["L1_ffn_" + n], D // P)
    hid = a["L1_ffn_W2"].shape[1]
    g["b1a"] = columns(a["L1_ffn_b1"][:, :hid], -(-hid // P))
    g["b1g"] = columns(a["L1_ffn_b1"][:, hid:], -(-hid // P))
    return {n: np.ascontiguousarray(v) for n, v in g.items()}


def kernel(**inputs):
    import concourse.bacc as _bacc
    from concourse import mybir as _mybir
    from concourse.bass_utils import run_bass_kernel_spmd as _run

    nc = _bacc.Bacc("TRN2", target_bir_lowering=False, num_devices=1)
    laid = lay_out(inputs)
    laid.update(tables())
    arrays = {f"in_{n}": v for n, v in laid.items()}
    ins = {n: nc.dram_tensor(f"in_{n}", v.shape, _mybir.dt.from_np(v.dtype), kind="ExternalInput").ap()
           for n, v in laid.items()}
    out = nc.dram_tensor("out", laid["x"].shape, F32, kind="ExternalOutput").ap()
    mk_decoder(nc, ins, out)
    r = _run(nc, [arrays], core_ids=[0])
    return r.results[0]["out"]
```
